# Optimizing a Trainium2 kernel written in Bass

```python
import numpy as np
import jax
import jax.numpy as jnp

def _softmax(x, axis=-1):
    return jax.nn.softmax(x, axis=axis)

def _gelu(x):
    return jax.nn.gelu(x, approximate=True)

def _silu(x):
    return jax.nn.silu(x)

def _sigmoid(x):
    return jax.nn.sigmoid(x)

def _layernorm(x, axis=-1, eps=1e-05):
    m = jnp.mean(x, axis=axis, keepdims=True)
    v = jnp.var(x, axis=axis, keepdims=True)
    return (x - m) / jnp.sqrt(v + eps)

def _scatter_add(tgt, idx, src, axis=0):
    return tgt.at[idx].add(src)

def _segment_sum(src, seg, n):
    return jax.ops.segment_sum(src, seg, n)
kernel_name = 'mk_early_fusion_d4_tok_img1024_r4_90a0c4'

def setup_inputs(seed: int=0):
    np.random.seed(seed)
    _w = jnp.asarray

    def _rec_inputs():
        import jax
        import jax.numpy as jnp
        _rk = jax.random.key(seed)
        x = -0.000392918 + 0.999932 * jax.random.normal(jax.random.fold_in(_rk, 1), (8, 256, 256, 1), jnp.float32)
        txt = -0.000282583 + 0.544222 * jax.random.normal(jax.random.fold_in(_rk, 2), (8, 77, 256), jnp.float32)
        return (x, txt)
    x, txt = _rec_inputs()

    def _L0_tok_setup():
        import jax, jax.numpy as jnp
        import numpy as np
        INV_SQRT2 = 0.7071067811865476
        LEVEL = 3

        def _split(x, axis):
            ax = axis % x.ndim
            sl0 = [slice(None)] * x.ndim
            sl0[ax] = slice(0, None, 2)
            sl1 = [slice(None)] * x.ndim
            sl1[ax] = slice(1, None, 2)
            x0, x1 = (x[tuple(sl0)], x[tuple(sl1)])
            return ((x0 + x1) * INV_SQRT2, (x0 - x1) * INV_SQRT2)

        def _merge(lo, hi, axis):
            ax = axis % lo.ndim
            e = (lo + hi) * INV_SQRT2
            o = (lo - hi) * INV_SQRT2
            s = jnp.stack([e, o], axis=ax + 1)
            shape = list(lo.shape)
            shape[ax] *= 2
            return s.reshape(shape)

        def _dwt2(x):
            lo, hi = _split(x, -1)
            a, h = _split(lo, -2)
            v, d = _split(hi, -2)
            return (a, h, v, d)

        def _idwt2(a, h, v, d):
            lo = _merge(a, h, -2)
            hi = _merge(v, d, -2)
            return _merge(lo, hi, -1)
        key = jax.random.key(seed)
        ks = jax.random.split(key, 8)
        B, H, W = (16, 256, 256)
        x = jax.random.normal(ks[0], (B, H, W, 1), dtype=jnp.float32)
        na = H // 8 * (W // 8)
        n2 = H // 4 * (W // 4)
        n1 = H // 2 * (W // 2)
        scale = 0.02
        Wa = jax.random.normal(ks[1], (na, 1), dtype=jnp.float32) * scale
        ba = jnp.zeros((1,), jnp.float32)
        Wd1 = jax.random.normal(ks[2], (3 * na, 3), dtype=jnp.float32) * scale
        bd1 = jnp.zeros((3,), jnp.float32)
        Wd2 = jax.random.normal(ks[3], (3 * n2, 3), dtype=jnp.float32) * scale
        bd2 = jnp.zeros((3,), jnp.float32)
        Wd3 = jax.random.normal(ks[4], (3 * n1, 3), dtype=jnp.float32) * scale
        bd3 = jnp.zeros((3,), jnp.float32)
        return {'x': x, 'Wa': Wa, 'ba': ba, 'Wd1': Wd1, 'bd1': bd1, 'Wd2': Wd2, 'bd2': bd2, 'Wd3': Wd3, 'bd3': bd3}
    _L0_tok_all = _L0_tok_setup()
    _L0_tok_in = {k: v for k, v in _L0_tok_all.items() if k in ('Wa', 'ba', 'Wd1', 'bd1', 'Wd2', 'bd2', 'Wd3', 'bd3')}
    del _L0_tok_all

    def _L0_attn_setup():
        import jax, jax.numpy as jnp
        import numpy as np
        import math
        H = 16
        EPS = 1e-05
        key = jax.random.key(seed)
        ks = jax.random.split(key, 4)
        B, T, D = (2, 512, 256)
        s = 1.0 / math.sqrt(D)
        return {'x': jax.random.normal(ks[0], (B, T, D), dtype=jnp.float32), 'ln_g': jnp.ones((D,), jnp.float32), 'ln_b': jnp.zeros((D,), jnp.float32), 'Wq': jax.random.normal(ks[1], (D, D), jnp.float32) * s, 'bq': jnp.zeros((D,), jnp.float32), 'Wk': jax.random.normal(ks[2], (D, D), jnp.float32) * s, 'bk': jnp.zeros((D,), jnp.float32), 'Wv': jax.random.normal(ks[3], (D, D), jnp.float32) * s, 'bv': jnp.zeros((D,), jnp.float32)}
    _L0_attn_all = _L0_attn_setup()
    _L0_attn_in = {k: v for k, v in _L0_attn_all.items() if k in ('ln_g', 'ln_b', 'Wq', 'bq', 'Wk', 'bk', 'Wv', 'bv')}
    del _L0_attn_all

    def _L0_ffn_setup():
        import jax, jax.numpy as jnp
        import numpy as np
        from jax import lax
        T, B, I, M, O = (64, 64, 256, 256, 256)

        def _xavier(key, shape):
            fan_out, fan_in = shape
            limit = float(np.sqrt(6.0 / (fan_in + fan_out)))
            return jax.random.uniform(key, shape, jnp.float32, -limit, limit)
        key = jax.random.key(seed)
        ks = jax.random.split(key, 9)
        x = jax.random.normal(ks[0], (T, B, I), jnp.float32)
        return {'x': x, 'wf': _xavier(ks[1], (M, I)), 'uf': _xavier(ks[2], (M, M)), 'bf': jnp.zeros((M,), jnp.float32), 'wi': _xavier(ks[3], (M, I)), 'ui': _xavier(ks[4], (M, M)), 'bi': jnp.zeros((M,), jnp.float32), 'wc': _xavier(ks[5], (M, I)), 'uc': _xavier(ks[6], (M, M)), 'bc': jnp.zeros((M,), jnp.float32), 'wo': _xavier(ks[7], (O, I)), 'uo': _xavier(ks[8], (O, M)), 'bo': jnp.zeros((O,), jnp.float32), 'in_c': jnp.zeros((M,), jnp.float32)}
    _L0_ffn_all = _L0_ffn_setup()
    _L0_ffn_in = {k: v for k, v in _L0_ffn_all.items() if k in ('wf', 'uf', 'bf', 'wi', 'ui', 'bi', 'wc', 'uc', 'bc', 'wo', 'uo', 'bo', 'in_c')}
    del _L0_ffn_all

    def _L1_attn_setup():
        import jax, jax.numpy as jnp
        import numpy as np
        from jax import lax
        DIM = 256
        B, N = (4, 1024)

        def _rmsnorm(x, gamma):
            scale = jnp.asarray(x.shape[-1], x.dtype) ** 0.5
            norm = jnp.sqrt(jnp.sum(x * x, axis=-1, keepdims=True))
            return x / jnp.maximum(norm, 1e-12) * scale * gamma
        key = jax.random.key(seed)
        k1, k2 = jax.random.split(key)
        x = jax.random.normal(k1, (B, N, DIM), dtype=jnp.float32)
        w_qkva = jax.random.normal(k2, (3 * DIM, DIM), dtype=jnp.float32) * DIM ** (-0.5)
        gamma = jnp.ones((DIM,), dtype=jnp.float32)
        return {'x': x, 'w_qkva': w_qkva, 'gamma': gamma}
    _L1_attn_all = _L1_attn_setup()
    _L1_attn_in = {k: v for k, v in _L1_attn_all.items() if k in ('w_qkva', 'gamma')}
    del _L1_attn_all

    def _L1_ffn_setup():
        import jax, jax.numpy as jnp
        import numpy as np
        GROUP = 16
        EPS = 1e-05

        def _dequant(q, scale):
            w = q.astype(jnp.float32) / 7.5 - 1.0
            return w * jnp.repeat(scale, GROUP, axis=1)

        def _qlora_linear(x, q, scale, bias, la, lb):
            w = _dequant(q, scale)
            base = jnp.einsum('btd,od->bto', x, w) + bias
            lora = jnp.einsum('btr,or->bto', jnp.einsum('btd,rd->btr', x, la), lb)
            return base + lora

        def _layernorm(x, g, b):
            mu = jnp.mean(x, axis=-1, keepdims=True)
            var = jnp.mean(jnp.square(x - mu), axis=-1, keepdims=True)
            return (x - mu) * jax.lax.rsqrt(var + EPS) * g + b
        key = jax.random.key(seed)
        ks = jax.random.split(key, 6)
        D, R, B, T = (256, 32, 8, 1024)
        x = jax.random.normal(ks[0], (B, T, D), dtype=jnp.float32)
        qweights = jax.random.randint(ks[1], (6, D, D), 0, 16, dtype=jnp.int32)
        scales = jax.random.uniform(ks[2], (6, D, D // GROUP), dtype=jnp.float32)
        biases = jax.random.normal(ks[3], (6, D), dtype=jnp.float32) * 0.02
        lora_a = jax.random.normal(ks[4], (6, R, D), dtype=jnp.float32) * 0.02
        lora_b = jax.random.normal(ks[5], (6, D, R), dtype=jnp.float32) * 0.02
        ln_gamma = jnp.ones((3, D), dtype=jnp.float32)
        ln_beta = jnp.zeros((3, D), dtype=jnp.float32)
        return {'x': x, 'qweights': qweights, 'scales': scales, 'biases': biases, 'lora_a': lora_a, 'lora_b': lora_b, 'ln_gamma': ln_gamma, 'ln_beta': ln_beta}
    _L1_ffn_all = _L1_ffn_setup()
    _L1_ffn_in = {k: v for k, v in _L1_ffn_all.items() if k in ('qweights', 'scales', 'biases', 'lora_a', 'lora_b', 'ln_gamma', 'ln_beta')}
    del _L1_ffn_all

    def _L2_attn_setup():
        import jax, jax.numpy as jnp
        import numpy as np
        B, L, H = (8, 512, 256)
        MASK_IDENTITY = True
        key = jax.random.key(seed)
        ks = jax.random.split(key, 7)
        s = 1.0 / np.sqrt(H)
        return {'x': jax.random.normal(ks[0], (B, L, H), dtype=jnp.float32), 'Wq': jax.random.uniform(ks[1], (H, H), jnp.float32, -s, s), 'bq': jax.random.uniform(ks[2], (H,), jnp.float32, -s, s), 'Wk': jax.random.uniform(ks[3], (H, H), jnp.float32, -s, s), 'bk': jax.random.uniform(ks[4], (H,), jnp.float32, -s, s), 'Wv': jax.random.uniform(ks[5], (H, H), jnp.float32, -s, s), 'bv': jax.random.uniform(ks[6], (H,), jnp.float32, -s, s)}
    _L2_attn_all = _L2_attn_setup()
    _L2_attn_in = {k: v for k, v in _L2_attn_all.items() if k in ('Wq', 'bq', 'Wk', 'bk', 'Wv', 'bv')}
    del _L2_attn_all

    def _L2_ffn_setup():
        import jax, jax.numpy as jnp
        import numpy as np
        B, S, H, FFN, E = (2, 512, 256, 1024, 8)
        key = jax.random.key(seed)
        k0, k1, k2, k3 = jax.random.split(key, 4)
        return {'hidden_states': jax.random.normal(k0, (B, S, H), dtype=jnp.float32), 'Wr': jax.random.normal(k1, (H, E), dtype=jnp.float32) * 0.02, 'br': jnp.zeros((E,), dtype=jnp.float32), 'W1': jax.random.normal(k2, (E, H, FFN), dtype=jnp.float32) * 0.02, 'W2': jax.random.normal(k3, (E, FFN, H), dtype=jnp.float32) * 0.02}
    _L2_ffn_all = _L2_ffn_setup()
    _L2_ffn_in = {k: v for k, v in _L2_ffn_all.items() if k in ('Wr', 'br', 'W1', 'W2')}
    del _L2_ffn_all

    def _L3_attn_setup():
        import jax, jax.numpy as jnp
        import numpy as np
        B, T = (2, 512)
        TOK, POS = (128, 128)
        H, D, KVH = (16, 64, 4)
        key = jax.random.key(seed)
        ks = jax.random.split(key, 7)

        def w(k, shape, fan_in):
            return jax.random.normal(k, shape, jnp.float32) / np.float32(np.sqrt(fan_in))
        x = jax.random.normal(ks[0], (B, T, TOK + POS), jnp.float32)
        Wq = w(ks[1], (POS, H * D), POS)
        Wk = w(ks[2], (POS, KVH * D), POS)
        Wv = w(ks[3], (TOK, KVH * D), TOK)
        Wo = w(ks[4], (H * D, TOK + POS), H * D)
        q_phase_angle = 0.1 * jax.random.normal(ks[5], (H,), jnp.float32)
        alibi_log_slopes = jnp.full((H,), np.float32(np.log(np.log(10.0))))
        return dict(x=x, Wq=Wq, Wk=Wk, Wv=Wv, Wo=Wo, q_phase_angle=q_phase_angle, alibi_log_slopes=alibi_log_slopes)
    _L3_attn_all = _L3_attn_setup()
    _L3_attn_in = {k: v for k, v in _L3_attn_all.items() if k in ('Wq', 'Wk', 'Wv', 'Wo', 'q_phase_angle', 'alibi_log_slopes')}
    del _L3_attn_all

    def _L3_ffn_setup():
        import jax, jax.numpy as jnp
        import numpy as np
        HIDDEN = 256
        FF = 1024
        N_EXPERTS = 8
        CAP_FACTOR = 1.0
        B, S = (4, 512)
        STD = 0.02

        def _gelu(x):
            return x * 0.5 * (1.0 + jax.lax.erf(x / 1.41421))
        key = jax.random.key(seed)
        ks = jax.random.split(key, 6)
        x = jax.random.normal(ks[0], (B, S, HIDDEN), dtype=jnp.float32)
        W_sw = jax.random.normal(ks[1], (HIDDEN, N_EXPERTS), dtype=jnp.float32) * STD
        b_sw = jnp.zeros((N_EXPERTS,), dtype=jnp.float32)
        W1 = jax.random.normal(ks[2], (N_EXPERTS, HIDDEN, FF), dtype=jnp.float32) * STD
        b1 = jnp.zeros((N_EXPERTS, FF), dtype=jnp.float32)
        W2 = jax.random.normal(ks[3], (N_EXPERTS, FF, HIDDEN), dtype=jnp.float32) * STD
        b2 = jnp.zeros((N_EXPERTS, HIDDEN), dtype=jnp.float32)
        return {'x': x, 'W_sw': W_sw, 'b_sw': b_sw, 'W1': W1, 'b1': b1, 'W2': W2, 'b2': b2}
    _L3_ffn_all = _L3_ffn_setup()
    _L3_ffn_in = {k: v for k, v in _L3_ffn_all.items() if k in ('W_sw', 'b_sw', 'W1', 'b1', 'W2', 'b2')}
    del _L3_ffn_all
    return {'x': x, 'txt': txt, 'L0_tok_Wa': _L0_tok_in['Wa'], 'L0_tok_ba': _L0_tok_in['ba'], 'L0_tok_Wd1': _L0_tok_in['Wd1'], 'L0_tok_bd1': _L0_tok_in['bd1'], 'L0_tok_Wd2': _L0_tok_in['Wd2'], 'L0_tok_bd2': _L0_tok_in['bd2'], 'L0_tok_Wd3': _L0_tok_in['Wd3'], 'L0_tok_bd3': _L0_tok_in['bd3'], 'L0_attn_ln_g': _L0_attn_in['ln_g'], 'L0_attn_ln_b': _L0_attn_in['ln_b'], 'L0_attn_Wq': _L0_attn_in['Wq'], 'L0_attn_bq': _L0_attn_in['bq'], 'L0_attn_Wk': _L0_attn_in['Wk'], 'L0_attn_bk': _L0_attn_in['bk'], 'L0_attn_Wv': _L0_attn_in['Wv'], 'L0_attn_bv': _L0_attn_in['bv'], 'L0_ffn_wf': _L0_ffn_in['wf'], 'L0_ffn_uf': _L0_ffn_in['uf'], 'L0_ffn_bf': _L0_ffn_in['bf'], 'L0_ffn_wi': _L0_ffn_in['wi'], 'L0_ffn_ui': _L0_ffn_in['ui'], 'L0_ffn_bi': _L0_ffn_in['bi'], 'L0_ffn_wc': _L0_ffn_in['wc'], 'L0_ffn_uc': _L0_ffn_in['uc'], 'L0_ffn_bc': _L0_ffn_in['bc'], 'L0_ffn_wo': _L0_ffn_in['wo'], 'L0_ffn_uo': _L0_ffn_in['uo'], 'L0_ffn_bo': _L0_ffn_in['bo'], 'L0_ffn_in_c': _L0_ffn_in['in_c'], 'L1_attn_w_qkva': _L1_attn_in['w_qkva'], 'L1_attn_gamma': _L1_attn_in['gamma'], 'L1_ffn_qweights': _L1_ffn_in['qweights'], 'L1_ffn_scales': _L1_ffn_in['scales'], 'L1_ffn_biases': _L1_ffn_in['biases'], 'L1_ffn_lora_a': _L1_ffn_in['lora_a'], 'L1_ffn_lora_b': _L1_ffn_in['lora_b'], 'L1_ffn_ln_gamma': _L1_ffn_in['ln_gamma'], 'L1_ffn_ln_beta': _L1_ffn_in['ln_beta'], 'L2_attn_Wq': _L2_attn_in['Wq'], 'L2_attn_bq': _L2_attn_in['bq'], 'L2_attn_Wk': _L2_attn_in['Wk'], 'L2_attn_bk': _L2_attn_in['bk'], 'L2_attn_Wv': _L2_attn_in['Wv'], 'L2_attn_bv': _L2_attn_in['bv'], 'L2_ffn_Wr': _L2_ffn_in['Wr'], 'L2_ffn_br': _L2_ffn_in['br'], 'L2_ffn_W1': _L2_ffn_in['W1'], 'L2_ffn_W2': _L2_ffn_in['W2'], 'L3_attn_Wq': _L3_attn_in['Wq'], 'L3_attn_Wk': _L3_attn_in['Wk'], 'L3_attn_Wv': _L3_attn_in['Wv'], 'L3_attn_Wo': _L3_attn_in['Wo'], 'L3_attn_q_phase_angle': _L3_attn_in['q_phase_angle'], 'L3_attn_alibi_log_slopes': _L3_attn_in['alibi_log_slopes'], 'L3_ffn_W_sw': _L3_ffn_in['W_sw'], 'L3_ffn_b_sw': _L3_ffn_in['b_sw'], 'L3_ffn_W1': _L3_ffn_in['W1'], 'L3_ffn_b1': _L3_ffn_in['b1'], 'L3_ffn_W2': _L3_ffn_in['W2'], 'L3_ffn_b2': _L3_ffn_in['b2']}

def reference(x, txt, L0_tok_Wa, L0_tok_ba, L0_tok_Wd1, L0_tok_bd1, L0_tok_Wd2, L0_tok_bd2, L0_tok_Wd3, L0_tok_bd3, L0_attn_ln_g, L0_attn_ln_b, L0_attn_Wq, L0_attn_bq, L0_attn_Wk, L0_attn_bk, L0_attn_Wv, L0_attn_bv, L0_ffn_wf, L0_ffn_uf, L0_ffn_bf, L0_ffn_wi, L0_ffn_ui, L0_ffn_bi, L0_ffn_wc, L0_ffn_uc, L0_ffn_bc, L0_ffn_wo, L0_ffn_uo, L0_ffn_bo, L0_ffn_in_c, L1_attn_w_qkva, L1_attn_gamma, L1_ffn_qweights, L1_ffn_scales, L1_ffn_biases, L1_ffn_lora_a, L1_ffn_lora_b, L1_ffn_ln_gamma, L1_ffn_ln_beta, L2_attn_Wq, L2_attn_bq, L2_attn_Wk, L2_attn_bk, L2_attn_Wv, L2_attn_bv, L2_ffn_Wr, L2_ffn_br, L2_ffn_W1, L2_ffn_W2, L3_attn_Wq, L3_attn_Wk, L3_attn_Wv, L3_attn_Wo, L3_attn_q_phase_angle, L3_attn_alibi_log_slopes, L3_ffn_W_sw, L3_ffn_b_sw, L3_ffn_W1, L3_ffn_b1, L3_ffn_W2, L3_ffn_b2):
    import jax
    import jax.numpy as jnp

    def _L0_tok_ref(x, Wa, ba, Wd1, bd1, Wd2, bd2, Wd3, bd3):
        import jax, jax.numpy as jnp
        import numpy as np
        INV_SQRT2 = 0.7071067811865476
        LEVEL = 3

        def _split(x, axis):
            ax = axis % x.ndim
            sl0 = [slice(None)] * x.ndim
            sl0[ax] = slice(0, None, 2)
            sl1 = [slice(None)] * x.ndim
            sl1[ax] = slice(1, None, 2)
            x0, x1 = (x[tuple(sl0)], x[tuple(sl1)])
            return ((x0 + x1) * INV_SQRT2, (x0 - x1) * INV_SQRT2)

        def _merge(lo, hi, axis):
            ax = axis % lo.ndim
            e = (lo + hi) * INV_SQRT2
            o = (lo - hi) * INV_SQRT2
            s = jnp.stack([e, o], axis=ax + 1)
            shape = list(lo.shape)
            shape[ax] *= 2
            return s.reshape(shape)

        def _dwt2(x):
            lo, hi = _split(x, -1)
            a, h = _split(lo, -2)
            v, d = _split(hi, -2)
            return (a, h, v, d)

        def _idwt2(a, h, v, d):
            lo = _merge(a, h, -2)
            hi = _merge(v, d, -2)
            return _merge(lo, hi, -1)
        img = x[..., 0]
        B = img.shape[0]
        details = []
        cur = img
        for _ in range(LEVEL):
            cur, h, v, d = _dwt2(cur)
            details.append((h, v, d))
        aw = jax.nn.sigmoid(cur.reshape(B, -1) @ Wa + ba)
        rec = cur * aw[:, :, None]
        det_params = [(Wd1, bd1), (Wd2, bd2), (Wd3, bd3)]
        for (h, v, d), (Wd, bd) in zip(reversed(details), det_params):
            flat = jnp.stack([h, v, d], axis=1).reshape(B, -1)
            w = jax.nn.softmax(flat @ Wd + bd, axis=-1)
            rec = _idwt2(rec, h * w[:, 0, None, None], v * w[:, 1, None, None], d * w[:, 2, None, None])
        return rec

    def _L0_attn_ref(x, ln_g, ln_b, Wq, bq, Wk, bk, Wv, bv):
        import jax, jax.numpy as jnp
        import numpy as np
        import math
        H = 16
        EPS = 1e-05
        B, T, D = x.shape
        mu = jnp.mean(x, axis=-1, keepdims=True)
        var = jnp.mean(jnp.square(x - mu), axis=-1, keepdims=True)
        xn = (x - mu) * jax.lax.rsqrt(var + EPS) * ln_g + ln_b
        q = (xn @ Wq + bq).reshape(B, T, H, D // H)
        k = (xn @ Wk + bk).reshape(B, T, H, D // H)
        v = (xn @ Wv + bv).reshape(B, T, H, D // H)
        scale = 1.0 / math.sqrt(D // H)
        attn = jnp.einsum('bnhd,bmhd->bnmh', q, k) * scale
        w = jax.nn.softmax(attn, axis=2)
        y = jnp.einsum('bnmh,bmhd->bnhd', w, v).reshape(B, T, D)
        return y

    def _L0_ffn_ref(x, wf, uf, bf, wi, ui, bi, wc, uc, bc, wo, uo, bo, in_c):
        import jax, jax.numpy as jnp
        import numpy as np
        from jax import lax
        T, B, I, M, O = (64, 64, 256, 256, 256)

        def _xavier(key, shape):
            fan_out, fan_in = shape
            limit = float(np.sqrt(6.0 / (fan_in + fan_out)))
            return jax.random.uniform(key, shape, jnp.float32, -limit, limit)
        batch = x.shape[1]
        c0 = jnp.broadcast_to(in_c, (batch, in_c.shape[0]))

        def step(c, xt):
            ft = jax.nn.sigmoid(xt @ wf.T + c @ uf.T + bf)
            it = jax.nn.sigmoid(xt @ wi.T + c @ ui.T + bi)
            gt = jnp.tanh(xt @ wc.T + c @ uc.T + bc)
            c = ft * c + it * gt
            return (c, None)
        c_final, _ = lax.scan(step, c0, x)
        h = jnp.tanh(jnp.einsum('tbi,oi->tbo', x, wo) + c_final @ uo.T + bo)
        return h

    def _L1_attn_ref(x, w_qkva, gamma):
        import jax, jax.numpy as jnp
        import numpy as np
        from jax import lax
        DIM = 256
        B, N = (4, 1024)

        def _rmsnorm(x, gamma):
            scale = jnp.asarray(x.shape[-1], x.dtype) ** 0.5
            norm = jnp.sqrt(jnp.sum(x * x, axis=-1, keepdims=True))
            return x / jnp.maximum(norm, 1e-12) * scale * gamma
        h = _rmsnorm(x, gamma)
        qkva = jnp.einsum('bnd,ed->bne', h, w_qkva)
        q, kv, a = jnp.split(qkva, 3, axis=-1)
        a = jax.nn.sigmoid(a)

        def binary_operator(e_i, e_j):
            a_i, kv_i = e_i
            a_j, kv_j = e_j
            return (a_j * a_i, a_j * kv_i + kv_j)
        _, y = lax.associative_scan(binary_operator, (a, kv), axis=1)
        return q * y

    def _L1_ffn_ref(x, qweights, scales, biases, lora_a, lora_b, ln_gamma, ln_beta):
        import jax, jax.numpy as jnp
        import numpy as np
        GROUP = 16
        EPS = 1e-05

        def _dequant(q, scale):
            w = q.astype(jnp.float32) / 7.5 - 1.0
            return w * jnp.repeat(scale, GROUP, axis=1)

        def _qlora_linear(x, q, scale, bias, la, lb):
            w = _dequant(q, scale)
            base = jnp.einsum('btd,od->bto', x, w) + bias
            lora = jnp.einsum('btr,or->bto', jnp.einsum('btd,rd->btr', x, la), lb)
            return base + lora

        def _layernorm(x, g, b):
            mu = jnp.mean(x, axis=-1, keepdims=True)
            var = jnp.mean(jnp.square(x - mu), axis=-1, keepdims=True)
            return (x - mu) * jax.lax.rsqrt(var + EPS) * g + b
        h = x
        for blk in range(3):
            i0, i1 = (2 * blk, 2 * blk + 1)
            y = _qlora_linear(h, qweights[i0], scales[i0], biases[i0], lora_a[i0], lora_b[i0])
            y = _layernorm(y, ln_gamma[blk], ln_beta[blk])
            y = jax.nn.gelu(y, approximate=False)
            y = _qlora_linear(y, qweights[i1], scales[i1], biases[i1], lora_a[i1], lora_b[i1])
            h = y + h
        return h

    def _L2_attn_ref(x, Wq, bq, Wk, bk, Wv, bv):
        import jax, jax.numpy as jnp
        import numpy as np
        B, L, H = (8, 512, 256)
        MASK_IDENTITY = True
        q = jnp.einsum('blh,oh->blo', x, Wq) + bq
        k = jnp.einsum('blh,oh->blo', x, Wk) + bk
        v = jnp.einsum('blh,oh->blo', x, Wv) + bv
        hidden = q.shape[-1]
        attn = jnp.einsum('blh,bmh->blm', q / hidden, k)
        if MASK_IDENTITY:
            mask_value = -jnp.finfo(attn.dtype).max
            eye = jnp.eye(attn.shape[-1], dtype=bool)
            attn = jnp.where(eye[None, :, :], mask_value, attn)
        attn = jax.nn.softmax(attn, axis=-1)
        return jnp.einsum('blm,bmh->blh', attn, v)

    def _L2_ffn_ref(hidden_states, Wr, br, W1, W2):
        import jax, jax.numpy as jnp
        import numpy as np
        B, S, H, FFN, E = (2, 512, 256, 1024, 8)
        b, s, h = hidden_states.shape
        x = hidden_states.reshape(-1, h)
        route = jax.nn.sigmoid(x @ Wr + br)
        max_prob = jnp.max(route, axis=1, keepdims=True)
        max_ind = jnp.argmax(route, axis=1)
        out = jnp.zeros_like(x)
        n_experts = Wr.shape[1]
        for e in range(n_experts):
            mask = (max_ind == e)[:, None].astype(x.dtype)
            y = jax.nn.gelu(x @ W1[e], approximate=False) @ W2[e]
            out = out + mask * y
        out = out * max_prob
        return out.reshape(b, s, h)

    def _L3_attn_ref(x, Wq, Wk, Wv, Wo, q_phase_angle, alibi_log_slopes):
        import jax, jax.numpy as jnp
        import numpy as np
        B, T = (2, 512)
        TOK, POS = (128, 128)
        H, D, KVH = (16, 64, 4)
        b, t, _ = x.shape
        x_tok = x[:, :, :TOK]
        x_pos = x[:, :, TOK:]
        q = (x_pos @ Wq).reshape(b, t, H, D).transpose(0, 2, 1, 3)
        k = (x_pos @ Wk).reshape(b, t, KVH, D).transpose(0, 2, 1, 3)
        v = (x_tok @ Wv).reshape(b, t, KVH, D).transpose(0, 2, 1, 3)
        c = jnp.cos(q_phase_angle)[None, :, None, None]
        s = jnp.sin(q_phase_angle)[None, :, None, None]
        q2 = q.reshape(b, H, t, D // 2, 2)
        q0, q1 = (q2[..., 0], q2[..., 1])
        q = jnp.stack([q0 * c - q1 * s, q0 * s + q1 * c], axis=-1).reshape(b, H, t, D)
        rep = H // KVH
        k = jnp.repeat(k, rep, axis=1)
        v = jnp.repeat(v, rep, axis=1)
        att = jnp.einsum('bhqd,bhkd->bhqk', q, k) / np.float32(np.sqrt(D))
        pos = jnp.arange(t)
        rel = (pos[:, None] - pos[None, :]).astype(jnp.float32)
        att = att + jnp.exp(alibi_log_slopes)[None, :, None, None] * rel[None, None]
        mask = pos[:, None] >= pos[None, :]
        att = jnp.where(mask[None, None], att, -jnp.inf)
        m = jnp.max(att, axis=-1, keepdims=True)
        e = jnp.exp(att - m)
        att = e / (1.0 + jnp.sum(e, axis=-1, keepdims=True))
        out = jnp.einsum('bhqk,bhkd->bhqd', att, v)
        out = out.transpose(0, 2, 1, 3).reshape(b, t, H * D)
        return out @ Wo

    def _L3_ffn_ref(x, W_sw, b_sw, W1, b1, W2, b2):
        import jax, jax.numpy as jnp
        import numpy as np
        HIDDEN = 256
        FF = 1024
        N_EXPERTS = 8
        CAP_FACTOR = 1.0
        B, S = (4, 512)
        STD = 0.02

        def _gelu(x):
            return x * 0.5 * (1.0 + jax.lax.erf(x / 1.41421))
        Bb, Ss, D = x.shape
        T = Bb * Ss
        E = W1.shape[0]
        capacity = int(CAP_FACTOR * T / E)
        xf = x.reshape(T, D)
        logits = xf @ W_sw + b_sw
        probs = jax.nn.softmax(logits, axis=-1)
        pmax = jnp.max(probs, axis=-1)
        routes = jnp.argmax(probs, axis=-1)
        factor = pmax / jax.lax.stop_gradient(pmax)
        xs = xf * factor[:, None]
        onehot = jax.nn.one_hot(routes, E, dtype=jnp.int32)
        pos = jnp.cumsum(onehot, axis=0) - 1
        pos_tok = jnp.take_along_axis(pos, routes[:, None], axis=1)[:, 0]
        keep = pos_tok < capacity
        pos_safe = jnp.where(keep, pos_tok, capacity)
        buf = jnp.zeros((E, capacity + 1, D), dtype=xs.dtype)
        buf = buf.at[routes, pos_safe].set(xs)
        buf = buf[:, :capacity]
        h = _gelu(jnp.einsum('ecd,edf->ecf', buf, W1) + b1[:, None, :])
        expert_out = jnp.einsum('ecf,efd->ecd', h, W2) + b2[:, None, :]
        gathered = expert_out[routes, jnp.minimum(pos_tok, capacity - 1)]
        final = jnp.where(keep[:, None], gathered, xs)
        return final.reshape(Bb, Ss, D)
    h = _L0_tok_ref(x, L0_tok_Wa, L0_tok_ba, L0_tok_Wd1, L0_tok_bd1, L0_tok_Wd2, L0_tok_bd2, L0_tok_Wd3, L0_tok_bd3)
    h = jnp.concatenate([h, txt], axis=1)
    h = h + _L0_attn_ref(_layernorm(h, axis=-1), L0_attn_ln_g, L0_attn_ln_b, L0_attn_Wq, L0_attn_bq, L0_attn_Wk, L0_attn_bk, L0_attn_Wv, L0_attn_bv)
    h = h + _L0_ffn_ref(_layernorm(h, axis=-1), L0_ffn_wf, L0_ffn_uf, L0_ffn_bf, L0_ffn_wi, L0_ffn_ui, L0_ffn_bi, L0_ffn_wc, L0_ffn_uc, L0_ffn_bc, L0_ffn_wo, L0_ffn_uo, L0_ffn_bo, L0_ffn_in_c)
    h = h + _L1_attn_ref(_layernorm(h, axis=-1), L1_attn_w_qkva, L1_attn_gamma)
    h = h + _L1_ffn_ref(_layernorm(h, axis=-1), L1_ffn_qweights, L1_ffn_scales, L1_ffn_biases, L1_ffn_lora_a, L1_ffn_lora_b, L1_ffn_ln_gamma, L1_ffn_ln_beta)
    h = h + _L2_attn_ref(_layernorm(h, axis=-1), L2_attn_Wq, L2_attn_bq, L2_attn_Wk, L2_attn_bk, L2_attn_Wv, L2_attn_bv)
    h = h + _L2_ffn_ref(_layernorm(h, axis=-1), L2_ffn_Wr, L2_ffn_br, L2_ffn_W1, L2_ffn_W2)
    h = h + _L3_attn_ref(_layernorm(h, axis=-1), L3_attn_Wq, L3_attn_Wk, L3_attn_Wv, L3_attn_Wo, L3_attn_q_phase_angle, L3_attn_alibi_log_slopes)
    h = h + _L3_ffn_ref(_layernorm(h, axis=-1), L3_ffn_W_sw, L3_ffn_b_sw, L3_ffn_W1, L3_ffn_b1, L3_ffn_W2, L3_ffn_b2)
    return h

_drawn_inputs = setup_inputs


def setup_inputs(seed=0):
    import zlib

    import numpy as np

    out = dict(_drawn_inputs(seed))
    spreads = {'L0_tok_bd1': (0.0, 0.308),
     'L0_tok_bd2': (0.0, 0.389),
     'L0_tok_bd3': (0.0, 0.51),
     'L0_attn_ln_g': (1.0, 0.2),
     'L0_attn_ln_b': (0.0, 0.1),
     'L0_attn_bq': (0.0, 0.1),
     'L0_attn_bk': (0.0, 2.0),
     'L0_attn_bv': (0.0, 0.1),
     'L0_ffn_bf': (0.0, 0.314),
     'L0_ffn_bi': (0.0, 0.311),
     'L0_ffn_bc': (0.0, 0.1),
     'L0_ffn_bo': (0.0, 0.1),
     'L0_ffn_in_c': (0.0, 0.412),
     'L1_attn_gamma': (1.0, 0.2),
     'L1_ffn_ln_gamma': (1.0, 0.2),
     'L1_ffn_ln_beta': (0.0, 0.1),
     'L2_ffn_br': (0.0, 0.8),
     'L3_attn_alibi_log_slopes': (0.834032416343689, 0.6),
     'L3_ffn_b_sw': (0.0, 0.1),
     'L3_ffn_b1': (0.0, 0.8),
     'L3_ffn_b2': (0.0, 0.726)}
    factors = {'L1_ffn_biases': 5.303,
     'L1_ffn_lora_a': 3.981,
     'L1_ffn_lora_b': 4.056,
     'L2_attn_Wq': 8.0,
     'L2_attn_bq': 25.796,
     'L2_attn_Wk': 8.0,
     'L2_attn_bk': 64.0,
     'L2_attn_bv': 5.186,
     'L2_ffn_Wr': 4.854,
     'L2_ffn_W1': 4.524,
     'L2_ffn_W2': 4.435,
     'L3_attn_Wq': 4.171,
     'L3_attn_Wk': 4.865,
     'L3_attn_q_phase_angle': 8.0,
     'L3_ffn_W1': 4.672,
     'L3_ffn_W2': 4.305}
    for name, (base, spread) in spreads.items():
        noise = np.random.default_rng([zlib.crc32(name.encode()), seed]).standard_normal(out[name].shape)
        drawn = base * np.exp(spread * noise) if base else spread * noise
        out[name] = jnp.asarray(drawn.astype(out[name].dtype))
    for name, factor in factors.items():
        out[name] = (out[name] * factor).astype(out[name].dtype)
    return out
```

```python
from contextlib import ExitStack

import concourse.bass as bass
from concourse import mybir

F32 = mybir.dt.float32
BF16 = mybir.dt.bfloat16
I32 = mybir.dt.int32
U32 = mybir.dt.uint32
ALU = mybir.AluOpType
ACT = mybir.ActivationFunctionType
AX = mybir.AxisListType

B = 8
T = 333
TT = 111
NT = 3
NTILES = B * NT
D = 256
KT = 2
IMG = 256
TXT = 77
EPS = 1e-5
E = 8

WNAMES = ["a_q", "a_k", "a_v", "f_wf", "f_uf", "f_wi", "f_ui", "f_wc", "f_uc", "f_wo", "f_uo",
          "s_q", "s_kv", "s_a", "m_q", "m_k", "m_v"]
WIDX = {n: i for i, n in enumerate(WNAMES)}
CNAMES = ["a_g", "a_b", "a_bq", "a_bk", "f_bf", "f_bi", "f_bc", "f_bo", "f_c0", "s_g", "q_g0", "q_g1",
          "q_g2", "q_b0", "q_b1", "q_b2", "m_bq", "m_bk"]
CIDX = {n: i for i, n in enumerate(CNAMES)}
RNAMES = ["a_bv", "m_bv", "q_0", "q_1", "q_2", "q_3", "q_4", "q_5"]
RIDX = {n: i for i, n in enumerate(RNAMES)}


class Shared:

    def __init__(self, nc, ctx, ins):
        sb = lambda name, shape, dt=F32: ctx.enter_context(nc.sbuf_tensor(name, shape, dt))
        self.nc, self.ins = nc, ins
        self.h = sb("h", [TT, NTILES, D])
        self.mv = sb("mv", [TT, NTILES, 2])
        self.rs = sb("rs", [TT, NTILES])
        self.moments = sb("moments", [TT, NT, 6])
        self.batch_mv = sb("batch_mv", [TT, NT, 2])
        self.ident = sb("ident", [128, 128])
        self.eps = sb("eps", [128, NTILES])
        self.mhalf = sb("mhalf", [128, NTILES])

    def early(self, ctx):
        sb = lambda name, shape: ctx.enter_context(self.nc.sbuf_tensor(name, shape, F32))
        self.cols = sb("cols", [128, len(CNAMES), KT])
        self.rows = sb("rows", [TT, len(RNAMES), D])
        self.w = sb("w", [128, len(WNAMES), KT, D])
        self.weights_in = ctx.enter_context(self.nc.semaphore("weights_in"))

    def col(self, name, k):
        return self.cols[:, CIDX[name], k:k + 1]

    def row(self, name):
        return self.rows[:, RIDX[name], :]

    def wt(self, name, k, a, b):
        return self.w[:, WIDX[name], k, a:b]


def both(eng, body, first=0):
    with eng.Fori(0, B // 2 - 1) as i:
        body(2 * i, 0, True)
        body(2 * i + 1, 1, True)
    body(B - 2, 0, True)
    body(B - 1, 1, False)


def batch_stats(nc, vector, sh, b, src=None, dst=None):
    v = nc.vector
    src = sh.h if src is None else src
    dst = sh.mv if dst is None else dst
    for t in range(NT):
        v.bn_stats(sh.moments[:, t, :], src[:, NT * b + t, :])
    vector.drain()
    for t in range(NT):
        v.bn_aggr(sh.batch_mv[:, t, :], sh.moments[:, t, :])
    vector.drain()
    v.tensor_copy(dst[:, bass.ds(NT * b, NT), :], sh.batch_mv[:, :, :])


def tokenise(nc, sh, ins, h0):
    RB = 16
    n1, n2, n3 = 8 * 128, 4 * 64, 2 * 32
    with ExitStack() as ctx:
        sb = lambda name, shape, dt=F32: ctx.enter_context(nc.sbuf_tensor(name, shape, dt))
        sem = lambda name: ctx.enter_context(nc.semaphore(name))
        img = sb("img", [128, RB, IMG])
        out = sb("img_out", [128, RB, IMG])
        s = sb("haar_s", [128, RB, 128])
        d = sb("haar_d", [128, RB, 128])
        a1 = sb("a1", [128, 8, 128])
        a2 = sb("a2", [128, 4, 64])
        a3 = sb("a3", [128, 2, 32])
        det = [sb("det1", [128, 3, n1]), sb("det2", [128, 3, n2]), sb("det3", [128, 3, n3])]
        wd = [sb("wd1", [128, 3, 3 * n1]), sb("wd2", [128, 3, 3 * n2]), sb("wd3", [128, 3, 3 * n3])]
        wa = sb("wa", [128, n3])
        gb = sb("gb", [128, 10])
        gs = sb("gs", [128, 10])
        group = sb("group", [128, 128])
        dots = sb("dots", [128, 10])
        z = sb("z", [128, 10])
        zm = sb("zm", [128, 3])
        ez = sb("ez", [128, 10])
        ps = ctx.enter_context(nc.psum_tensor("ps_gate", [128, 512], F32))
        img_in, wa_in, h0_out, h_in, txt_out = (sem(n) for n in ("img_in", "wa_in", "h0_out", "h_in", "txt_out"))
        wd_in = [sem(f"wd_in{i}") for i in range(3)]
        dots_done, summed, z_ready, exp_done, image_ready, group_ready = (
            sem(n) for n in ("dots_done", "summed", "z_ready", "exp_done", "image_ready", "group_ready"))
        const_ready = sem("const_ready")
        block = ctx.enter_context(nc.Block())

        @block.sync
        def _(sync):
            sync.dma_start(img[:, :, :], ins["x"].rearrange("(p r) c -> p r c", r=RB)).then_inc(img_in, 16)
            for lv in (2, 1, 0):
                for b in range(B):
                    sync.dma_start(wd[lv][16 * b:16 * b + 16, :, :], ins[f"wd{lv}"]).then_inc(wd_in[lv], 16)
            sync.dma_start(h0[:, IMG:T, :], ins["txt"]).then_inc(txt_out, 16)
            sync.wait_ge(image_ready, 1)
            for b in range(B):
                sync.dma_start(h0[b, 0:IMG, :].rearrange("(p r) c -> p r c", r=RB),
                               out[16 * b:16 * b + 16, :, :]).then_inc(h0_out, 16)
            sync.wait_ge(txt_out, 16)
            sync.wait_ge(h0_out, 16 * B)
            sync.dma_start(sh.h[:, :, :],
                           h0.rearrange("b (t p) c -> p (b t) c", p=TT)).then_inc(h_in, 16)
            sync.wait_ge(sh.weights_in, 48)

        @block.gpsimd
        def _(pool):
            nc.gpsimd.memset(sh.ident[:, :], 0.0)
            nc.gpsimd.memset(group[:, :], 1.0)
            nc.gpsimd.memset(sh.eps[:, :], EPS)
            nc.gpsimd.memset(sh.mhalf[:, :], -0.5)
            pool.drain()
            nc.gpsimd.affine_select(out=sh.ident[:, :], in_=sh.ident[:, :], compare_op=ALU.not_equal, fill=1.0,
                                    base=0, pattern=[[-1, 128]], channel_multiplier=1)
            g3 = group[:, :].rearrange("p (g r) -> p g r", r=16)
            nc.gpsimd.affine_select(out=g3, in_=g3, compare_op=ALU.is_ge, fill=0.0,
                                    base=0, pattern=[[-16, 8], [0, 16]], channel_multiplier=1)
            pool.drain()
            nc.gpsimd.affine_select(out=g3, in_=g3, compare_op=ALU.is_ge, fill=0.0,
                                    base=15, pattern=[[16, 8], [0, 16]],
                                    channel_multiplier=-1).then_inc(group_ready, 1)

        @block.scalar
        def _(act):
            act.dma_start(wa[:, :], ins["wa"]).then_inc(wa_in, 16)
            act.dma_start(gb[:, :], ins["gb"].partition_broadcast(128)).then_inc(wa_in, 16)
            act.dma_start(sh.cols[:, :, :], ins["cols"]).then_inc(sh.weights_in, 16)
            act.dma_start(sh.rows[:, :, :], ins["rows"].partition_broadcast(TT)).then_inc(sh.weights_in, 16)
            act.dma_start(sh.w[:, :, :, :], ins["w"]).then_inc(sh.weights_in, 16)
            act.wait_ge(z_ready, 1)
            nc.scalar.activation(ez[:, 0:1], z[:, 0:1], ACT.Exp, scale=-1.0)
            nc.scalar.activation(ez[:, 1:10], z[:, 1:10], ACT.Exp).then_inc(exp_done, 1)

        @block.tensor
        def _(pe):
            pe.wait_ge(group_ready, 1)
            pe.wait_ge(dots_done, 1)
            nc.tensor.matmul(ps[:, 0:10], group[:, :], dots[:, :], start=True, stop=True).then_inc(summed, 1)

        @block.vector
        def _(dve):
            v = nc.vector
            dve.wait_ge(img_in, 16)

            def analysis(src, rows, cols, approx, details):
                s_ = s[:, 0:rows, 0:cols // 2]
                d_ = d[:, 0:rows, 0:cols // 2]
                v.tensor_tensor(s_, src[:, :, 0:cols:2], src[:, :, 1:cols:2], ALU.add)
                v.tensor_tensor(d_, src[:, :, 0:cols:2], src[:, :, 1:cols:2], ALU.subtract)
                dve.drain()
                dt = details[:, :, :].rearrange("p j (r c) -> p j r c", c=cols // 2)
                v.tensor_tensor(approx, s_[:, 0:rows:2, :], s_[:, 1:rows:2, :], ALU.add)
                v.tensor_tensor(dt[:, 0], s_[:, 0:rows:2, :], s_[:, 1:rows:2, :], ALU.subtract)
                v.tensor_tensor(dt[:, 1], d_[:, 0:rows:2, :], d_[:, 1:rows:2, :], ALU.add)
                v.tensor_tensor(dt[:, 2], d_[:, 0:rows:2, :], d_[:, 1:rows:2, :], ALU.subtract)
                dve.drain()

            analysis(img, 16, 256, a1[:, :, :], det[0])
            analysis(a1, 8, 128, a2[:, :, :], det[1])
            analysis(a2, 4, 64, a3[:, :, :], det[2])
            for c, lv in enumerate((2, 1, 0)):
                v.memset(gs[:, 1 + 3 * c:4 + 3 * c], 2.0 ** -(lv + 1))
            v.memset(gs[:, 0:1], 2.0 ** -3)
            dve.wait_ge(wa_in, 32)
            junk = out[:, :, :].rearrange("p r c -> p (r c)")
            v.tensor_tensor_reduce(junk[:, 0:n3], a3[:, :, :].rearrange("p r c -> p (r c)"), wa[:, :], 1.0, 0.0,
                                   ALU.mult, ALU.add, dots[:, 0:1])
            for c, (lv, n) in enumerate(((2, n3), (1, n2), (0, n1))):
                dve.wait_ge(wd_in[lv], 16 * B)
                for j in range(3):
                    dve.drain()
                    r = v.tensor_tensor_reduce(junk[:, 0:3 * n], det[lv][:, :, :].rearrange("p j n -> p (j n)"),
                                               wd[lv][:, j, :], 1.0, 0.0, ALU.mult, ALU.add,
                                               dots[:, 1 + 3 * c + j:2 + 3 * c + j])
            r.then_inc(dots_done, 1)
            dve.wait_ge(summed, 1)
            v.tensor_tensor(z[:, :], ps[:, 0:10], gs[:, :], ALU.mult)
            dve.drain()
            v.tensor_tensor(z[:, :], z[:, :], gb[:, :], ALU.add)
            dve.drain()
            z3 = z[:, 1:10].rearrange("p (l j) -> p l j", j=3)
            v.tensor_reduce(zm[:, :], z3, AX.X, ALU.max)
            dve.drain()
            v.tensor_tensor(z3, z3, zm[:, :].unsqueeze(2).to_broadcast([128, 3, 3]), ALU.subtract).then_inc(z_ready, 1)
            dve.wait_ge(exp_done, 1)
            e3 = ez[:, 1:10].rearrange("p (l j) -> p l j", j=3)
            v.tensor_reduce(zm[:, :], e3, AX.X, ALU.add)
            v.tensor_scalar(ez[:, 0:1], ez[:, 0:1], 1.0, None, ALU.add)
            dve.drain()
            v.reciprocal(zm[:, :], zm[:, :])
            v.reciprocal(ez[:, 0:1], ez[:, 0:1])
            dve.drain()
            v.tensor_tensor(e3, e3, zm[:, :].unsqueeze(2).to_broadcast([128, 3, 3]), ALU.mult)
            dve.drain()
            for a, b, f in ((0, 4, 2.0 ** -6), (4, 7, 2.0 ** -4), (7, 10, 2.0 ** -2)):
                v.tensor_scalar(ez[:, a:b], ez[:, a:b], f, None, ALU.mult)
            dve.drain()
            v.tensor_scalar(z[:, :], ez[:, :], -1.0, None, ALU.mult)
            dve.drain()
            v.tensor_scalar(a3[:, :, :], a3[:, :, :], ez[:, 0:1], None, ALU.mult)
            dve.drain()

            def synthesis(rec, details, g, rows, cols, dst):
                dt = details[:, :, :].rearrange("p j (r c) -> p j r c", c=cols)
                lo = s[:, 0:2 * rows, 0:cols]
                hi = d[:, 0:2 * rows, 0:cols]
                w = lambda j: ez[:, g + j:g + j + 1]
                nw = lambda j: z[:, g + j:g + j + 1]
                v.scalar_tensor_tensor(lo[:, 0:2 * rows:2, :], dt[:, 0], w(0), rec, ALU.mult, ALU.add)
                v.scalar_tensor_tensor(lo[:, 1:2 * rows:2, :], dt[:, 0], nw(0), rec, ALU.mult, ALU.add)
                v.tensor_scalar(dt[:, 1], dt[:, 1], w(1), None, ALU.mult)
                dve.drain()
                v.scalar_tensor_tensor(hi[:, 0:2 * rows:2, :], dt[:, 2], w(2), dt[:, 1], ALU.mult, ALU.add)
                v.scalar_tensor_tensor(hi[:, 1:2 * rows:2, :], dt[:, 2], nw(2), dt[:, 1], ALU.mult, ALU.add)
                dve.drain()
                v.tensor_tensor(dst[:, :, 0:2 * cols:2], lo, hi, ALU.add)
                r = v.tensor_tensor(dst[:, :, 1:2 * cols:2], lo, hi, ALU.subtract)
                return r

            synthesis(a3[:, :, :], det[2], 1, 2, 32, a2)
            dve.drain()
            synthesis(a2[:, :, :], det[1], 4, 4, 64, a1)
            dve.drain()
            synthesis(a1[:, :, :], det[0], 7, 8, 128, out).then_inc(image_ready, 1)
            dve.wait_ge(h_in, 16)
            with dve.Fori(0, B) as b:
                batch_stats(nc, dve, sh, b)


def token_scale(nc, pool, sh, tmp, kind, done):
    g = nc.gpsimd
    var, r = sh.mv[:, :, 1], sh.rs[:, :]
    a, b = tmp[:, 0, :], tmp[:, 1, :]
    eps, mh = sh.eps[0:TT, :], sh.mhalf[0:TT, :]
    g.tensor_tensor(a, var, eps, ALU.add)
    pool.drain()
    if kind == "plain":
        g.tensor_tensor(r, a, mh, ALU.pow).then_inc(done, 1)
        return
    g.tensor_tensor(r, a, mh, ALU.pow)
    pool.drain()
    g.tensor_tensor(b, r, r, ALU.mult)
    pool.drain()
    g.tensor_tensor(b, b, var, ALU.mult)
    pool.drain()
    if kind == "twice":
        g.tensor_tensor(b, b, eps, ALU.add)
        pool.drain()
    else:
        g.tensor_scalar(b, b, 1e-24 / D, None, ALU.max)
        pool.drain()
    g.tensor_tensor(b, b, mh, ALU.pow)
    pool.drain()
    g.tensor_tensor(r, r, b, ALU.mult).then_inc(done, 1)


def attention16(nc, sh, fills):
    H, DH = 16, 16
    HC = 8
    NU = H * NT
    NP = 9
    with ExitStack() as ctx:
        sb = lambda name, shape, dt=F32: ctx.enter_context(nc.sbuf_tensor(name, shape, dt))
        pb = lambda name: ctx.enter_context(nc.psum_tensor(name, [128, 512], F32))
        sem = lambda name: ctx.enter_context(nc.semaphore(name))
        xn = sb("xn", [TT, NT, D])
        xT = sb("xT", [128, KT, T])
        qT = [sb(f"qT{i}", [128, KT, T]) for i in range(2)]
        kT = [sb(f"kT{i}", [128, KT, T]) for i in range(2)]
        vS = [sb(f"vS{i}", [TT, NT, H, 32]) for i in range(2)]
        kz = [sb(f"kz{i}", [128, T]) for i in range(3)]
        P = [sb(f"P{i}", [TT, T]) for i in range(3)]
        PT = [sb(f"PT{i}", [TT, NT, T]) for i in range(2)]
        oS = sb("oS", [128, T])
        nm = sb("nm", [TT, 4])
        rec = sb("rec", [TT, NT, 4])
        tmp = sb("tmp", [TT, NT, 4, DH])
        ps_tmp = sb("ps_tmp", [TT, 2, NTILES])
        hm = sb("hm", [128, HC])
        bq4 = sb("bq4", [128, KT])
        zeros = sb("zeros", [128, 1792])
        psS = [pb(f"psS{i}") for i in range(3)]
        psP = [pb(f"psP{i}") for i in range(2)]
        psO, psOT, psM = pb("psO"), pb("psOT"), pb("psM")
        (scaled, consts, xn_ready, piece_done, piece_out, s_done, max_done, exp_done, t_done, pt_done, pv_done,
         o_out, ot_done, o_added, kz_ready, head_begun) = (sem(n) for n in (
             "scaled", "consts", "xn_ready", "piece_done", "piece_out", "s_done", "max_done", "exp_done", "t_done",
             "pt_done", "pv_done", "o_out", "ot_done", "o_added", "kz_ready", "head_begun"))
        filled = sem("filled")
        block = ctx.enter_context(nc.Block())
        qt = lambda a: slice(a * TT, (a + 1) * TT)

        @block.sync
        def _(sync):
            sync.wait_ge(consts, 3)
            n = 0
            for f in fills:
                parts = 128 if f.shape[0] % 128 == 0 else TT
                flat = f.rearrange("(p r) c -> p (r c)", p=parts)
                for a in range(0, flat.shape[1], 1792):
                    m = min(1792, flat.shape[1] - a)
                    sync.dma_start(flat[:, a:a + m], zeros[0:parts, 0:m]).then_inc(filled, 16)
                    n += 16
            sync.wait_ge(filled, n)

        @block.gpsimd
        def _(pool):
            token_scale(nc, pool, sh, ps_tmp, "twice", scaled)
            nc.gpsimd.memset(zeros[:, :], 0.0).then_inc(consts, 1)
            nc.gpsimd.memset(hm[:, :], 1.0)
            pool.drain()
            nc.gpsimd.affine_select(out=hm[:, :], in_=hm[:, :], compare_op=ALU.is_ge, fill=0.0, base=0,
                                    pattern=[[-DH, HC]], channel_multiplier=1)
            pool.drain()
            nc.gpsimd.affine_select(out=hm[:, :], in_=hm[:, :], compare_op=ALU.is_ge, fill=0.0, base=DH - 1,
                                    pattern=[[DH, HC]], channel_multiplier=-1)
            for p in range(2):
                nc.gpsimd.memset(vS[p][:, :, :, DH:32], 0.0)
            pool.drain()
            for p in range(2):
                c = nc.gpsimd.memset(vS[p][:, :, :, DH:DH + 1], 1.0)
            c.then_inc(consts, 1)
            pool.drain()

            def body(b, p, has_next):
                pool.wait_ge(piece_out, NP * b + 6)
                for h in range(H):
                    pool.wait_ge(s_done, NU * b + (3 * (h - 3) + 3 if h >= 3 else 0))
                    pool.sem_inc(head_begun, 1)
                    nc.gpsimd.tensor_scalar(kz[h % 3][:, :], kT[p][:, h // HC, :], hm[:, h % HC:h % HC + 1], None,
                                            ALU.mult).then_inc(kz_ready, 1)
            both(pool, body)

        @block.vector
        def _(dve):
            v = nc.vector
            v.tensor_scalar(bq4[:, :], sh.cols[:, CIDX["a_bq"], :], DH ** -0.5, None, ALU.mult).then_inc(consts, 1)
            dve.wait_ge(scaled, 1)
            dve.wait_ge(consts, 3)

            def norm(b):
                for t in range(NT):
                    r = v.tensor_scalar(xn[:, t, :], sh.h[:, 3 * b + t, :], sh.mv[:, 3 * b + t, 0:1],
                                        sh.rs[:, bass.ds(3 * b + t, 1)], ALU.subtract, ALU.mult)
                r.then_inc(xn_ready, 1)

            def piece(b, p, k):
                if k >= 6:
                    dve.wait_ge(piece_done, NP * b + k + 1)
                    v.tensor_tensor(vS[p][:, k - 6, :, 0:DH], psM[0:TT, 0:D].rearrange("p (h d) -> p h d", d=DH),
                                    sh.row("a_bv").rearrange("p (h d) -> p h d", d=DH),
                                    ALU.add).then_inc(piece_out, 1)

            def row_max(b, u):
                dve.wait_ge(s_done, NU * b + u + 1)
                v.tensor_reduce(nm[:, u % 4:u % 4 + 1], psS[u % 3][0:TT, 0:T], AX.X, ALU.max,
                                negate=True).then_inc(max_done, 1)

            def turned(b, u):
                h = u // 3
                dve.wait_ge(t_done, NU * b + u + 1)
                if u % 3 == 0:
                    dve.wait_ge(pv_done, H * b + (h - 1 if h >= 2 else 0))
                v.tensor_copy(PT[h % 2][:, :, qt(u % 3)],
                              psP[u % 2][0:TT, 0:T].rearrange("k (a q) -> k a q", a=NT)).then_inc(pt_done, 1)

            def combine(b, g):
                dve.wait_ge(ot_done, 4 * b + g + 1)
                o4 = psOT[0:TT, 0:384].rearrange("q (t h d) -> q t h d", t=NT, h=4)
                v.reciprocal(rec[:, :, :], o4[:, :, :, DH])
                dve.drain()
                for t in range(NT):
                    v.tensor_tensor(tmp[:, t], o4[:, t, :, 0:DH],
                                    rec[:, t].unsqueeze(2).to_broadcast([TT, 4, DH]), ALU.mult)
                dve.drain()
                for t in range(NT):
                    hh = sh.h[:, 3 * b + t, 64 * g:64 * g + 64]
                    r = v.tensor_tensor(hh, hh, tmp[:, t].rearrange("q h d -> q (h d)"), ALU.add)
                r.then_inc(o_added, 1)

            norm(0)
            for k in range(NP):
                piece(0, 0, k)

            def body(b, p, has_next):
                for u in range(NU):
                    row_max(b, u)
                    if u >= 2:
                        turned(b, u - 2)
                    if u == 2 and has_next:
                        dve.wait_ge(piece_done, NP * b + NP)
                        norm(b + 1)
                    if u % 3 == 1 and has_next and 0 <= u // 3 - 2 < NP:
                        piece(b + 1, 1 - p, u // 3 - 2)
                    if u % 12 == 10 and u > 12:
                        combine(b, u // 12 - 1)
                turned(b, NU - 2)
                turned(b, NU - 1)
                combine(b, 3)
                dve.drain()
                batch_stats(nc, dve, sh, b)
            both(dve, body)

        @block.scalar
        def _(act):
            s = nc.scalar
            act.wait_ge(consts, 3)

            def piece(b, p, k):
                if k >= 6:
                    return
                act.wait_ge(piece_done, NP * b + k + 1)
                src = psM[:, 0:T]
                j = k % 2
                if k < 2:
                    r = s.activation(xT[:, j, :], src, ACT.Identity, bias=sh.col("a_b", j), scale=sh.col("a_g", j))
                elif k < 4:
                    r = s.activation(qT[p][:, j, :], src, ACT.Identity, bias=bq4[:, j:j + 1], scale=DH ** -0.5)
                else:
                    r = s.activation(kT[p][:, j, :], src, ACT.Identity, bias=sh.col("a_bk", j))
                r.then_inc(piece_out, 1)

            def exp(b, u):
                act.wait_ge(max_done, NU * b + u + 1)
                act.wait_ge(t_done, NU * b + (u - 2 if u >= 3 else 0))
                s.activation(P[u % 3][:, :], psS[u % 3][0:TT, 0:T], ACT.Exp,
                             bias=nm[:, u % 4:u % 4 + 1]).then_inc(exp_done, 1)

            def out(b, g):
                act.wait_ge(pv_done, H * b + 4 * g + 4)
                act.wait_ge(ot_done, 4 * b + g)
                s.activation(oS[:, :], psO[:, 0:T], ACT.Copy).then_inc(o_out, 1)

            for k in range(NP):
                piece(0, 0, k)

            def body(b, p, has_next):
                for u in range(NU):
                    exp(b, u)
                    if u % 3 == 1 and has_next and 0 <= u // 3 - 2 < NP:
                        piece(b + 1, 1 - p, u // 3 - 2)
                    if u % 12 == 5 and u > 12:
                        out(b, u // 12 - 1)
                out(b, 3)
            both(act, body)

        @block.tensor
        def _(pe):
            mm = nc.tensor.matmul

            def piece(b, p, k):
                if k == 0:
                    pe.wait_ge(xn_ready, b + 1)
                pe.wait_ge(piece_out, NP * b + k)
                j = k % 2
                if k < 2:
                    for t in range(NT):
                        r = nc.tensor.transpose(psM[:, qt(t)], xn[:, t, 128 * j:128 * j + 128],
                                                sh.ident[0:TT, 0:TT])
                elif k < 6:
                    for c in range(KT):
                        r = mm(psM[:, 0:T], sh.wt("a_q" if k < 4 else "a_k", c, 128 * j, 128 * j + 128),
                               xT[:, c, :], start=c == 0, stop=c == KT - 1)
                else:
                    for c in range(KT):
                        r = mm(psM[0:TT, 0:D], xT[:, c, qt(k - 6)], sh.wt("a_v", c, 0, D),
                               start=c == 0, stop=c == KT - 1)
                r.then_inc(piece_done, 1)

            def scores(b, p, u):
                h = u // 3
                if u % 3 == 0:
                    pe.wait_ge(kz_ready, H * b + h + 1)
                pe.wait_ge(exp_done, NU * b + (u - 2 if u >= 3 else 0))
                mm(psS[u % 3][0:TT, 0:T], qT[p][:, h // HC, qt(u % 3)], kz[h % 3][:, :],
                   start=True, stop=True).then_inc(s_done, 1)

            def turn(b, u):
                pe.wait_ge(exp_done, NU * b + u + 1)
                pe.wait_ge(pt_done, NU * b + (u - 1 if u >= 2 else 0))
                for a in range(NT):
                    r = nc.tensor.transpose(psP[u % 2][0:TT, qt(a)], P[u % 3][:, qt(a)], sh.ident[0:TT, 0:TT])
                r.then_inc(t_done, 1)

            def values(b, p, h):
                pe.wait_ge(pt_done, NU * b + 3 * h + 3)
                if h % 4 == 0:
                    pe.wait_ge(o_out, 4 * b + h // 4)
                s = 32 * (h % 4)
                for a in range(NT):
                    r = mm(psO[s:s + 32, 0:T], vS[p][:, a, h, :], PT[h % 2][:, a, :],
                           start=a == 0, stop=a == NT - 1)
                r.then_inc(pv_done, 1)

            def back(b, g):
                pe.wait_ge(o_out, 4 * b + g + 1)
                pe.wait_ge(o_added, 4 * b + g)
                for t in range(NT):
                    r = nc.tensor.transpose(psOT[0:TT, 128 * t:128 * t + 128], oS[:, qt(t)], sh.ident[:, :])
                r.then_inc(ot_done, 1)

            for k in range(NP):
                piece(0, 0, k)

            def body(b, p, has_next):
                pe.wait_ge(piece_out, NP * b + NP)
                scores(b, p, 0)
                scores(b, p, 1)
                for u in range(NU):
                    if u + 2 < NU:
                        scores(b, p, u + 2)
                    turn(b, u)
                    h = u // 3
                    if u % 3 == 1 and h >= 1:
                        values(b, p, h - 1)
                    if u % 3 == 2 and has_next and 0 <= h - 1 < NP:
                        piece(b + 1, 1 - p, h - 1)
                    if u % 12 == 7 and u > 12:
                        back(b, u // 12 - 1)
                values(b, p, H - 1)
                back(b, 3)
            both(pe, body)


def recurrence(nc, sh):
    with ExitStack() as ctx:
        sb = lambda name, shape, dt=F32: ctx.enter_context(nc.sbuf_tensor(name, shape, dt))
        pb = lambda name: ctx.enter_context(nc.psum_tensor(name, [128, 512], F32))
        sem = lambda name: ctx.enter_context(nc.semaphore(name))
        xn = sb("r_xn", [TT, NT, D])
        xT = sb("r_xT", [128, B, KT, T])
        c = sb("r_c", [128, KT, T])
        gates = [sb(f"r_g{i}", [128, KT, T]) for i in range(3)]
        cu = sb("r_cu", [128, KT, T])
        y = [sb(f"r_y{i}", [128, KT, T]) for i in range(2)]
        ps_tmp = sb("r_tmp", [TT, 2, NTILES])
        ps = [pb(f"r_ps{i}") for i in range(8)]
        (scaled, xn_ready, t_done, xT_ready, gate_done, act_done, c_ready, cu_done, cu_out, y_done, y_added, y_out,
         back_done, h_added) = (sem("r_" + n) for n in (
             "scaled", "xn_ready", "t_done", "xT_ready", "gate_done", "act_done", "c_ready", "cu_done", "cu_out",
             "y_done", "y_added", "y_out", "back_done", "h_added"))
        block = ctx.enter_context(nc.Block())
        qt = lambda a: slice(a * TT, (a + 1) * TT)
        GATES = (("f_wf", "f_uf", "f_bf"), ("f_wi", "f_ui", "f_bi"), ("f_wc", "f_uc", "f_bc"))

        @block.gpsimd
        def _(pool):
            token_scale(nc, pool, sh, ps_tmp, "plain", scaled)

        @block.vector
        def _(dve):
            v = nc.vector
            v.memset(c[:, :, :], 0.0)
            dve.drain()
            for k in range(KT):
                r = v.tensor_scalar(c[:, k, :], c[:, k, :], sh.col("f_c0", k), None, ALU.add)
            r.then_inc(c_ready, 1)
            dve.wait_ge(scaled, 1)

            def norm(b):
                for t in range(NT):
                    r = v.tensor_scalar(xn[:, t, :], sh.h[:, 3 * b + t, :], sh.mv[:, 3 * b + t, 0:1],
                                        sh.rs[:, bass.ds(3 * b + t, 1)], ALU.subtract, ALU.mult)
                r.then_inc(xn_ready, 1)

            norm(0)

            def step(b, p, has_next):
                if has_next:
                    dve.wait_ge(t_done, 2 * b + 2)
                    norm(b + 1)
                dve.wait_ge(act_done, 6 * b + 6)
                f, i, g = (x[:, :, :] for x in gates)
                v.tensor_tensor(c[:, :, :], f, c[:, :, :], ALU.mult)
                v.tensor_tensor(i, i, g, ALU.mult)
                dve.drain()
                v.tensor_tensor(c[:, :, :], c[:, :, :], i, ALU.add).then_inc(c_ready, 1)
            both(dve, step)

            def add_state(b, p):
                dve.wait_ge(y_done, b + 1)
                dve.wait_ge(cu_out, 2)
                for k in range(KT):
                    r = v.tensor_tensor(y[p][:, k, :], ps[2 * p + k][:, 0:T], cu[:, k, :], ALU.add)
                r.then_inc(y_added, 1)

            def body(b, p, has_next):
                if has_next:
                    add_state(b + 1, 1 - p)
                dve.wait_ge(back_done, b + 1)
                for t in range(NT):
                    hh = sh.h[:, 3 * b + t, :]
                    v.tensor_tensor(hh, hh, ps[4 + 2 * p + t // 2][0:TT, D * (t % 2):D * (t % 2) + D], ALU.add)
                dve.drain()
                batch_stats(nc, dve, sh, b)
                dve.sem_inc(h_added, 1)
            add_state(0, 0)
            both(dve, body)

        @block.scalar
        def _(act):
            s = nc.scalar

            def turn_out(b):
                for k in range(KT):
                    act.wait_ge(t_done, 2 * b + k + 1)
                    s.activation(xT[:, b, k, :], ps[6 + k][:, 0:T], ACT.Copy).then_inc(xT_ready, 1)
            turn_out(0)

            def step(b, p, has_next):
                if has_next:
                    turn_out(b + 1)
                for g in range(3):
                    for k in range(KT):
                        act.wait_ge(gate_done, 6 * b + 2 * g + k + 1)
                        s.activation(gates[g][:, k, :], ps[2 * g + k][:, 0:T], ACT.Tanh if g == 2 else ACT.Sigmoid,
                                     bias=sh.col(GATES[g][2], k)).then_inc(act_done, 1)
            both(act, step)
            act.wait_ge(cu_done, 1)
            for k in range(KT):
                s.activation(cu[:, k, :], ps[4 + k][:, 0:T], ACT.Identity, bias=sh.col("f_bo", k)).then_inc(cu_out, 1)

            def body(b, p, has_next):
                act.wait_ge(y_added, b + 1)
                s.activation(y[p][:, :, :], y[p][:, :, :], ACT.Tanh).then_inc(y_out, 1)
            both(act, body)

        @block.tensor
        def _(pe):
            mm = nc.tensor.matmul

            def turn(b):
                pe.wait_ge(xn_ready, b + 1)
                pe.wait_ge(xT_ready, 2 * b)
                for k in range(KT):
                    for t in range(NT):
                        r = nc.tensor.transpose(ps[6 + k][:, qt(t)], xn[:, t, 128 * k:128 * k + 128],
                                                sh.ident[0:TT, 0:TT])
                    r.then_inc(t_done, 1)

            def input_part(b):
                pe.wait_ge(xT_ready, 2 * b + 2)
                for g in range(3):
                    for m in range(KT):
                        pe.wait_ge(act_done, 6 * b + (2 * g + m - 5 if not isinstance(b, int) or b > 0 else 0))
                        for k in range(KT):
                            mm(ps[2 * g + m][:, 0:T], sh.wt(GATES[g][0], k, 128 * m, 128 * m + 128), xT[:, b, k, :],
                               start=k == 0, stop=False, skip_group_check=True)

            turn(0)
            input_part(0)

            def step(b, p, has_next):
                pe.wait_ge(c_ready, b + 1)
                for g in range(3):
                    for m in range(KT):
                        for k in range(KT):
                            r = mm(ps[2 * g + m][:, 0:T], sh.wt(GATES[g][1], k, 128 * m, 128 * m + 128), c[:, k, :],
                                   start=False, stop=k == KT - 1, skip_group_check=True)
                        r.then_inc(gate_done, 1)
                    if g == 0 and has_next:
                        turn(b + 1)
                if has_next:
                    input_part(b + 1)
            both(pe, step)
            pe.wait_ge(c_ready, B + 1)
            for m in range(KT):
                for k in range(KT):
                    r = mm(ps[4 + m][:, 0:T], sh.wt("f_uo", k, 128 * m, 128 * m + 128), c[:, k, :],
                           start=k == 0, stop=k == KT - 1)
            r.then_inc(cu_done, 1)

            def output(b, p):
                pe.wait_ge(y_added, b - 1 if not isinstance(b, int) or b > 0 else 0)
                for m in range(KT):
                    for k in range(KT):
                        r = mm(ps[2 * p + m][:, 0:T], sh.wt("f_wo", k, 128 * m, 128 * m + 128), xT[:, b, k, :],
                               start=k == 0, stop=k == KT - 1)
                r.then_inc(y_done, 1)
            output(0, 0)
            pe.wait_ge(cu_out, 2)

            def body(b, p, has_next):
                if has_next:
                    output(b + 1, 1 - p)
                pe.wait_ge(y_out, b + 1)
                pe.wait_ge(h_added, b)
                for t in range(NT):
                    for k in range(KT):
                        at = D * (t % 2) + 128 * k
                        r = nc.tensor.transpose(ps[4 + 2 * p + t // 2][0:TT, at:at + 128], y[p][:, k, qt(t)],
                                                sh.ident[:, :])
                r.then_inc(back_done, 1)
            both(pe, body)


def scan_layer(nc, sh):
    with ExitStack() as ctx:
        sb = lambda name, shape, dt=F32: ctx.enter_context(nc.sbuf_tensor(name, shape, dt))
        pb = lambda name: ctx.enter_context(nc.psum_tensor(name, [128, 512], F32))
        sem = lambda name: ctx.enter_context(nc.semaphore(name))
        xn = sb("s_xn", [TT, NT, D])
        xT = [sb(f"s_xT{i}", [128, KT, T]) for i in range(2)]
        decay = sb("s_decay", [128, KT, T])
        y = sb("s_y", [128, KT, T])
        ps_tmp = sb("s_tmp", [TT, 2, NTILES])
        psA = [pb(f"s_psA{i}") for i in range(2)]
        psK = [pb(f"s_psK{i}") for i in range(2)]
        psQ = [pb(f"s_psQ{i}") for i in range(2)]
        psT = [pb(f"s_psT{i}") for i in range(2)]
        scaled, xn_ready, t_done, xT_ready, a_done, a_out, k_done, q_done, y_ready, back_done, h_added = (
            sem("s_" + n) for n in ("scaled", "xn_ready", "t_done", "xT_ready", "a_done", "a_out", "k_done",
                                    "q_done", "y_ready", "back_done", "h_added"))
        block = ctx.enter_context(nc.Block())
        qt = lambda a: slice(a * TT, (a + 1) * TT)

        @block.gpsimd
        def _(pool):
            token_scale(nc, pool, sh, ps_tmp, "rms", scaled)

        @block.vector
        def _(dve):
            v = nc.vector
            dve.wait_ge(scaled, 1)

            def norm(b):
                for t in range(NT):
                    r = v.tensor_scalar(xn[:, t, :], sh.h[:, 3 * b + t, :], sh.mv[:, 3 * b + t, 0:1],
                                        sh.rs[:, bass.ds(3 * b + t, 1)], ALU.subtract, ALU.mult)
                r.then_inc(xn_ready, 1)
            norm(0)

            def body(b, p, has_next):
                if has_next:
                    dve.wait_ge(t_done, 2 * b + 2)
                    norm(b + 1)
                for m in range(KT):
                    dve.wait_ge(a_out, 2 * b + m + 1)
                    dve.wait_ge(k_done, 2 * b + m + 1)
                    v.tensor_tensor_scan(y[:, m, :], decay[:, m, :], psK[m][:, 0:T], 0.0, ALU.mult, ALU.add)
                for m in range(KT):
                    dve.drain()
                    dve.wait_ge(q_done, 2 * b + m + 1)
                    v.tensor_tensor(y[:, m, :], y[:, m, :], psQ[m][:, 0:T], ALU.mult).then_inc(y_ready, 1)
                dve.wait_ge(back_done, b + 1)
                for t in range(NT):
                    hh = sh.h[:, 3 * b + t, :]
                    r = v.tensor_tensor(hh, hh, psT[t // 2][0:TT, D * (t % 2):D * (t % 2) + D], ALU.add)
                r.then_inc(h_added, 1)
                dve.drain()
                batch_stats(nc, dve, sh, b)
            both(dve, body)

        @block.scalar
        def _(act):
            s = nc.scalar

            def turn_out(b, p):
                for k in range(KT):
                    act.wait_ge(t_done, 2 * b + k + 1)
                    s.activation(xT[p][:, k, :], psT[k][:, 0:T], ACT.Identity, scale=sh.col("s_g", k)).then_inc(xT_ready, 1)
            turn_out(0, 0)

            def body(b, p, has_next):
                if has_next:
                    turn_out(b + 1, 1 - p)
                for m in range(KT):
                    act.wait_ge(a_done, 2 * b + m + 1)
                    act.wait_ge(y_ready, 2 * b)
                    s.activation(decay[:, m, :], psA[m][:, 0:T], ACT.Sigmoid).then_inc(a_out, 1)
            both(act, body)

        @block.tensor
        def _(pe):
            mm = nc.tensor.matmul

            def turn(b):
                pe.wait_ge(xn_ready, b + 1)
                pe.wait_ge(h_added, b - 1 if not isinstance(b, int) or b > 0 else 0)
                for k in range(KT):
                    for t in range(NT):
                        r = nc.tensor.transpose(psT[k][:, qt(t)], xn[:, t, 128 * k:128 * k + 128],
                                                sh.ident[0:TT, 0:TT])
                    r.then_inc(t_done, 1)

            def project(name, dst, p, m, done):
                for k in range(KT):
                    r = mm(dst[m][:, 0:T], sh.wt(name, k, 128 * m, 128 * m + 128), xT[p][:, k, :],
                           start=k == 0, stop=k == KT - 1)
                r.then_inc(done, 1)
            turn(0)

            def body(b, p, has_next):
                pe.wait_ge(xT_ready, 2 * b + 2)
                if has_next:
                    turn(b + 1)
                pe.wait_ge(a_out, 2 * b)
                pe.wait_ge(y_ready, 2 * b)
                for m in range(KT):
                    project("s_a", psA, p, m, a_done)
                    project("s_kv", psK, p, m, k_done)
                for m in range(KT):
                    project("s_q", psQ, p, m, q_done)
                pe.wait_ge(y_ready, 2 * b + 2)
                if has_next:
                    pe.wait_ge(xT_ready, 2 * b + 4)
                for t in range(NT):
                    for k in range(KT):
                        at = D * (t % 2) + 128 * k
                        r = nc.tensor.transpose(psT[t // 2][0:TT, at:at + 128], y[:, k, qt(t)], sh.ident[:, :])
                r.then_inc(back_done, 1)
            both(pe, body)


def quantised(nc, sh, ins):
    R = 32
    GROUP = 16
    with ExitStack() as ctx:
        sb = lambda name, shape, dt=F32: ctx.enter_context(nc.sbuf_tensor(name, shape, dt))
        pb = lambda name: ctx.enter_context(nc.psum_tensor(name, [128, 512], F32))
        sem = lambda name: ctx.enter_context(nc.semaphore(name))
        wq = sb("q_wq", [128, 6, KT, D])
        qi = sb("q_qi", [128, 6, KT, D], I32)
        sc = sb("q_sc", [128, 6, KT, D])
        la = sb("q_la", [R, 6, D])
        lb = sb("q_lb", [R, 6, D])
        g = sb("q_g", [TT, NTILES, D])
        y = sb("q_y", [TT, NTILES, D])
        xn = sb("q_xn", [TT, NT, D])
        xT = [sb(f"q_xT{i}", [128, KT, T]) for i in range(2)]
        mv = sb("q_mv", [TT, NTILES, 2])
        ps_tmp = sb("q_tmp", [TT, 2, NTILES])
        psT = [[pb(f"q_psT{p}{k}") for k in range(KT)] for p in range(2)]
        psY = [[pb(f"q_psY{p}{k}") for k in range(2)] for p in range(2)]
        scaled, w_in, lora_done, w_ready, x_ready, t_done, xT_ready, y_done, y_out, stats_ready, y_scaled, g_ready = (
            sem("q_" + n) for n in ("scaled", "w_in", "lora_done", "w_ready", "x_ready", "t_done", "xT_ready",
                                    "y_done", "y_out", "stats_ready", "y_scaled", "g_ready"))
        block = ctx.enter_context(nc.Block())
        qt = lambda a: slice(a * TT, (a + 1) * TT)
        PASSES = 6

        @block.sync
        def _(sync):
            sync.dma_start(qi[:, :, :, :], ins["qw"]).then_inc(w_in, 16)
            for r in range(128 // GROUP):
                sync.dma_start(sc[GROUP * r:GROUP * r + GROUP, :, :, :], ins["qs"][r].partition_broadcast(GROUP)).then_inc(w_in, 16)
            sync.dma_start(la[:, :, :], ins["qla"]).then_inc(w_in, 16)
            sync.dma_start(lb[:, :, :], ins["qlb"]).then_inc(w_in, 16)

        @block.gpsimd
        def _(pool):
            token_scale(nc, pool, sh, ps_tmp, "plain", scaled)
            gp = nc.gpsimd
            for j in range(3):
                pool.wait_ge(g_ready, j + 1)

                def stage(b, p, has_next, j=j):
                    pool.wait_ge(t_done, B * 2 * j + b)
                    for t in range(NT):
                        r = gp.tensor_copy(xn[:, t, :], g[:, 3 * b + t, :])
                    r.then_inc(x_ready, 1)
                both(pool, stage)
                pool.wait_ge(stats_ready, j + 1)
                gp.tensor_tensor(ps_tmp[:, 0, :], mv[:, :, 1], sh.eps[0:TT, :], ALU.add)
                pool.drain()
                gp.tensor_tensor(sh.rs[:, :], ps_tmp[:, 0, :], sh.mhalf[0:TT, :], ALU.pow).then_inc(y_scaled, 1)
                pool.drain()

        @block.vector
        def _(dve):
            v = nc.vector
            dve.wait_ge(w_in, 16 * 11)
            v.tensor_scalar(wq[:, :, :, :], qi[:, :, :, :], 1.0 / 7.5, 1.0, ALU.mult, ALU.subtract)
            dve.drain()
            v.tensor_tensor(wq[:, :, :, :], wq[:, :, :, :], sc[:, :, :, :], ALU.mult)
            for i in range(6):
                dve.drain()
                dve.wait_ge(lora_done, i + 1)
                v.tensor_tensor(wq[:, i, :, :], wq[:, i, :, :],
                                psT[i % 2][0][:, :].rearrange("p (k o) -> p k o", k=KT), ALU.add).then_inc(w_ready, 1)
            dve.wait_ge(scaled, 1)
            with dve.Fori(0, NTILES) as t:
                v.tensor_scalar(g[:, t, :], sh.h[:, t, :], sh.mv[:, t, 0:1],
                                sh.rs[:, bass.ds(t, 1)], ALU.subtract, ALU.mult)
            dve.drain()
            dve.sem_inc(g_ready, 1)
            for n in range(PASSES):
                first = n % 2 == 0
                j = n // 2
                if not first:
                    dve.wait_ge(y_scaled, j + 1)

                    def norm(b):
                        for t in range(NT):
                            r = v.tensor_scalar(xn[:, t, :], y[:, 3 * b + t, :], mv[:, 3 * b + t, 0:1],
                                                sh.rs[:, bass.ds(3 * b + t, 1)], ALU.subtract, ALU.mult)
                        r.then_inc(x_ready, 1)
                    norm(0)

                def body(b, p, has_next, n=n, first=first):
                    if has_next and not first:
                        dve.wait_ge(t_done, B * n + b + 1)
                        norm(b + 1)
                    dve.wait_ge(y_done, B * n + b + 1)
                    for t in range(NT):
                        src = psY[p][t // 2][0:TT, D * (t % 2):D * (t % 2) + D]
                        r = v.tensor_tensor(y[:, 3 * b + t, :], src, sh.row(f"q_{n}"), ALU.add)
                    r.then_inc(y_out, 1)
                    dve.drain()
                    if first:
                        batch_stats(nc, dve, sh, b, y, mv)
                    else:
                        bt = bass.ds(NT * b, NT)
                        v.tensor_tensor(g[:, bt, :], g[:, bt, :], y[:, bt, :], ALU.add)
                        if n == PASSES - 1:
                            dve.drain()
                            v.tensor_tensor(sh.h[:, bt, :], sh.h[:, bt, :], g[:, bt, :], ALU.add)
                            dve.drain()
                            batch_stats(nc, dve, sh, b)
                both(dve, body)
                dve.drain()
                if first:
                    dve.sem_inc(stats_ready, 1)
                elif n < PASSES - 1:
                    dve.sem_inc(g_ready, 1)

        @block.scalar
        def _(act):
            s = nc.scalar
            for n in range(PASSES):
                def turn_out(b, p, n=n):
                    act.wait_ge(t_done, B * n + b + 1)
                    for k in range(KT):
                        src = psT[p][k][:, 0:T]
                        if n % 2 == 0:
                            r = s.activation(xT[p][:, k, :], src, ACT.Copy)
                        else:
                            r = s.activation(xT[p][:, k, :], src, ACT.Gelu, bias=sh.col(f"q_b{n // 2}", k),
                                             scale=sh.col(f"q_g{n // 2}", k))
                    r.then_inc(xT_ready, 1)
                both(act, lambda b, p, has_next: turn_out(b, p))

        @block.tensor
        def _(pe):
            mm = nc.tensor.matmul
            pe.wait_ge(w_in, 16 * 11)
            for i in range(6):
                if i >= 2:
                    pe.wait_ge(w_ready, i - 1)
                for k in range(KT):
                    r = mm(psT[i % 2][0][:, D * k:D * k + D], la[:, i, 128 * k:128 * k + 128], lb[:, i, :],
                           start=True, stop=True)
                r.then_inc(lora_done, 1)
            pe.wait_ge(w_ready, 6)
            for n in range(PASSES):

                def turn(b, p, n=n):
                    pe.wait_ge(x_ready, B * n + b + 1)
                    pe.wait_ge(xT_ready, B * n + b - 1 if n > 0 or not isinstance(b, int) or b > 0 else 0)
                    for k in range(KT):
                        for t in range(NT):
                            r = nc.tensor.transpose(psT[p][k][:, qt(t)], xn[:, t, 128 * k:128 * k + 128],
                                                    sh.ident[0:TT, 0:TT])
                    r.then_inc(t_done, 1)
                turn(0, 0)

                def body(b, p, has_next, n=n):
                    if has_next:
                        turn(b + 1, 1 - p)
                    pe.wait_ge(xT_ready, B * n + b + 1)
                    pe.wait_ge(y_out, B * n + b - 1 if n > 0 else (b if not isinstance(b, int) else max(b - 1, 0)))
                    for t in range(NT):
                        for k in range(KT):
                            r = mm(psY[p][t // 2][0:TT, D * (t % 2):D * (t % 2) + D], xT[p][:, k, qt(t)],
                                   wq[:, n, k, :], start=k == 0, stop=k == KT - 1, skip_group_check=True)
                    r.then_inc(y_done, 1)
                both(pe, body)


def masked_attention(nc, sh, ins, experts):
    NP = 9
    LOWEST = -3.4028234663852886e38
    with ExitStack() as ctx:
        sb = lambda name, shape, dt=F32: ctx.enter_context(nc.sbuf_tensor(name, shape, dt))
        pb = lambda name: ctx.enter_context(nc.psum_tensor(name, [128, 512], F32))
        sem = lambda name: ctx.enter_context(nc.semaphore(name))
        xn = sb("m_xn", [TT, NT, D])
        xT = sb("m_xT", [128, KT, T])
        qT = [sb(f"m_qT{i}", [128, KT, T]) for i in range(2)]
        kT = [sb(f"m_kT{i}", [128, KT, T]) for i in range(2)]
        vS = [sb(f"m_vS{i}", [TT, NT, D]) for i in range(2)]
        mask = sb("m_mask", [TT, 5 * TT])
        Sm = [sb(f"m_S{i}", [TT, T]) for i in range(2)]
        P = [sb(f"m_P{i}", [TT, T]) for i in range(2)]
        PT = [sb(f"m_PT{i}", [TT, NT, TT]) for i in range(2)]
        mx, nm, su, rec = (sb("m_" + n, [TT, 2]) for n in ("mx", "nm", "su", "rec"))
        bq = sb("m_bq", [128, KT])
        ps_tmp = sb("m_tmp", [TT, 2, NTILES])
        psM = [pb(f"m_psM{i}") for i in range(2)]
        psV = pb("m_psV")
        psS = [pb(f"m_psS{i}") for i in range(2)]
        psP = [pb(f"m_psP{i}") for i in range(2)]
        psO = pb("m_psO")
        (scaled, consts, xn_ready, piece_done, piece_out, v_done, v_out, s_done, max_done, exp_done, t_done, pt_done,
         pv_done, h_added, row_begun) = (sem("m_" + n) for n in (
             "scaled", "consts", "xn_ready", "piece_done", "piece_out", "v_done", "v_out", "s_done", "max_done",
             "exp_done", "t_done", "pt_done", "pv_done", "h_added", "row_begun"))
        block = ctx.enter_context(nc.Block())
        qt = lambda a: slice(a * TT, (a + 1) * TT)

        @block.sync
        def _(sync):
            experts.load(sync, ins["moe1"], range(3, E))

        @block.gpsimd
        def _(pool):
            token_scale(nc, pool, sh, ps_tmp, "plain", scaled)
            nc.gpsimd.memset(mask[:, :], 0.0)
            pool.drain()
            nc.gpsimd.affine_select(out=mask[:, :], in_=mask[:, :], compare_op=ALU.not_equal, fill=LOWEST,
                                    base=2 * TT, pattern=[[-1, 5 * TT]], channel_multiplier=1).then_inc(consts, 1)

        @block.vector
        def _(dve):
            v = nc.vector
            v.tensor_scalar(bq[:, :], sh.cols[:, CIDX["m_bq"], :], 1.0 / D, None, ALU.mult).then_inc(consts, 1)
            dve.wait_ge(consts, 2)
            dve.wait_ge(scaled, 1)

            def norm(b):
                for t in range(NT):
                    r = v.tensor_scalar(xn[:, t, :], sh.h[:, 3 * b + t, :], sh.mv[:, 3 * b + t, 0:1],
                                        sh.rs[:, bass.ds(3 * b + t, 1)], ALU.subtract, ALU.mult)
                r.then_inc(xn_ready, 1)

            def value_out(b, p, t):
                dve.wait_ge(v_done, NT * b + t + 1)
                v.tensor_tensor(vS[p][:, t, :], psV[0:TT, 0:D], sh.row("m_bv"), ALU.add).then_inc(v_out, 1)

            norm(0)
            for t in range(NT):
                value_out(0, 0, t)

            def body(b, p, has_next):
                def row_max(u):
                    i = (p + u) % 2
                    dve.wait_ge(s_done, NT * b + u + 1)
                    dve.wait_ge(exp_done, NT * b + (u - 1 if u >= 1 else 0))
                    dve.sem_inc(row_begun, 1)
                    at = (2 - u) * TT
                    v.tensor_tensor_reduce(Sm[i][:, :], psS[i][0:TT, 0:T], mask[:, at:at + T], 1.0, LOWEST,
                                           ALU.add, ALU.max, mx[:, i:i + 1])
                    dve.drain()
                    v.tensor_scalar(nm[:, i:i + 1], mx[:, i:i + 1], -1.0, None, ALU.mult).then_inc(max_done, 1)

                def turned(u):
                    i = (p + u) % 2
                    dve.wait_ge(t_done, NT * b + u + 1)
                    dve.wait_ge(pv_done, NT * b + (u - 1 if u >= 1 else 0))
                    v.tensor_copy(PT[i][:, :, :], psP[i][0:TT, 0:T].rearrange("k (a q) -> k a q", a=NT)).then_inc(pt_done, 1)

                def combine(u):
                    i = (p + u) % 2
                    v.reciprocal(rec[:, i:i + 1], su[:, i:i + 1])
                    dve.drain()
                    dve.wait_ge(pv_done, NT * b + u + 1)
                    hh = sh.h[:, 3 * b + u, :]
                    v.scalar_tensor_tensor(hh, psO[0:TT, 0:D], rec[:, i:i + 1], hh, ALU.mult, ALU.add).then_inc(h_added, 1)

                row_max(0)
                if has_next:
                    dve.wait_ge(piece_done, 6 * b + 2)
                    norm(b + 1)
                row_max(1)
                turned(0)
                row_max(2)
                turned(1)
                combine(0)
                turned(2)
                combine(1)
                if has_next:
                    value_out(b + 1, 1 - p, 0)
                combine(2)
                if has_next:
                    value_out(b + 1, 1 - p, 1)
                    value_out(b + 1, 1 - p, 2)
                dve.drain()
                batch_stats(nc, dve, sh, b)
            both(dve, body)

        @block.scalar
        def _(act):
            s = nc.scalar
            act.wait_ge(consts, 2)

            def piece(b, p, k):
                act.wait_ge(piece_done, 6 * b + k + 1)
                src = psM[k % 2][:, 0:T]
                j = k % 2
                if k < 2:
                    r = s.activation(xT[:, j, :], src, ACT.Copy)
                elif k < 4:
                    r = s.activation(qT[p][:, j, :], src, ACT.Identity, bias=bq[:, j:j + 1], scale=1.0 / D)
                else:
                    r = s.activation(kT[p][:, j, :], src, ACT.Identity, bias=sh.col("m_bk", j))
                r.then_inc(piece_out, 1)
            for k in range(6):
                piece(0, 0, k)

            def body(b, p, has_next):
                def exp(u):
                    i = (p + u) % 2
                    act.wait_ge(max_done, NT * b + u + 1)
                    act.wait_ge(t_done, NT * b + (u - 1 if u >= 1 else 0))
                    act.wait_ge(h_added, NT * b + (u - 1 if u >= 1 else 0))
                    s.activation(P[i][:, :], Sm[i][:, :], ACT.Exp, bias=nm[:, i:i + 1],
                                 accum_out=su[:, i:i + 1]).then_inc(exp_done, 1)

                def next_piece(k):
                    if has_next:
                        piece(b + 1, 1 - p, k)
                exp(0)
                next_piece(0)
                next_piece(1)
                exp(1)
                next_piece(2)
                exp(2)
                next_piece(3)
                next_piece(4)
                next_piece(5)
            both(act, body)

        @block.tensor
        def _(pe):
            mm = nc.tensor.matmul

            def piece(b, p, k):
                if k == 0:
                    pe.wait_ge(xn_ready, b + 1)
                if k in (0, 1):
                    pe.wait_ge(piece_out, 6 * b)
                else:
                    pe.wait_ge(piece_out, 6 * b + max(2, k - 1))
                j = k % 2
                if k < 2:
                    for t in range(NT):
                        r = nc.tensor.transpose(psM[j][:, qt(t)], xn[:, t, 128 * j:128 * j + 128],
                                                sh.ident[0:TT, 0:TT])
                else:
                    for c in range(KT):
                        r = mm(psM[j][:, 0:T], sh.wt("m_q" if k < 4 else "m_k", c, 128 * j, 128 * j + 128),
                               xT[:, c, :], start=c == 0, stop=c == KT - 1)
                r.then_inc(piece_done, 1)

            def value(b, t):
                pe.wait_ge(v_out, NT * b + t)
                for c in range(KT):
                    r = mm(psV[0:TT, 0:D], xT[:, c, qt(t)], sh.wt("m_v", c, 0, D), start=c == 0, stop=c == KT - 1)
                r.then_inc(v_done, 1)

            for k in range(6):
                piece(0, 0, k)
            for t in range(NT):
                value(0, t)

            def body(b, p, has_next):
                def scores(u):
                    i = (p + u) % 2
                    pe.wait_ge(max_done, NT * b + (u - 1 if u >= 1 else 0))
                    for c in range(KT):
                        r = mm(psS[i][0:TT, 0:T], qT[p][:, c, qt(u)], kT[p][:, c, :], start=c == 0, stop=c == KT - 1)
                    r.then_inc(s_done, 1)

                def turn(u):
                    i = (p + u) % 2
                    pe.wait_ge(exp_done, NT * b + u + 1)
                    pe.wait_ge(pt_done, NT * b + (u - 1 if u >= 1 else 0))
                    for a in range(NT):
                        r = nc.tensor.transpose(psP[i][0:TT, qt(a)], P[i][:, qt(a)], sh.ident[0:TT, 0:TT])
                    r.then_inc(t_done, 1)

                def product(u):
                    i = (p + u) % 2
                    pe.wait_ge(pt_done, NT * b + u + 1)
                    pe.wait_ge(h_added, NT * b + u)
                    for a in range(NT):
                        r = mm(psO[0:TT, 0:D], PT[i][:, a, :], vS[p][:, a, :], start=a == 0, stop=a == NT - 1)
                    r.then_inc(pv_done, 1)

                def next_piece(k):
                    if has_next:
                        piece(b + 1, 1 - p, k)

                def next_value(t):
                    if has_next:
                        value(b + 1, t)
                pe.wait_ge(piece_out, 6 * b + 6)
                pe.wait_ge(v_out, NT * b + NT)
                scores(0)
                scores(1)
                next_piece(0)
                next_piece(1)
                turn(0)
                scores(2)
                next_piece(2)
                turn(1)
                product(0)
                next_piece(3)
                next_piece(4)
                turn(2)
                product(1)
                next_piece(5)
                next_value(0)
                product(2)
                next_value(1)
                next_value(2)
            both(pe, body)


class Experts:
    SIZE = KT * 1024 + 8 * D

    def __init__(self, nc, ctx):
        end = 212863 // 32 * 32
        self.at = end - 4 * E * self.SIZE
        self.w = nc.alloc_sbuf_tensor_at("expert_w", [128, E, self.SIZE], F32, offset=self.at)
        self.loaded = ctx.enter_context(nc.semaphore("experts_loaded"))

    def load(self, eng, src, which):
        for e in which:
            eng.dma_start(self.w[:, e, :], src[e]).then_inc(self.loaded, 16)


def router(nc, sh, ins, pre, wname, bname, capacity, o):
    NX = NTILES * E
    with ExitStack() as ctx:
        sb = lambda name, shape, dt=F32: ctx.enter_context(nc.sbuf_tensor(pre + name, shape, dt))
        pb = lambda name: ctx.enter_context(nc.psum_tensor(pre + name, [128, 512], F32))
        sem = lambda name: ctx.enter_context(nc.semaphore(pre + name))
        xn = [sb(f"xn{i}", [TT, NT, D]) for i in range(2)]
        xT = [sb(f"xT{i}", [128, KT, T]) for i in range(2)]
        wr = sb("wr", [128, KT, E])
        br = sb("br", [TT, E])
        L = sb("L", [TT, NTILES, E])
        oh = sb("oh", [TT, NTILES, E])
        w = sb("w", [TT, NTILES, E])
        m = sb("m", [TT, NTILES])
        idx = sb("idx", [TT, NTILES])
        em8 = sb("em8", [TT, E])
        tri = sb("tri", [TT, TT])
        ones = sb("ones", [TT, TT])
        cnt = sb("cnt", [TT, E, NTILES])
        inc = sb("inc", [TT, E, NTILES])
        again = sb("again", [TT, E, NTILES])
        one8 = sb("one8", [TT, E])
        tot = sb("tot", [TT, E])
        toti = sb("toti", [TT, E], I32)
        base = sb("base", [TT, E])
        tok = sb("tok", [TT, NTILES])
        sl = sb("sl", [TT, NTILES])
        ps_tmp = sb("tmp", [TT, 2, NTILES])
        NS = o["tiles"] if not capacity else 1
        tno = sb("tno", [TT, NS])
        te = sb("te", [TT, NS, E])
        ts1 = sb("ts1", [TT, NS])
        psT = [[pb(f"psT{p}{k}") for k in range(KT)] for p in range(2)]
        psL = [pb(f"psL{p}") for p in range(2)]
        psR, psC = pb("psR"), pb("psC")
        scaled, wr_in, consts, xn_ready, copied, t_done, xT_ready, l_done, l_out, oh_ready, counted, m_ready, p_ready = (
            sem(n) for n in ("scaled", "wr_in", "consts", "xn_ready", "copied", "t_done", "xT_ready", "l_done", "l_out",
                             "oh_ready", "counted", "m_ready", "p_ready"))
        block = ctx.enter_context(nc.Block())
        qt = lambda a: slice(a * TT, (a + 1) * TT)
        bc = lambda x: x.unsqueeze(2).to_broadcast([TT, NTILES, E])

        @block.sync
        def _(sync):
            sync.dma_start(wr[:, :, :], ins[wname]).then_inc(wr_in, 16)
            sync.dma_start(br[:, :], ins[bname].partition_broadcast(TT)).then_inc(wr_in, 16)

        @block.gpsimd
        def _(pool):
            g = nc.gpsimd
            token_scale(nc, pool, sh, ps_tmp, "plain", scaled)
            g.iota(em8[:, :], pattern=[[1, E]], base=-E, channel_multiplier=0, allow_small_or_imprecise_dtypes=True)
            g.iota(tok[:, :], pattern=[[TT, NTILES]], base=0, channel_multiplier=1,
                   allow_small_or_imprecise_dtypes=True)
            g.iota(tno[:, :], pattern=[[1, NS]], base=0, channel_multiplier=0, allow_small_or_imprecise_dtypes=True)
            g.memset(ones[:, :], 1.0)
            g.memset(one8[:, :], 1.0)
            g.memset(again[:, :, :], 1.0)
            pool.drain()
            g.memset(again[:, :, 0:1], 0.0)
            g.affine_select(out=tri[:, :], in_=ones[:, :], compare_op=ALU.is_gt, fill=0.0, base=0,
                            pattern=[[1, TT]], channel_multiplier=-1).then_inc(consts, 1)

            def body(b, p, has_next):
                pool.wait_ge(xn_ready, b + 1)
                for t in range(NT):
                    r = g.tensor_copy(o["xall"][:, 3 * b + t, :], xn[p][:, t, :])
                r.then_inc(copied, 1)
            both(pool, body)

        @block.vector
        def _(dve):
            v = nc.vector
            dve.wait_ge(scaled, 1)

            def norm(b, p):
                ago = b - 1 if not isinstance(b, int) or b > 0 else 0
                dve.wait_ge(copied, ago)
                dve.wait_ge(t_done, ago)
                for t in range(NT):
                    r = v.tensor_scalar(xn[p][:, t, :], sh.h[:, 3 * b + t, :], sh.mv[:, 3 * b + t, 0:1],
                                        sh.rs[:, bass.ds(3 * b + t, 1)], ALU.subtract, ALU.mult)
                r.then_inc(xn_ready, 1)
            norm(0, 0)
            dve.wait_ge(wr_in, 32)

            def body(b, p, has_next):
                if has_next:
                    norm(b + 1, 1 - p)
                dve.wait_ge(l_done, b + 1)
                v.tensor_tensor(L[:, bass.ds(3 * b, 3), :], psL[p][0:TT, 0:3 * E].rearrange("q (t e) -> q t e", e=E),
                                br[:, :].unsqueeze(1).to_broadcast([TT, NT, E]), ALU.add).then_inc(l_out, 1)
            both(dve, body)
            dve.drain()
            dve.wait_ge(consts, 1)
            if not capacity:
                v.tensor_scalar(L[:, :, :], L[:, :, :], 16.635532, None, ALU.min)
                dve.drain()
            v.tensor_reduce(m[:, :], L[:, :, :], AX.X, ALU.max).then_inc(m_ready, 1)
            dve.drain()
            v.tensor_tensor(w[:, :, :], L[:, :, :], bc(m[:, :]), ALU.is_ge)
            dve.drain()
            ebc = em8[:, :].unsqueeze(1).to_broadcast([TT, NTILES, E])
            v.tensor_tensor(w[:, :, :], w[:, :, :], ebc, ALU.mult)
            dve.drain()
            v.tensor_reduce(idx[:, :], w[:, :, :], AX.X, ALU.min)
            dve.drain()
            v.tensor_tensor(oh[:, :, :], ebc, bc(idx[:, :]), ALU.is_equal).then_inc(oh_ready, 1)
            dve.wait_ge(counted, 1)
            v.tensor_copy(cnt[:, :, :], psC[0:TT, 0:NX].rearrange("q (t e) -> q e t", e=E))
            dve.drain()
            v.tensor_tensor_scan(inc[:, :, :].rearrange("q e t -> q (e t)"), again[:, :, :].rearrange("q e t -> q (e t)"),
                                 cnt[:, :, :].rearrange("q e t -> q (e t)"), 0.0, ALU.mult, ALU.add)
            dve.drain()
            v.tensor_copy(tot[:, :], inc[:, :, NTILES - 1])
            v.tensor_tensor(cnt[:, :, :], inc[:, :, :], cnt[:, :, :], ALU.subtract)
            dve.drain()
            v.tensor_tensor(w[:, :, :], psR[0:TT, 0:NX].rearrange("q (t e) -> q t e", e=E),
                            cnt[:, :, :].rearrange("q e t -> q t e"), ALU.add)
            if not capacity:
                v.tensor_scalar(tot[:, :], tot[:, :], 127.0, None, ALU.add)
                dve.drain()
                v.tensor_copy(toti[:, :], tot[:, :])
                dve.drain()
                v.tensor_scalar(toti[:, :], toti[:, :], 7, None, ALU.arith_shift_right)
                dve.drain()
                v.tensor_copy(tot[:, :], toti[:, :])
                dve.drain()
                v.tensor_tensor_scan(base[:, :], one8[:, :], tot[:, :], 0.0, ALU.mult, ALU.add)
                dve.drain()
                v.tensor_tensor(te[:, :, :], base[:, :].unsqueeze(1).to_broadcast([TT, NS, E]),
                                tno[:, :].unsqueeze(2).to_broadcast([TT, NS, E]), ALU.is_le)
                dve.drain()
                v.tensor_reduce(ts1[:, :], te[:, :, :], AX.X, ALU.add)
                dve.drain()
                v.tensor_scalar(ts1[:, :], ts1[:, :], float(E - 1), None, ALU.min)
                v.tensor_tensor(base[:, :], base[:, :], tot[:, :], ALU.subtract)
                dve.drain()
                v.tensor_copy(o["tile_expert"][:, :], ts1[:, :])
                v.tensor_scalar(base[:, :], base[:, :], 128.0, None, ALU.mult)
                dve.drain()
                v.tensor_tensor(w[:, :, :], w[:, :, :], base[:, :].unsqueeze(1).to_broadcast([TT, NTILES, E]), ALU.add)
                dve.drain()
                v.tensor_tensor(w[:, :, :], w[:, :, :], oh[:, :, :], ALU.mult)
                dve.drain()
                v.tensor_reduce(sl[:, :], w[:, :, :], AX.X, ALU.add)
                dve.drain()
                v.tensor_copy(o["slot"][:, :], sl[:, :])
                dve.wait_ge(p_ready, 1)
                v.tensor_scalar(o["prob"][:, :], o["prob"][:, :], 1.0, None, ALU.add)
                dve.drain()
                v.reciprocal(o["prob"][:, :], o["prob"][:, :])
            else:
                dve.drain()
                v.tensor_tensor(w[:, :, :], w[:, :, :], oh[:, :, :], ALU.mult)
                dve.drain()
                v.tensor_reduce(sl[:, :], w[:, :, :], AX.X, ALU.add)
                v.tensor_scalar(idx[:, :], idx[:, :], float(E), float(capacity), ALU.add, ALU.mult)
                dve.drain()
                v.tensor_scalar(o["keep"][:, :], sl[:, :], float(capacity), None, ALU.is_lt)
                v.tensor_scalar(o["drop"][:, :], sl[:, :], float(capacity), None, ALU.is_ge)
                v.tensor_scalar(m[:, :], sl[:, :], float(capacity - 1), None, ALU.min)
                dve.drain()
                v.tensor_tensor(m[:, :], m[:, :], idx[:, :], ALU.add)
                v.tensor_tensor(sl[:, :], sl[:, :], idx[:, :], ALU.add)
                v.tensor_scalar(tok[:, :], tok[:, :], float(E * capacity), None, ALU.add)
                dve.drain()
                v.tensor_copy(o["back"][:, :], m[:, :])
                v.tensor_tensor(sl[:, :], sl[:, :], o["keep"][:, :], ALU.mult)
                v.tensor_tensor(tok[:, :], tok[:, :], o["drop"][:, :], ALU.mult)
                dve.drain()
                v.tensor_tensor(sl[:, :], sl[:, :], tok[:, :], ALU.add)
                dve.drain()
                v.tensor_copy(o["slot"][:, :], sl[:, :])

        @block.scalar
        def _(act):
            s = nc.scalar

            def body(b, p, has_next):
                act.wait_ge(t_done, b + 1)
                for k in range(KT):
                    r = s.activation(xT[p][:, k, :], psT[p][k][:, 0:T], ACT.Copy)
                r.then_inc(xT_ready, 1)
            both(act, body)
            if not capacity:
                act.wait_ge(m_ready, 1)
                s.activation(o["prob"][:, :], m[:, :], ACT.Exp, scale=-1.0).then_inc(p_ready, 1)

        @block.tensor
        def _(pe):
            mm = nc.tensor.matmul

            def turn(b, p):
                pe.wait_ge(xn_ready, b + 1)
                pe.wait_ge(xT_ready, b - 1 if not isinstance(b, int) or b > 0 else 0)
                for k in range(KT):
                    for t in range(NT):
                        r = nc.tensor.transpose(psT[p][k][:, qt(t)], xn[p][:, t, 128 * k:128 * k + 128],
                                                sh.ident[0:TT, 0:TT])
                r.then_inc(t_done, 1)
            turn(0, 0)
            pe.wait_ge(wr_in, 32)

            def body(b, p, has_next):
                if has_next:
                    turn(b + 1, 1 - p)
                pe.wait_ge(xT_ready, b + 1)
                pe.wait_ge(l_out, b)
                for t in range(NT):
                    for k in range(KT):
                        r = mm(psL[p][0:TT, E * t:E * t + E], xT[p][:, k, qt(t)], wr[:, k, :],
                               start=k == 0, stop=k == KT - 1, skip_group_check=True)
                r.then_inc(l_done, 1)
            both(pe, body)
            pe.wait_ge(oh_ready, 1)
            ohf = oh[:, :, :].rearrange("q t e -> q (t e)")
            mm(psC[0:TT, 0:NX], ones[:, :], ohf, start=True, stop=True)
            mm(psR[0:TT, 0:NX], tri[:, :], ohf, start=True, stop=True).then_inc(counted, 1)


MOE_TILES = (B * T + E * 127) // 128


def top1_experts(nc, sh, ins, experts, xs, ys):
    FF = 1024
    with ExitStack() as ctx:
        o = {"tiles": MOE_TILES}
        o["slot"] = ctx.enter_context(nc.sbuf_tensor("t_slot", [TT, NTILES], U32))
        o["prob"] = ctx.enter_context(nc.sbuf_tensor("t_prob", [TT, NTILES], F32))
        o["tile_expert"] = ctx.enter_context(nc.sbuf_tensor("t_te", [TT, MOE_TILES], I32))
        sem = lambda name: ctx.enter_context(nc.semaphore("t_" + name))
        with ExitStack() as c1:
            o["xall"] = c1.enter_context(nc.sbuf_tensor("t_xall", [TT, NTILES, D], F32))
            router(nc, sh, ins, "tr_", "t_wr", "t_br", 0, o)
            scatter_tokens(nc, o, xs, "ts_", lambda sync: experts.load(sync, ins["moe1"], range(0, 3)))

        with ExitStack() as c2:
            sb = lambda name, shape, dt=F32: c2.enter_context(nc.sbuf_tensor("t_" + name, shape, dt))
            pb = lambda name: c2.enter_context(nc.psum_tensor("t_" + name, [128, 512], F32))
            xb = [sb(f"xb{i}", [128, D]) for i in range(2)]
            xT = [sb(f"xT{i}", [128, KT, 128]) for i in range(2)]
            hg = [sb(f"hg{i}", [128, FF]) for i in range(2)]
            hT = sb("hT", [128, 8, 128])
            yb = [sb(f"yb{i}", [128, D]) for i in range(2)]
            psT = pb("psT")
            psH = [[pb(f"psH{p}{i}") for i in range(2)] for p in range(2)]
            psG = [pb(f"psG{i}") for i in range(2)]
            psY = pb("psY")
            x_in = [sem(f"x_in{i}") for i in range(2)]
            y_sent = [sem(f"y_sent{i}") for i in range(2)]
            x_turned, xT_ready, h_done, g_ready, g_turned, gT_ready, y_done, y_out = (sem(n) for n in (
                "x_turned", "xT_ready", "h_done", "g_ready", "g_turned", "gT_ready", "y_done", "y_out"))
            NS = MOE_TILES
            block = c2.enter_context(nc.Block())

            def pairs(eng, body):
                with eng.Fori(0, NS // 2 - 1) as i:
                    body(2 * i, 0, i, True, True)
                    body(2 * i + 1, 1, i, True, True)
                body(NS - 2, 0, NS // 2 - 1, True, False)
                body(NS - 1, 1, NS // 2 - 1, False, False)

            @block.sync
            def _(sync):
                def load(s, p):
                    sync.dma_start(xb[p][:, :], xs[bass.ds(s * 128, 128), :]).then_inc(x_in[p], 16)
                load(0, 0)
                load(1, 1)

                def body(s, p, i, nx, nx2):
                    if nx2:
                        sync.wait_ge(x_turned, s + 1)
                        load(s + 2, p)
                pairs(sync, body)

            @block.scalar
            def _(act):
                sc = nc.scalar

                def body(s, p, i, nx, nx2):
                    for q in range(2):
                        act.wait_ge(h_done, 2 * s + q + 1)
                        act.wait_ge(g_turned, s)
                        sc.activation(hg[p][:, 512 * q:512 * q + 512], psH[p][q][:, :], ACT.Gelu).then_inc(g_ready, 1)
                    act.wait_ge(y_done, s + 1)
                    act.wait_ge(y_sent[p], 16 * i)
                    sc.activation(yb[p][:, :], psY[:, 0:D], ACT.Copy).then_inc(y_out, 1)
                    act.wait_ge(y_out, s + 1)
                    act.dma_start(ys[bass.ds(s * 128, 128), :], yb[p][:, :]).then_inc(y_sent[p], 16)
                pairs(act, body)
                for p in range(2):
                    act.wait_ge(y_sent[p], 16 * (NS // 2))

            @block.vector
            def _(dve):
                v = nc.vector

                def turn_out(s, p):
                    dve.wait_ge(x_turned, s + 1)
                    v.tensor_copy(xT[p][:, :, :], psT[:, 0:2 * 128].rearrange("p (k q) -> p k q", k=KT)).then_inc(xT_ready, 1)
                turn_out(0, 0)
                turn_out(1, 1)

                def body(s, p, i, nx, nx2):
                    for q in range(2):
                        dve.wait_ge(g_turned, s + 1) if q == 0 else None
                        dve.wait_ge(y_done, s)
                        v.tensor_copy(hT[:, 4 * q:4 * q + 4, :],
                                      psG[q][:, :].rearrange("p (c q) -> p c q", c=4)).then_inc(gT_ready, 1)
                    if nx2:
                        turn_out(s + 2, p)
                pairs(dve, body)

            @block.tensor
            def _(pe):
                mm = nc.tensor.matmul

                def expert(s):
                    return nc.tensor.value_load(o["tile_expert"][0:1, bass.ds(s, 1)], min_val=0, max_val=E - 1)

                def turn(s, p, i):
                    pe.wait_ge(x_in[p], 16 * (i + 1))
                    pe.wait_ge(xT_ready, s)
                    for k in range(KT):
                        r = nc.tensor.transpose(psT[:, 128 * k:128 * k + 128], xb[p][:, 128 * k:128 * k + 128], sh.ident[:, :])
                    r.then_inc(x_turned, 1)

                def first(s, p):
                    e = expert(s)
                    pe.wait_ge(xT_ready, s + 1)
                    for q in range(2):
                        pe.wait_ge(g_ready, 2 * s - 2 if not isinstance(s, int) or s > 0 else 0)
                        for k in range(KT):
                            r = mm(psH[p][q][:, :], xT[p][:, k, :],
                                   experts.w[:, e, 1024 * k + 512 * q:1024 * k + 512 * q + 512],
                                   start=k == 0, stop=k == KT - 1)
                        r.then_inc(h_done, 1)
                turn(0, 0, 0)
                turn(1, 1, 0)
                pe.wait_ge(experts.loaded, 16 * E)
                first(0, 0)

                def body(s, p, i, nx, nx2):
                    if nx:
                        first(s + 1, 1 - p)
                    pe.wait_ge(g_ready, 2 * s + 2)
                    pe.wait_ge(gT_ready, 2 * s)
                    for c in range(8):
                        r = nc.tensor.transpose(psG[c // 4][:, 128 * (c % 4):128 * (c % 4) + 128],
                                                hg[p][:, 128 * c:128 * c + 128], sh.ident[:, :])
                    r.then_inc(g_turned, 1)
                    e = expert(s)
                    if nx2:
                        turn(s + 2, p, i + 1)
                    pe.wait_ge(y_out, s)
                    for c in range(8):
                        if c % 4 == 0:
                            pe.wait_ge(gT_ready, 2 * s + c // 4 + 1)
                        at = KT * FF + D * c
                        r = mm(psY[:, 0:D], hT[:, c, :], experts.w[:, e, at:at + D], start=c == 0, stop=c == 7)
                    r.then_inc(y_done, 1)
                pairs(pe, body)

        combine_experts(nc, sh, ctx, o, ys, "tc_", None)


def scatter_tokens(nc, o, xs, pre, meanwhile):
    with nc.semaphore(pre + "scattered") as scattered, nc.Block() as block:
        @block.gpsimd
        def _(pool):
            for t in range(NTILES):
                nc.gpsimd.indirect_dma_start(out=xs[:, :], out_offset=bass.IndirectOffsetOnAxis(o["slot"][:, t:t + 1], 0),
                                             in_=o["xall"][:, t, :], in_offset=None).then_inc(scattered, 16)

        @block.sync
        def _(sync):
            meanwhile(sync)
            sync.wait_ge(scattered, 16 * NTILES)


def combine_experts(nc, sh, ctx, o, ys, pre, out):
    with ExitStack() as c2:
        y = c2.enter_context(nc.sbuf_tensor(pre + "y", [TT, NTILES, D], F32))
        st = c2.enter_context(nc.sbuf_tensor(pre + "st", [TT, 6], F32))
        fetched = [c2.enter_context(nc.semaphore(f"{pre}fetched{b}")) for b in range(B)]
        added = c2.enter_context(nc.semaphore(pre + "added"))
        sent = c2.enter_context(nc.semaphore(pre + "sent"))
        block = c2.enter_context(nc.Block())
        rows = o["slot"] if out is None else o["back"]

        @block.gpsimd
        def _(pool):
            for t in range(NTILES):
                nc.gpsimd.indirect_dma_start(out=y[:, t, :], out_offset=None, in_=ys[:, :],
                                             in_offset=bass.IndirectOffsetOnAxis(rows[:, t:t + 1], 0)).then_inc(fetched[t // NT], 16)

        @block.vector
        def _(dve):
            v = nc.vector
            for b in range(B):
                dve.wait_ge(fetched[b], 16 * NT)
                for t in range(NT * b, NT * b + NT):
                    hh = sh.h[:, t, :]
                    if out is None:
                        r = v.scalar_tensor_tensor(hh, y[:, t, :], o["prob"][:, t:t + 1], hh, ALU.mult, ALU.add)
                    else:
                        v.tensor_scalar(y[:, t, :], y[:, t, :], o["keep"][:, t:t + 1], None, ALU.mult)
                        dve.drain()
                        v.scalar_tensor_tensor(y[:, t, :], o["xall"][:, t, :], o["drop"][:, t:t + 1], y[:, t, :],
                                               ALU.mult, ALU.add)
                        dve.drain()
                        r = v.tensor_tensor(hh, hh, y[:, t, :], ALU.add)
                if out is None:
                    dve.drain()
                    batch_stats(nc, dve, sh, b)
                else:
                    r.then_inc(added, 1)

        @block.sync
        def _(sync):
            if out is not None:
                for b in range(B):
                    sync.wait_ge(added, b + 1)
                    sync.dma_start(out[b].rearrange("(t p) c -> p t c", p=TT),
                                   sh.h[:, NT * b:NT * b + NT, :]).then_inc(sent, 16)
                sync.wait_ge(sent, 16 * B)


H3, KVH, DH3 = 16, 4, 64
HEAD_ORDER = [(2 * (c // 4) + half) * (H3 // KVH) + c % 4 for c in range(8) for half in range(2)]


def alibi_attention(nc, sh, ins, stream):
    NU = H3 * NT
    NP = 15
    BIG = 3.4028234663852886e38
    PI = 3.141592653589793
    with ExitStack() as ctx:
        sb = lambda name, shape, dt=F32: ctx.enter_context(nc.sbuf_tensor("l_" + name, shape, dt))
        pb = lambda name: ctx.enter_context(nc.psum_tensor("l_" + name, [128, 512], F32))
        sem = lambda name: ctx.enter_context(nc.semaphore("l_" + name))
        wq_in = sb("wq_in", [128, H3, DH3 // 2, 2])
        wq = sb("wq", [128, H3, DH3 // 2, 2])
        wtmp = sb("wtmp", [128, H3, DH3 // 2])
        wk = sb("wk", [128, D])
        wv = sb("wv", [128, D])
        wo = sb("wo", [128, 8, D])
        ang = sb("ang", [128, 2, H3])
        turns = sb("turns", [128, 2, H3])
        cs = sb("cs", [128, 2, H3])
        slope = sb("slope", [TT, H3])
        rel = sb("rel", [TT, T])
        future = sb("future", [TT, T])
        am = sb("am", [TT, H3, T])
        xn = sb("xn", [TT, NT, D])
        xT = sb("xT", [128, KT, T])
        qT = [sb(f"qT{i}", [128, 8, T]) for i in range(2)]
        kz = [sb(f"kz{i}", [128, KVH, T]) for i in range(2)]
        vS = [sb(f"vS{i}", [TT, NT, D]) for i in range(2)]
        Sm = [sb(f"S{i}", [TT, T]) for i in range(3)]
        P = [sb(f"P{i}", [TT, T]) for i in range(6)]
        PT = [sb(f"PT{i}", [TT, NT, T]) for i in range(2)]
        oT = [sb(f"oT{i}", [128, T]) for i in range(2)]
        nm = sb("nm", [TT, 6])
        su = sb("su", [TT, 6])
        ri = sb("ri", [TT, 6])
        ps_tmp = sb("tmp", [TT, 2, NTILES])
        psS = [pb(f"psS{i}") for i in range(2)]
        psP = [pb(f"psP{i}") for i in range(2)]
        psO, psM = pb("psO"), pb("psM")
        psW = [pb(f"psW{i}") for i in range(2)]
        (w_in, scaled, rel_ready, consts, ang_ready, sin_ready, slope_ready, xn_ready, piece_done, piece_out, s_done,
         min_done, exp_done, rec_done, p_ready, t_done, pt_done, pv_done, o_out, w_done, h_added, row_begun,
         head_begun) = (sem(n) for n in (
             "w_in", "scaled", "rel_ready", "consts", "ang_ready", "sin_ready", "slope_ready", "xn_ready", "piece_done",
             "piece_out", "s_done", "min_done", "exp_done", "rec_done", "p_ready", "t_done", "pt_done", "pv_done",
             "o_out", "w_done", "h_added", "row_begun", "head_begun"))
        block = ctx.enter_context(nc.Block())
        qt = lambda a: slice(a * TT, (a + 1) * TT)

        @block.sync
        def _(sync):
            for half in range(2):
                sync.dma_start(ang[:, half, :], ins["l_ang"].partition_broadcast(128)).then_inc(w_in, 16)
            sync.dma_start(slope[:, :], ins["l_slope"].partition_broadcast(TT)).then_inc(w_in, 16)
            sync.dma_start(wq_in[:, :, :, :], ins["l_wq"].rearrange("p (h d r) -> p h d r", h=H3, r=2)).then_inc(w_in, 16)
            sync.dma_start(wk[:, :], ins["l_wk"]).then_inc(w_in, 16)
            sync.dma_start(wv[:, :], ins["l_wv"]).then_inc(w_in, 16)
            sync.dma_start(wo[:, :, :], ins["l_wo"]).then_inc(w_in, 16)
            stream.prefetch(sync)

        @block.gpsimd
        def _(pool):
            g = nc.gpsimd
            token_scale(nc, pool, sh, ps_tmp, "plain", scaled)
            g.iota(rel[:, :], pattern=[[-1, T]], base=2 * TT, channel_multiplier=1, allow_small_or_imprecise_dtypes=True)
            g.memset(future[:, :], 0.0)
            for i in range(2):
                g.memset(kz[i][:, :, :], 0.0)
            pool.drain()
            g.affine_select(out=future[:, :], in_=future[:, :], compare_op=ALU.is_ge, fill=BIG, base=2 * TT,
                            pattern=[[-1, T]], channel_multiplier=1).then_inc(rel_ready, 1)

            def body(b, p, has_next):
                for u in range(NU):
                    n = TT * (u % 3 + 1)
                    if u % 3 == 0:
                        pool.wait_ge(rec_done, H3 * b + u // 3 + 1)
                        pool.sem_inc(head_begun, 1)
                    g.tensor_scalar(P[u % 6][:, 0:n], P[u % 6][:, 0:n], ri[:, u % 6:u % 6 + 1], None,
                                    ALU.mult).then_inc(p_ready, 1)
            both(pool, body)

        @block.vector
        def _(dve):
            v = nc.vector
            dve.wait_ge(w_in, 16 * 7)
            v.tensor_scalar(ang[:, 1, :], ang[:, 1, :], PI / 2, None, ALU.add)
            dve.drain()
            v.tensor_scalar(turns[:, :, :], ang[:, :, :], 1.0 / (2 * PI), None, ALU.mult)
            dve.drain()
            v.tensor_scalar(turns[:, :, :], turns[:, :, :], 12582912.0, None, ALU.add)
            dve.drain()
            v.tensor_scalar(turns[:, :, :], turns[:, :, :], 12582912.0, None, ALU.subtract)
            dve.drain()
            v.scalar_tensor_tensor(ang[:, :, :], turns[:, :, :], -6.28125, ang[:, :, :], ALU.mult, ALU.add)
            dve.drain()
            v.scalar_tensor_tensor(ang[:, :, :], turns[:, :, :], -(2 * PI - 6.28125), ang[:, :, :], ALU.mult, ALU.add)
            dve.drain()
            v.tensor_scalar(ang[:, :, :], ang[:, :, :], 3.1415925, -3.1415925, ALU.min, ALU.max).then_inc(ang_ready, 1)
            dve.wait_ge(sin_ready, 1)
            v.tensor_scalar(cs[:, :, :], cs[:, :, :], -(DH3 ** -0.5), None, ALU.mult)
            dve.drain()
            sn = cs[:, 0, :].unsqueeze(2).to_broadcast([128, H3, DH3 // 2])
            cn = cs[:, 1, :].unsqueeze(2).to_broadcast([128, H3, DH3 // 2])
            v.tensor_tensor(wq[:, :, :, 0], wq_in[:, :, :, 0], cn, ALU.mult)
            v.tensor_tensor(wtmp[:, :, :], wq_in[:, :, :, 1], sn, ALU.mult)
            dve.drain()
            v.tensor_tensor(wq[:, :, :, 0], wq[:, :, :, 0], wtmp[:, :, :], ALU.subtract)
            v.tensor_tensor(wq[:, :, :, 1], wq_in[:, :, :, 0], sn, ALU.mult)
            dve.drain()
            v.tensor_tensor(wtmp[:, :, :], wq_in[:, :, :, 1], cn, ALU.mult)
            dve.drain()
            v.tensor_tensor(wq[:, :, :, 1], wq[:, :, :, 1], wtmp[:, :, :], ALU.add).then_inc(consts, 1)
            dve.wait_ge(rel_ready, 1)
            dve.wait_ge(slope_ready, 1)
            v.tensor_scalar(slope[:, :], slope[:, :], -1.0, None, ALU.mult)
            dve.drain()
            for h in range(H3):
                v.scalar_tensor_tensor(am[:, h, :], rel[:, :], slope[:, h:h + 1], future[:, :], ALU.mult, ALU.add)
            dve.wait_ge(scaled, 1)

            def norm(b):
                for t in range(NT):
                    r = v.tensor_scalar(xn[:, t, :], sh.h[:, 3 * b + t, :], sh.mv[:, 3 * b + t, 0:1],
                                        sh.rs[:, bass.ds(3 * b + t, 1)], ALU.subtract, ALU.mult)
                r.then_inc(xn_ready, 1)

            def piece(b, p, k):
                if k >= 12:
                    dve.wait_ge(piece_done, NP * b + k + 1)
                    v.tensor_copy(vS[p][:, k - 12, :], psM[0:TT, 0:D]).then_inc(piece_out, 1)

            def row(b, u):
                n = TT * (u % 3 + 1)
                dve.wait_ge(s_done, NU * b + u + 1)
                dve.wait_ge(exp_done, NU * b + (u - 2 if u >= 3 else 0))
                dve.sem_inc(row_begun, 1)
                v.tensor_tensor_reduce(Sm[u % 3][:, 0:n], psS[u % 2][0:TT, 0:n], am[:, u // 3, T - n:T], 1.0, BIG,
                                       ALU.add, ALU.min, nm[:, u % 6:u % 6 + 1]).then_inc(min_done, 1)

            def reciprocals(b, h):
                dve.wait_ge(exp_done, NU * b + 3 * h + 3)
                a = 3 * (h % 2)
                v.tensor_scalar(ri[:, a:a + 3], su[:, a:a + 3], 1.0, None, ALU.add)
                dve.drain()
                v.reciprocal(ri[:, a:a + 3], ri[:, a:a + 3]).then_inc(rec_done, 1)

            def turned(b, u):
                h, t = u // 3, u % 3
                dve.wait_ge(t_done, NU * b + u + 1)
                if t == 0:
                    dve.wait_ge(pv_done, H3 * b + (h - 1 if h >= 2 else 0))
                v.tensor_copy(PT[h % 2][:, 0:t + 1, qt(t)],
                              psP[u % 2][0:TT, 0:TT * (t + 1)].rearrange("k (a q) -> k a q", a=t + 1)).then_inc(pt_done, 1)

            norm(0)
            for k in range(NP):
                piece(0, 0, k)

            def body(b, p, has_next):
                for u in range(NU):
                    row(b, u)
                    if u >= 5:
                        turned(b, u - 5)
                    if u % 3 == 1 and u >= 4:
                        reciprocals(b, u // 3 - 1)
                    if u == 2 and has_next:
                        dve.wait_ge(piece_done, NP * b + NP)
                        norm(b + 1)
                    if u % 3 == 1 and has_next and u >= 7:
                        piece(b + 1, 1 - p, (u - 7) // 3)
                reciprocals(b, H3 - 1)
                for u in range(NU - 5, NU):
                    turned(b, u)
                if has_next:
                    piece(b + 1, 1 - p, NP - 1)
                dve.wait_ge(w_done, b + 1)
                for t in range(NT):
                    hh = sh.h[:, 3 * b + t, :]
                    r = v.tensor_tensor(hh, hh, psW[t // 2][0:TT, D * (t % 2):D * (t % 2) + D], ALU.add)
                r.then_inc(h_added, 1)
                dve.drain()
                batch_stats(nc, dve, sh, b)
            both(dve, body)

        @block.scalar
        def _(act):
            s = nc.scalar
            act.wait_ge(ang_ready, 1)
            s.activation(cs[:, :, :], ang[:, :, :], ACT.Sin).then_inc(sin_ready, 1)
            s.activation(slope[:, :], slope[:, :], ACT.Exp).then_inc(slope_ready, 1)
            act.wait_ge(rel_ready, 1)

            def piece(b, p, k):
                if k >= 12:
                    return
                act.wait_ge(piece_done, NP * b + k + 1)
                if k < 2:
                    r = s.activation(xT[:, k, :], psM[:, 0:T], ACT.Copy)
                elif k < 10:
                    r = s.activation(qT[p][:, k - 2, :], psM[:, 0:T], ACT.Copy)
                else:
                    for half in range(2):
                        ph = slice(64 * half, 64 * half + 64)
                        r = s.activation(kz[p][ph, 2 * (k - 10) + half, :], psM[ph, 0:T], ACT.Copy)
                r.then_inc(piece_out, 1)

            def exp(b, u):
                n = TT * (u % 3 + 1)
                act.wait_ge(min_done, NU * b + u + 1)
                act.wait_ge(t_done, NU * b + (u - 5 if u >= 6 else 0))
                s.activation(P[u % 6][:, 0:n], Sm[u % 3][:, 0:n], ACT.Exp, bias=nm[:, u % 6:u % 6 + 1], scale=-1.0,
                             accum_out=su[:, u % 6:u % 6 + 1]).then_inc(exp_done, 1)

            def out(b, c):
                act.wait_ge(pv_done, H3 * b + 2 * c + 2)
                act.wait_ge(w_done, b)
                s.activation(oT[c % 2][:, :], psO[:, 0:T], ACT.Copy).then_inc(o_out, 1)

            for k in range(NP):
                piece(0, 0, k)

            def body(b, p, has_next):
                for u in range(NU):
                    exp(b, u)
                    if u % 3 == 1 and has_next and u >= 7:
                        piece(b + 1, 1 - p, (u - 7) // 3)
                    if u % 6 == 0 and u >= 12:
                        out(b, u // 6 - 2)
                out(b, 6)
                out(b, 7)
            both(act, body)

        @block.tensor
        def _(pe):
            mm = nc.tensor.matmul
            pe.wait_ge(consts, 1)

            def piece(b, p, k):
                if k == 0:
                    pe.wait_ge(xn_ready, b + 1)
                pe.wait_ge(piece_out, NP * b + k)
                if k < 2:
                    for t in range(NT):
                        r = nc.tensor.transpose(psM[:, qt(t)], xn[:, t, 128 * k:128 * k + 128], sh.ident[0:TT, 0:TT])
                elif k < 10:
                    r = mm(psM[:, 0:T], wq[:, 2 * (k - 2):2 * (k - 2) + 2, :, :].rearrange("p h d r -> p (h d r)"),
                           xT[:, 1, :], start=True, stop=True)
                elif k < 12:
                    r = mm(psM[:, 0:T], wk[:, 128 * (k - 10):128 * (k - 10) + 128], xT[:, 1, :], start=True, stop=True)
                else:
                    r = mm(psM[0:TT, 0:D], xT[:, 0, qt(k - 12)], wv[:, :], start=True, stop=True)
                r.then_inc(piece_done, 1)

            def scores(b, p, u):
                h, t = u // 3, u % 3
                n = TT * (t + 1)
                pe.wait_ge(min_done, NU * b + (u - 1 if u >= 2 else 0))
                c = h // 2
                mm(psS[u % 2][0:TT, 0:n], qT[p][:, c, qt(t)], kz[p][:, 2 * (c // 4) + h % 2, 0:n],
                   start=True, stop=True).then_inc(s_done, 1)

            def turn(b, u):
                pe.wait_ge(p_ready, NU * b + u + 1)
                pe.wait_ge(pt_done, NU * b + (u - 1 if u >= 2 else 0))
                for a in range(u % 3 + 1):
                    r = nc.tensor.transpose(psP[u % 2][0:TT, qt(a)], P[u % 6][:, qt(a)], sh.ident[0:TT, 0:TT])
                r.then_inc(t_done, 1)

            def values(b, p, h):
                pe.wait_ge(pt_done, NU * b + 3 * h + 3)
                if h % 2 == 0:
                    pe.wait_ge(o_out, 8 * b + h // 2)
                c = h // 2
                kv = 2 * (c // 4) + h % 2
                ph = slice(64 * (h % 2), 64 * (h % 2) + 64)
                for a in range(NT):
                    r = mm(psO[ph, TT * a:T], vS[p][:, a, DH3 * kv:DH3 * kv + DH3], PT[h % 2][:, a, TT * a:T],
                           start=a == 0, stop=a == NT - 1, skip_group_check=True)
                r.then_inc(pv_done, 1)

            def project(b, c):
                pe.wait_ge(o_out, 8 * b + c + 1)
                if c == 0:
                    pe.wait_ge(h_added, b)
                for t in range(NT):
                    r = mm(psW[t // 2][0:TT, D * (t % 2):D * (t % 2) + D], oT[c % 2][:, qt(t)], wo[:, c, :],
                           start=c == 0 and t != 1, stop=c == 7, skip_group_check=True)
                if c == 7:
                    r.then_inc(w_done, 1)

            for k in range(NP):
                piece(0, 0, k)

            def body(b, p, has_next):
                pe.wait_ge(piece_out, NP * b + NP)
                for u in range(5):
                    scores(b, p, u)
                for u in range(NU):
                    if u + 5 < NU:
                        scores(b, p, u + 5)
                    turn(b, u)
                    if u % 3 == 1 and u >= 4:
                        values(b, p, u // 3 - 1)
                    if u % 3 == 2 and has_next and u // 3 < NP:
                        piece(b + 1, 1 - p, u // 3)
                    if u % 6 == 1 and u >= 13:
                        project(b, u // 6 - 2)
                values(b, p, H3 - 1)
                project(b, 6)
                project(b, 7)
            both(pe, body)


CAP = B * T // E
GELU_IN = 1.4142135623730951 / 1.41421
GELU_OUT = 1.41421 / 1.4142135623730951


class Stream:

    def __init__(self, nc, ctx, src):
        self.src = src
        self.w = [ctx.enter_context(nc.sbuf_tensor(f"c_w{i}", [128, Experts.SIZE], F32)) for i in range(2)]
        self.w_in = [ctx.enter_context(nc.semaphore(f"c_w_in{i}")) for i in range(2)]

    def load(self, eng, e, p):
        eng.dma_start(self.w[p][:, :], self.src[e]).then_inc(self.w_in[p], 16)

    def prefetch(self, eng):
        self.load(eng, 0, 0)
        self.load(eng, 1, 1)


def capacity_experts(nc, sh, ins, stream, xs, ys, out):
    assert CAP == T
    with ExitStack() as ctx:
        o = {}
        o["xall"] = ctx.enter_context(nc.sbuf_tensor("c_xall", [TT, NTILES, D], F32))
        for n, dt in (("slot", U32), ("back", U32), ("keep", F32), ("drop", F32)):
            o[n] = ctx.enter_context(nc.sbuf_tensor("c_" + n, [TT, NTILES], dt))
        router(nc, sh, ins, "cr_", "c_wr", "c_br", CAP, o)
        scatter_tokens(nc, o, xs, "cs_", lambda sync: None)

        with ExitStack() as c2:
            sb = lambda name, shape, dt=F32: c2.enter_context(nc.sbuf_tensor("c_" + name, shape, dt))
            pb = lambda name: c2.enter_context(nc.psum_tensor("c_" + name, [128, 512], F32))
            sem = lambda name: c2.enter_context(nc.semaphore("c_" + name))
            NF = 8
            xb = [sb(f"xb{i}", [TT, NT, D]) for i in range(2)]
            xT = [sb(f"xT{i}", [128, KT, T]) for i in range(2)]
            hT = [sb(f"hT{i}", [128, NF, T]) for i in range(2)]
            yb = [sb(f"yb{i}", [TT, NT, D]) for i in range(2)]
            b1 = sb("b1", [128, E, NF])
            b2 = sb("b2", [TT, E, D])
            psT = [pb(f"psT{i}") for i in range(2)]
            psH = [pb(f"psH{i}") for i in range(4)]
            psY = [pb(f"psY{i}") for i in range(2)]
            b_in = sem("b_in")
            x_in = [sem(f"x_in{i}") for i in range(2)]
            y_sent = [sem(f"y_sent{i}") for i in range(2)]
            b1_ready, x_turned, xT_ready, h_done, g_ready, y_done, y_out = (sem(n) for n in (
                "b1_ready", "x_turned", "xT_ready", "h_done", "g_ready", "y_done", "y_out"))
            block = c2.enter_context(nc.Block())
            qt = lambda a: slice(a * TT, (a + 1) * TT)

            @block.sync
            def _(sync):
                def load(e, p):
                    sync.dma_start(xb[p][:, :, :], xs[bass.ds(e * CAP, CAP), :].rearrange("(t p) c -> p t c", p=TT)).then_inc(x_in[p], 16)

                def store(e, p):
                    sync.wait_ge(y_out, NT * e + NT)
                    sync.dma_start(ys[bass.ds(e * CAP, CAP), :].rearrange("(t p) c -> p t c", p=TT), yb[p][:, :, :]).then_inc(y_sent[p], 16)
                load(0, 0)
                load(1, 1)
                with sync.Fori(0, E // 2 - 1) as i:
                    for p in range(2):
                        sync.wait_ge(x_turned, 2 * i + p + 1)
                        load(2 * i + p + 2, p)
                        sync.wait_ge(y_done, NT * (2 * i + p + 1))
                        sync.dma_start(stream.w[p][:, :], ins["moe2"][bass.ds(2 * i + p + 2, 1), :, :].rearrange("e p n -> (e p) n")).then_inc(stream.w_in[p], 16)
                        store(2 * i + p, p)
                store(E - 2, 0)
                store(E - 1, 1)
                for p in range(2):
                    sync.wait_ge(y_sent[p], 16 * (E // 2))

            @block.gpsimd
            def _(pool):
                pool.dma_start(b1[:, :, :], ins["c_b1"]).then_inc(b_in, 16)
                pool.dma_start(b2[:, :, :], ins["c_b2"].partition_broadcast(TT)).then_inc(b_in, 16)

            def experts2(eng, body):
                with eng.Fori(0, E // 2 - 1) as i:
                    body(2 * i, 0, i, True)
                    body(2 * i + 1, 1, i, True)
                body(E - 2, 0, E // 2 - 1, True)
                body(E - 1, 1, E // 2 - 1, False)

            @block.vector
            def _(dve):
                v = nc.vector
                dve.wait_ge(b_in, 32)
                v.tensor_scalar(b1[:, :, :], b1[:, :, :], GELU_IN, None, ALU.mult).then_inc(b1_ready, 1)

                def turn_out(e, p):
                    for k in range(KT):
                        dve.wait_ge(x_turned, e + 1) if k == 0 else None
                        r = v.tensor_copy(xT[p][:, k, :], psT[k][:, 0:T])
                    r.then_inc(xT_ready, 1)
                turn_out(0, 0)

                def body(e, p, i, has_next):
                    if has_next:
                        turn_out(e + 1, 1 - p)
                    dve.wait_ge(y_sent[p], 16 * i)
                    for t in range(NT):
                        dve.wait_ge(y_done, NT * e + t + 1)
                        v.scalar_tensor_tensor(yb[p][:, t, :], psY[t % 2][0:TT, 0:D], GELU_OUT, b2[:, e, :],
                                               ALU.mult, ALU.add).then_inc(y_out, 1)
                experts2(dve, body)

            @block.scalar
            def _(act):
                s = nc.scalar
                act.wait_ge(b1_ready, 1)

                def body(e, p, i, has_next):
                    for f in range(NF):
                        act.wait_ge(h_done, NF * e + f + 1)
                        s.activation(hT[p][:, f, :], psH[f % 4][:, 0:T], ACT.Gelu, bias=b1[:, e, f:f + 1],
                                     scale=GELU_IN).then_inc(g_ready, 1)
                experts2(act, body)

            @block.tensor
            def _(pe):
                mm = nc.tensor.matmul

                def turn(e, p, i):
                    pe.wait_ge(x_in[p], 16 * (i + 1))
                    pe.wait_ge(xT_ready, e)
                    for k in range(KT):
                        for t in range(NT):
                            r = nc.tensor.transpose(psT[k][:, qt(t)], xb[p][:, t, 128 * k:128 * k + 128],
                                                    sh.ident[0:TT, 0:TT])
                    r.then_inc(x_turned, 1)

                def first(e, p, i):
                    pe.wait_ge(stream.w_in[p], 16 * (i + 1))
                    pe.wait_ge(xT_ready, e + 1)
                    for f in range(NF):
                        pe.wait_ge(g_ready, NF * e + (f - 3 if f >= 4 else (f - 3 if not isinstance(e, int) or e > 0 else 0)))
                        for k in range(KT):
                            r = mm(psH[f % 4][:, 0:T], stream.w[p][:, 1024 * k + 128 * f:1024 * k + 128 * f + 128],
                                   xT[p][:, k, :], start=k == 0, stop=k == KT - 1)
                        r.then_inc(h_done, 1)
                turn(0, 0, 0)
                first(0, 0, 0)

                def body(e, p, i, has_next):
                    if has_next:
                        turn(e + 1, 1 - p, i + p)
                        first(e + 1, 1 - p, i + p)
                    pe.wait_ge(g_ready, NF * e + NF)
                    for t in range(NT):
                        pe.wait_ge(y_out, NT * e + (t - 1 if t >= 2 else 0))
                        for f in range(NF):
                            at = KT * 1024 + D * f
                            r = mm(psY[t % 2][0:TT, 0:D], hT[p][:, f, qt(t)], stream.w[p][:, at:at + D],
                                   start=f == 0, stop=f == NF - 1)
                        r.then_inc(y_done, 1)
                experts2(pe, body)

        combine_experts(nc, sh, ctx, o, ys, "cc_", out)


def clear_semaphores(nc):
    used = sorted(nc.released_uncleared_semaphores)
    runs = []
    for n in used:
        if runs and runs[-1][1] == n:
            runs[-1][1] = n + 1
        else:
            runs.append([n, n + 1])
    with nc.Block() as block:
        @block.sync
        def _(sync):
            for a, b in runs:
                sync.sem_clear(range(a, b))


def program(nc, ins, out):
    dram = lambda name, rows: nc.dram_tensor(name, [rows, D], F32, kind="Internal").ap()
    with ExitStack() as ctx:
        h0 = nc.dram_tensor("h0_scratch", [B, T, D], F32, kind="Internal").ap()
        xs, ys = dram("xs_scratch", 128 * MOE_TILES), dram("ys_scratch", 128 * MOE_TILES)
        xs2, ys2 = dram("xs2_scratch", E * CAP + B * T), dram("ys2_scratch", E * CAP)
        sh = Shared(nc, ctx, ins)
        experts = Experts(nc, ctx)
        with ExitStack() as early:
            sh.early(early)
            tokenise(nc, sh, ins, h0)
            attention16(nc, sh, [xs, xs2[0:E * CAP, :]])
            recurrence(nc, sh)
            scan_layer(nc, sh)
            quantised(nc, sh, ins)
            masked_attention(nc, sh, ins, experts)
        clear_semaphores(nc)
        top1_experts(nc, sh, ins, experts, xs, ys)
        stream = Stream(nc, ctx, ins["moe2"])
        alibi_attention(nc, sh, ins, stream)
        capacity_experts(nc, sh, ins, stream, xs2, ys2, out)


def layout(inp):
    import numpy as np
    a = {k: np.asarray(v) for k, v in inp.items()}
    o = {}
    o["x"] = a["x"].reshape(B * IMG, IMG)
    o["txt"] = a["txt"]
    for lv, name, n in ((0, "L0_tok_Wd3", 8 * 128), (1, "L0_tok_Wd2", 4 * 64), (2, "L0_tok_Wd1", 2 * 32)):
        o[f"wd{lv}"] = a[name].reshape(3, 16, n, 3).transpose(1, 3, 0, 2).reshape(16, 3, 3 * n)
    o["wa"] = np.tile(a["L0_tok_Wa"].reshape(16, 64), (8, 1))
    o["gb"] = np.concatenate([a["L0_tok_ba"], a["L0_tok_bd1"], a["L0_tok_bd2"], a["L0_tok_bd3"]])
    w = {"a_q": a["L0_attn_Wq"], "a_k": a["L0_attn_Wk"], "a_v": a["L0_attn_Wv"]}
    for n in ("wf", "uf", "wi", "ui", "wc", "uc", "wo", "uo"):
        w["f_" + n] = a["L0_ffn_" + n].T
    w["s_q"], w["s_kv"], w["s_a"] = (a["L1_attn_w_qkva"][i * D:(i + 1) * D].T for i in range(3))
    w["m_q"], w["m_k"], w["m_v"] = (a["L2_attn_" + n].T for n in ("Wq", "Wk", "Wv"))
    o["w"] = np.stack([w[n].reshape(KT, 128, D).transpose(1, 0, 2) for n in WNAMES], 1)
    c = {"a_g": a["L0_attn_ln_g"], "a_b": a["L0_attn_ln_b"], "a_bq": a["L0_attn_bq"], "a_bk": a["L0_attn_bk"],
         "f_bf": a["L0_ffn_bf"], "f_bi": a["L0_ffn_bi"], "f_bc": a["L0_ffn_bc"], "f_bo": a["L0_ffn_bo"],
         "f_c0": a["L0_ffn_in_c"], "s_g": a["L1_attn_gamma"], "m_bq": a["L2_attn_bq"], "m_bk": a["L2_attn_bk"]}
    for i in range(3):
        c[f"q_g{i}"], c[f"q_b{i}"] = a["L1_ffn_ln_gamma"][i], a["L1_ffn_ln_beta"][i]
    o["cols"] = np.stack([c[n].reshape(KT, 128).T for n in CNAMES], 1)
    r = {"a_bv": a["L0_attn_bv"], "m_bv": a["L2_attn_bv"]}
    for i in range(6):
        r[f"q_{i}"] = a["L1_ffn_biases"][i]
    o["rows"] = np.stack([r[n] for n in RNAMES])
    moe = lambda w1, w2: np.concatenate([
        w1.reshape(E, KT, 128, 1024).transpose(0, 2, 1, 3).reshape(E, 128, -1),
        w2.reshape(E, 8, 128, D).transpose(0, 2, 1, 3).reshape(E, 128, -1)], 2)
    o["moe1"] = moe(a["L2_ffn_W1"], a["L2_ffn_W2"])
    o["t_wr"], o["t_br"] = a["L2_ffn_Wr"].reshape(KT, 128, E).transpose(1, 0, 2), a["L2_ffn_br"]
    o["moe2"] = moe(a["L3_ffn_W1"], a["L3_ffn_W2"])
    o["c_wr"], o["c_br"] = a["L3_ffn_W_sw"].reshape(KT, 128, E).transpose(1, 0, 2), a["L3_ffn_b_sw"]
    o["c_b1"] = a["L3_ffn_b1"].reshape(E, 8, 128).transpose(2, 0, 1)
    o["c_b2"] = a["L3_ffn_b2"]
    order = np.array(HEAD_ORDER)
    o["l_wq"] = a["L3_attn_Wq"].reshape(128, H3, DH3)[:, order].reshape(128, H3 * DH3)
    o["l_wk"], o["l_wv"] = a["L3_attn_Wk"], a["L3_attn_Wv"]
    o["l_wo"] = a["L3_attn_Wo"].reshape(H3, DH3, D)[order].reshape(8, 128, D).transpose(1, 0, 2)
    o["l_ang"], o["l_slope"] = a["L3_attn_q_phase_angle"][order], a["L3_attn_alibi_log_slopes"][order]
    o["qw"] = a["L1_ffn_qweights"].transpose(2, 0, 1).reshape(KT, 128, 6, D).transpose(1, 2, 0, 3)
    o["qs"] = a["L1_ffn_scales"].transpose(2, 0, 1).reshape(KT, 8, 6, D).transpose(1, 2, 0, 3)
    o["qla"] = a["L1_ffn_lora_a"].transpose(1, 0, 2)
    o["qlb"] = a["L1_ffn_lora_b"].transpose(2, 0, 1)
    return {k: np.ascontiguousarray(v) for k, v in o.items()}


def kernel(**inputs):
    import concourse.bacc as _bacc
    from concourse import mybir as _mybir
    from concourse.bass_utils import run_bass_kernel_spmd as _run

    nc = _bacc.Bacc("TRN2", target_bir_lowering=False, num_devices=1)
    arrays, args = {}, {}
    for name, a in layout(inputs).items():
        arrays[f"in_{name}_dram"] = a
        args[name] = nc.dram_tensor(f"in_{name}_dram", a.shape, _mybir.dt.from_np(a.dtype), kind="ExternalInput").ap()
    out = nc.dram_tensor("out_0_dram", (B, T, D), F32, kind="ExternalOutput").ap()
    program(nc, args, out)
    r = _run(nc, [arrays], core_ids=[0])
    return r.results[0]["out_0_dram"]
```

```python
from contextlib import ExitStack

import concourse.bass as bass
from concourse import mybir

F32 = mybir.dt.float32
F32R = mybir.dt.float32r
BF16 = mybir.dt.bfloat16
I32 = mybir.dt.int32
U32 = mybir.dt.uint32
ALU = mybir.AluOpType
ACT = mybir.ActivationFunctionType
AX = mybir.AxisListType

B = 8
T = 333
TT = 111
NT = 3
NTILES = B * NT
D = 256
KT = 2
IMG = 256
TXT = 77
EPS = 1e-5
E = 8

WNAMES = ["a_q", "a_k", "a_v", "f_wf", "f_uf", "f_wi", "f_ui", "f_wc", "f_uc", "f_wo", "f_uo",
          "s_q", "s_kv", "s_a", "m_q", "m_k", "m_v"]
WIDX = {n: i for i, n in enumerate(WNAMES)}
CNAMES = ["a_g", "a_b", "a_bq", "a_bk", "f_bf", "f_bi", "f_bc", "f_bo", "f_c0", "s_g", "q_g0", "q_g1",
          "q_g2", "q_b0", "q_b1", "q_b2", "m_bq", "m_bk"]
CIDX = {n: i for i, n in enumerate(CNAMES)}
RNAMES = ["a_bv", "m_bv", "q_0", "q_1", "q_2", "q_3", "q_4", "q_5"]
RIDX = {n: i for i, n in enumerate(RNAMES)}


class Shared:

    def __init__(self, nc, ctx, ins):
        sb = lambda name, shape, dt=F32: ctx.enter_context(nc.sbuf_tensor(name, shape, dt))
        self.nc, self.ins = nc, ins
        self.h = sb("h", [TT, NTILES, D])
        self.mv = sb("mv", [TT, NTILES, 2])
        self.rs = sb("rs", [TT, NTILES])
        self.moments = sb("moments", [TT, NT, 6])
        self.batch_mv = sb("batch_mv", [TT, NT, 2])
        self.ident = sb("ident", [128, 128])
        self.eps = sb("eps", [128, NTILES])
        self.mhalf = sb("mhalf", [128, NTILES])

    def early(self, ctx):
        sb = lambda name, shape: ctx.enter_context(self.nc.sbuf_tensor(name, shape, F32))
        self.cols = sb("cols", [128, len(CNAMES), KT])
        self.rows = sb("rows", [TT, len(RNAMES), D])
        self.w = sb("w", [128, len(WNAMES), KT, D])
        self.weights_in = ctx.enter_context(self.nc.semaphore("weights_in"))

    def col(self, name, k):
        return self.cols[:, CIDX[name], k:k + 1]

    def row(self, name):
        return self.rows[:, RIDX[name], :]

    def wt(self, name, k, a, b):
        return self.w[:, WIDX[name], k, a:b]


def both(eng, body, first=0):
    with eng.Fori(0, B // 2 - 1) as i:
        body(2 * i, 0, True)
        body(2 * i + 1, 1, True)
    body(B - 2, 0, True)
    body(B - 1, 1, False)


def batch_stats(nc, vector, sh, b, src=None, dst=None):
    v = nc.vector
    src = sh.h if src is None else src
    dst = sh.mv if dst is None else dst
    for t in range(NT):
        v.bn_stats(sh.moments[:, t, :], src[:, NT * b + t, :])
    vector.drain()
    for t in range(NT):
        v.bn_aggr(sh.batch_mv[:, t, :], sh.moments[:, t, :])
    vector.drain()
    v.tensor_copy(dst[:, bass.ds(NT * b, NT), :], sh.batch_mv[:, :, :])


def tokenise(nc, sh, ins, h0):
    RB = 16
    n1, n2, n3 = 8 * 128, 4 * 64, 2 * 32
    with ExitStack() as ctx:
        sb = lambda name, shape, dt=F32: ctx.enter_context(nc.sbuf_tensor(name, shape, dt))
        sem = lambda name: ctx.enter_context(nc.semaphore(name))
        img = sb("img", [128, RB, IMG])
        out = sb("img_out", [128, RB, IMG])
        s = sb("haar_s", [128, RB, 128])
        d = sb("haar_d", [128, RB, 128])
        a1 = sb("a1", [128, 8, 128])
        a2 = sb("a2", [128, 4, 64])
        a3 = sb("a3", [128, 2, 32])
        det = [sb("det1", [128, 3, n1]), sb("det2", [128, 3, n2]), sb("det3", [128, 3, n3])]
        wd = [sb("wd1", [128, 3, 3 * n1]), sb("wd2", [128, 3, 3 * n2]), sb("wd3", [128, 3, 3 * n3])]
        wa = sb("wa", [128, n3])
        gb = sb("gb", [128, 10])
        gs = sb("gs", [128, 10])
        group = sb("group", [128, 128])
        dots = sb("dots", [128, 10])
        z = sb("z", [128, 10])
        zm = sb("zm", [128, 3])
        ez = sb("ez", [128, 10])
        ps = ctx.enter_context(nc.psum_tensor("ps_gate", [128, 512], F32))
        img_in, wa_in, h0_out, h_in, txt_out = (sem(n) for n in ("img_in", "wa_in", "h0_out", "h_in", "txt_out"))
        wd_in = [sem(f"wd_in{i}") for i in range(3)]
        dots_done, summed, z_ready, exp_done, image_ready, group_ready = (
            sem(n) for n in ("dots_done", "summed", "z_ready", "exp_done", "image_ready", "group_ready"))
        const_ready = sem("const_ready")
        block = ctx.enter_context(nc.Block())

        @block.sync
        def _(sync):
            sync.dma_start(img[:, :, :], ins["x"].rearrange("(p r) c -> p r c", r=RB)).then_inc(img_in, 16)
            for lv in (2, 1, 0):
                for b in range(B):
                    sync.dma_start(wd[lv][16 * b:16 * b + 16, :, :], ins[f"wd{lv}"]).then_inc(wd_in[lv], 16)
            sync.dma_start(h0[:, IMG:T, :], ins["txt"]).then_inc(txt_out, 16)
            sync.wait_ge(image_ready, 1)
            for b in range(B):
                sync.dma_start(h0[b, 0:IMG, :].rearrange("(p r) c -> p r c", r=RB),
                               out[16 * b:16 * b + 16, :, :]).then_inc(h0_out, 16)
            sync.wait_ge(txt_out, 16)
            sync.wait_ge(h0_out, 16 * B)
            sync.dma_start(sh.h[:, :, :],
                           h0.rearrange("b (t p) c -> p (b t) c", p=TT)).then_inc(h_in, 16)
            sync.wait_ge(sh.weights_in, 48)

        @block.gpsimd
        def _(pool):
            nc.gpsimd.memset(sh.ident[:, :], 0.0)
            nc.gpsimd.memset(group[:, :], 1.0)
            nc.gpsimd.memset(sh.eps[:, :], EPS)
            nc.gpsimd.memset(sh.mhalf[:, :], -0.5)
            pool.drain()
            nc.gpsimd.affine_select(out=sh.ident[:, :], in_=sh.ident[:, :], compare_op=ALU.not_equal, fill=1.0,
                                    base=0, pattern=[[-1, 128]], channel_multiplier=1)
            g3 = group[:, :].rearrange("p (g r) -> p g r", r=16)
            nc.gpsimd.affine_select(out=g3, in_=g3, compare_op=ALU.is_ge, fill=0.0,
                                    base=0, pattern=[[-16, 8], [0, 16]], channel_multiplier=1)
            pool.drain()
            nc.gpsimd.affine_select(out=g3, in_=g3, compare_op=ALU.is_ge, fill=0.0,
                                    base=15, pattern=[[16, 8], [0, 16]],
                                    channel_multiplier=-1).then_inc(group_ready, 1)

        @block.scalar
        def _(act):
            act.dma_start(wa[:, :], ins["wa"]).then_inc(wa_in, 16)
            act.dma_start(gb[:, :], ins["gb"].partition_broadcast(128)).then_inc(wa_in, 16)
            act.dma_start(sh.cols[:, :, :], ins["cols"]).then_inc(sh.weights_in, 16)
            act.dma_start(sh.rows[:, :, :], ins["rows"].partition_broadcast(TT)).then_inc(sh.weights_in, 16)
            act.dma_start(sh.w[:, :, :, :], ins["w"]).then_inc(sh.weights_in, 16)
            act.wait_ge(z_ready, 1)
            nc.scalar.activation(ez[:, 0:1], z[:, 0:1], ACT.Exp, scale=-1.0)
            nc.scalar.activation(ez[:, 1:10], z[:, 1:10], ACT.Exp).then_inc(exp_done, 1)

        @block.tensor
        def _(pe):
            pe.wait_ge(group_ready, 1)
            pe.wait_ge(dots_done, 1)
            nc.tensor.matmul(ps[:, 0:10], group[:, :], dots[:, :], start=True, stop=True).then_inc(summed, 1)

        @block.vector
        def _(dve):
            v = nc.vector
            dve.wait_ge(img_in, 16)

            def analysis(src, rows, cols, approx, details):
                s_ = s[:, 0:rows, 0:cols // 2]
                d_ = d[:, 0:rows, 0:cols // 2]
                v.tensor_tensor(s_, src[:, :, 0:cols:2], src[:, :, 1:cols:2], ALU.add)
                v.tensor_tensor(d_, src[:, :, 0:cols:2], src[:, :, 1:cols:2], ALU.subtract)
                dve.drain()
                dt = details[:, :, :].rearrange("p j (r c) -> p j r c", c=cols // 2)
                v.tensor_tensor(approx, s_[:, 0:rows:2, :], s_[:, 1:rows:2, :], ALU.add)
                v.tensor_tensor(dt[:, 0], s_[:, 0:rows:2, :], s_[:, 1:rows:2, :], ALU.subtract)
                v.tensor_tensor(dt[:, 1], d_[:, 0:rows:2, :], d_[:, 1:rows:2, :], ALU.add)
                v.tensor_tensor(dt[:, 2], d_[:, 0:rows:2, :], d_[:, 1:rows:2, :], ALU.subtract)
                dve.drain()

            analysis(img, 16, 256, a1[:, :, :], det[0])
            analysis(a1, 8, 128, a2[:, :, :], det[1])
            analysis(a2, 4, 64, a3[:, :, :], det[2])
            for c, lv in enumerate((2, 1, 0)):
                v.memset(gs[:, 1 + 3 * c:4 + 3 * c], 2.0 ** -(lv + 1))
            v.memset(gs[:, 0:1], 2.0 ** -3)
            dve.wait_ge(wa_in, 32)
            junk = out[:, :, :].rearrange("p r c -> p (r c)")
            v.tensor_tensor_reduce(junk[:, 0:n3], a3[:, :, :].rearrange("p r c -> p (r c)"), wa[:, :], 1.0, 0.0,
                                   ALU.mult, ALU.add, dots[:, 0:1])
            for c, (lv, n) in enumerate(((2, n3), (1, n2), (0, n1))):
                dve.wait_ge(wd_in[lv], 16 * B)
                for j in range(3):
                    dve.drain()
                    r = v.tensor_tensor_reduce(junk[:, 0:3 * n], det[lv][:, :, :].rearrange("p j n -> p (j n)"),
                                               wd[lv][:, j, :], 1.0, 0.0, ALU.mult, ALU.add,
                                               dots[:, 1 + 3 * c + j:2 + 3 * c + j])
            r.then_inc(dots_done, 1)
            dve.wait_ge(summed, 1)
            v.tensor_tensor(z[:, :], ps[:, 0:10], gs[:, :], ALU.mult)
            dve.drain()
            v.tensor_tensor(z[:, :], z[:, :], gb[:, :], ALU.add)
            dve.drain()
            z3 = z[:, 1:10].rearrange("p (l j) -> p l j", j=3)
            v.tensor_reduce(zm[:, :], z3, AX.X, ALU.max)
            dve.drain()
            v.tensor_tensor(z3, z3, zm[:, :].unsqueeze(2).to_broadcast([128, 3, 3]), ALU.subtract).then_inc(z_ready, 1)
            dve.wait_ge(exp_done, 1)
            e3 = ez[:, 1:10].rearrange("p (l j) -> p l j", j=3)
            v.tensor_reduce(zm[:, :], e3, AX.X, ALU.add)
            v.tensor_scalar(ez[:, 0:1], ez[:, 0:1], 1.0, None, ALU.add)
            dve.drain()
            v.reciprocal(zm[:, :], zm[:, :])
            v.reciprocal(ez[:, 0:1], ez[:, 0:1])
            dve.drain()
            v.tensor_tensor(e3, e3, zm[:, :].unsqueeze(2).to_broadcast([128, 3, 3]), ALU.mult)
            dve.drain()
            for a, b, f in ((0, 4, 2.0 ** -6), (4, 7, 2.0 ** -4), (7, 10, 2.0 ** -2)):
                v.tensor_scalar(ez[:, a:b], ez[:, a:b], f, None, ALU.mult)
            dve.drain()
            v.tensor_scalar(z[:, :], ez[:, :], -1.0, None, ALU.mult)
            dve.drain()
            v.tensor_scalar(a3[:, :, :], a3[:, :, :], ez[:, 0:1], None, ALU.mult)
            dve.drain()

            def synthesis(rec, details, g, rows, cols, dst):
                dt = details[:, :, :].rearrange("p j (r c) -> p j r c", c=cols)
                lo = s[:, 0:2 * rows, 0:cols]
                hi = d[:, 0:2 * rows, 0:cols]
                w = lambda j: ez[:, g + j:g + j + 1]
                nw = lambda j: z[:, g + j:g + j + 1]
                v.scalar_tensor_tensor(lo[:, 0:2 * rows:2, :], dt[:, 0], w(0), rec, ALU.mult, ALU.add)
                v.scalar_tensor_tensor(lo[:, 1:2 * rows:2, :], dt[:, 0], nw(0), rec, ALU.mult, ALU.add)
                v.tensor_scalar(dt[:, 1], dt[:, 1], w(1), None, ALU.mult)
                dve.drain()
                v.scalar_tensor_tensor(hi[:, 0:2 * rows:2, :], dt[:, 2], w(2), dt[:, 1], ALU.mult, ALU.add)
                v.scalar_tensor_tensor(hi[:, 1:2 * rows:2, :], dt[:, 2], nw(2), dt[:, 1], ALU.mult, ALU.add)
                dve.drain()
                v.tensor_tensor(dst[:, :, 0:2 * cols:2], lo, hi, ALU.add)
                r = v.tensor_tensor(dst[:, :, 1:2 * cols:2], lo, hi, ALU.subtract)
                return r

            synthesis(a3[:, :, :], det[2], 1, 2, 32, a2)
            dve.drain()
            synthesis(a2[:, :, :], det[1], 4, 4, 64, a1)
            dve.drain()
            synthesis(a1[:, :, :], det[0], 7, 8, 128, out).then_inc(image_ready, 1)
            dve.wait_ge(h_in, 16)
            with dve.Fori(0, B) as b:
                batch_stats(nc, dve, sh, b)


def token_scale(nc, pool, sh, tmp, kind, done):
    g = nc.gpsimd
    var, r = sh.mv[:, :, 1], sh.rs[:, :]
    a, b = tmp[:, 0, :], tmp[:, 1, :]
    eps, mh = sh.eps[0:TT, :], sh.mhalf[0:TT, :]
    g.tensor_tensor(a, var, eps, ALU.add)
    pool.drain()
    if kind == "plain":
        g.tensor_tensor(r, a, mh, ALU.pow).then_inc(done, 1)
        return
    g.tensor_tensor(r, a, mh, ALU.pow)
    pool.drain()
    g.tensor_tensor(b, r, r, ALU.mult)
    pool.drain()
    g.tensor_tensor(b, b, var, ALU.mult)
    pool.drain()
    if kind == "twice":
        g.tensor_tensor(b, b, eps, ALU.add)
        pool.drain()
    else:
        g.tensor_scalar(b, b, 1e-24 / D, None, ALU.max)
        pool.drain()
    g.tensor_tensor(b, b, mh, ALU.pow)
    pool.drain()
    g.tensor_tensor(r, r, b, ALU.mult).then_inc(done, 1)


def attention16(nc, sh, fills):
    H, DH = 16, 16
    NPAIR = 8
    TE = T + 1
    HIGH = -4096
    with ExitStack() as ctx:
        sb = lambda name, shape, dt=F32: ctx.enter_context(nc.sbuf_tensor(name, shape, dt))
        pb = lambda name: ctx.enter_context(nc.psum_tensor(name, [128, 512], F32))
        sem = lambda name: ctx.enter_context(nc.semaphore(name))
        xn = sb("xn", [TT, NT, D])
        xT = sb("xT", [128, KT, T])
        raw = [sb(f"raw{i}", [128, T]) for i in range(2)]
        high = [sb(f"high{i}", [128, T]) for i in range(2)]
        mhigh = sb("mhigh", [8, T])
        halves = sb("halves", [128, 4, 2, TE], F32R)
        qs = [sb(f"qs{i}", [128, NPAIR, TE], F32R) for i in range(2)]
        ks = [sb(f"ks{i}", [128, H, TE], F32R) for i in range(2)]
        pick = sb("pick", [128, 2, 2, 4, 128], F32R)
        vS = [sb(f"vS{i}", [TT, NT, H, 32]) for i in range(2)]
        mx = sb("mx", [TT, NT, H])
        mT = [sb(f"mT{i}", [128, TE], F32R) for i in range(2)]
        spread = sb("spread", [128, 8, TT], F32R)
        PT = [sb(f"PT{i}", [TT, NT, T]) for i in range(4)]
        oS = sb("oS", [128, T])
        rec = sb("rec", [TT, NT, 4])
        tmp = sb("tmp", [TT, NT, 4, DH])
        ps_tmp = sb("ps_tmp", [TT, 2, NTILES])
        bq4 = sb("bq4", [128, KT])
        zeros = sb("zeros", [128, 1792])
        psS = ctx.enter_context(nc.psum_tensor("psS", [128, NT, 512], F32))
        psT = [pb(f"psT{i}") for i in range(2)]
        psO = pb("psO")
        psM = [pb(f"psM{i}") for i in range(2)]
        (scaled, consts, xn_ready, halves_ready, s_done, max_done, mT_ready, st_done, exp_done, pv_done, o_out,
         piece_done) = (sem(n) for n in (
             "scaled", "consts", "xn_ready", "halves_ready", "s_done", "max_done", "mT_ready", "st_done", "exp_done",
             "pv_done", "o_out", "piece_done"))
        piece_out = [sem(f"piece_out{i}") for i in range(2)]
        high_ready, begun = sem("high_ready"), sem("begun")
        filled, zeros_ready = sem("filled"), sem("zeros_ready")
        block = ctx.enter_context(nc.Block())
        qt = lambda a: slice(a * TT, (a + 1) * TT)

        PIECES = [(1, "x", 0), (1, "x", 1), (2, "qk", 0), (2, "ot", 3), (2, "qk", 1),
                  (3, "qk", 2), (3, "qk", 3), (4, "stack", 0), (4, "stack", 1), (5, "stack", 2), (5, "stack", 3),
                  (6, "most", 1), (6, "ot", 0), (7, "stack", 4), (7, "stack", 5), (8, "stack", 6), (8, "stack", 7),
                  (9, "stack", 8), (9, "stack", 9), (10, "stack", 10), (10, "ot", 1), (10, "stack", 11),
                  (11, "stack", 12), (11, "stack", 13), (12, "stack", 14), (12, "stack", 15), (13, "most", 0),
                  (14, "v", 0), (14, "ot", 2), (15, "v", 1)]
        AHEAD = 11
        own = lambda kind, j: kind == "ot" or (kind, j) == ("most", 1)
        PROLOGUE = [(kind, j) for _, kind, j in PIECES if not own(kind, j)]
        N0, NB = len(PROLOGUE), len(PIECES)
        assert NB % 2 == 0

        def place(b, c):
            return c % 2, NB // 2 * b + c // 2, NB * b + c

        def pieces(b, p, step, first, last):
            c = N0 if first else N0 - 1
            found = []
            for at, kind, j in PIECES:
                before = (kind, j, at) == ("ot", 3, 2)
                if first and before or last and not own(kind, j):
                    continue
                if at == step:
                    of = (b - 1, 1 - p) if before else (b, p) if own(kind, j) else (b + 1, 1 - p)
                    found.append((kind, j, *of, *place(b, c)))
                c += 1
            return found

        def last_piece(b, p):
            return ("ot", 3, b, p, *place(b, N0 - 1 + sum(own(kind, j) for _, kind, j in PIECES)))

        def stack_places(b, h):
            js = (2 * (h // 2), 2 * (h // 2) + 1)
            if isinstance(b, int) and b == 0:
                return [place(0, PROLOGUE.index(("stack", j))) for j in js]
            at = [(kind, j) for _, kind, j in PIECES]
            return [place(b - 1, N0 - 1 + at.index(("stack", j))) for j in js]

        def batches(eng, body):
            body(0, 0, True, False)
            with eng.Fori(0, (B - 2) // 2) as i:
                body(2 * i + 1, 1, False, False)
                body(2 * i + 2, 0, False, False)
            body(B - 1, 1, False, True)

        def some(n):
            return not isinstance(n, int) or n > 0

        @block.sync
        def _(sync):
            sync.wait_ge(zeros_ready, 1)
            n = 0
            for f in fills:
                parts = 128 if f.shape[0] % 128 == 0 else TT
                flat = f.rearrange("(p r) c -> p (r c)", p=parts)
                for a in range(0, flat.shape[1], 1792):
                    m = min(1792, flat.shape[1] - a)
                    sync.dma_start(flat[:, a:a + m], zeros[0:parts, 0:m]).then_inc(filled, 16)
                    n += 16
            sync.wait_ge(filled, n)

        @block.gpsimd
        def _(pool):
            g = nc.gpsimd
            token_scale(nc, pool, sh, ps_tmp, "twice", scaled)
            for i in range(2):
                g.memset(mT[i][:, :].bitcast(I32), 0)
                g.memset(ks[i][:, :, :].bitcast(I32), 0)
            for p in range(2):
                g.memset(vS[p][:, :, :, DH:32], 0.0)
            pool.drain()
            for p in range(2):
                c = g.memset(vS[p][:, :, :, DH:DH + 1], 1.0)
            c.then_inc(consts, 1)
            g.memset(zeros[:, :], 0.0).then_inc(zeros_ready, 1)
            pool.drain()

            def halve(b, j):
                pool.wait_ge(high_ready, 4 * b + j + 1)
                pool.sem_inc(begun, 1)
                g.tensor_copy(halves[:, j, 0, 0:T], high[j % 2][:, :])
                g.tensor_tensor(halves[:, j, 1, 0:T], raw[j % 2][:, :], high[j % 2][:, :],
                                ALU.subtract).then_inc(halves_ready, 1)

            pool.wait_ge(consts, 3)
            for j in range(4):
                halve(0, j)

            def body(b, p, first, last):
                for j in range(4):
                    if not last:
                        halve(b + 1, j)
            batches(pool, body)

        @block.vector
        def _(dve):
            v = nc.vector
            dve.wait_ge(scaled, 1)

            def norm(b):
                for t in range(NT):
                    r = v.tensor_scalar(xn[:, t, :], sh.h[:, 3 * b + t, :], sh.mv[:, 3 * b + t, 0:1],
                                        sh.rs[:, bass.ds(3 * b + t, 1)], ALU.subtract, ALU.mult)
                r.then_inc(xn_ready, 1)

            def largest(b, h):
                dve.wait_ge(s_done, H * b + h + 1)
                v.tensor_reduce(mx[:, :, h], psS[0:TT, :, 0:T], AX.X, ALU.max, negate=True).then_inc(max_done, 1)

            def piece(kind, j, b, p, bank, before, number):
                if kind == "qk":
                    dve.wait_ge(piece_out[bank], before + 1)
                    if some(n := 4 * b + j - 1):
                        dve.wait_ge(halves_ready, n)
                    v.tensor_scalar(high[j % 2][:, :].bitcast(I32), raw[j % 2][:, :].bitcast(I32), HIGH, None,
                                    ALU.bitwise_and).then_inc(high_ready, 1)
                if kind not in ("v", "most", "ot") and (kind, j % 2) != ("stack", 1):
                    return
                dve.wait_ge(piece_done, number + 1)
                src = psM[bank]
                if kind == "stack":
                    for s in range(2):
                        rows = slice(64 * s, 64 * s + 64)
                        r = v.tensor_copy(ks[p][rows, j - 1 + s, :], src[rows, 0:TE])
                    r.then_inc(piece_out[bank], 1)
                if kind == "v":
                    for t in range(2 * j, min(2 * j + 2, NT)):
                        at = D * (t % 2)
                        r = v.tensor_tensor(vS[p][:, t, :, 0:DH], src[0:TT, at:at + D].rearrange("p (h d) -> p h d", d=DH),
                                            sh.row("a_bv").rearrange("p (h d) -> p h d", d=DH), ALU.add)
                    r.then_inc(piece_out[bank], 1)
                if kind == "most":
                    v.tensor_scalar(mhigh[:, :].bitcast(I32), src[0:8, 0:T].bitcast(I32), HIGH, None, ALU.bitwise_and)
                    dve.drain()
                    v.tensor_copy(mT[j][0:8, 0:T], mhigh[:, :])
                    v.tensor_tensor(mT[j][32:40, 0:T], src[0:8, 0:T], mhigh[:, :], ALU.subtract).then_inc(piece_out[bank], 1)
                    dve.drain()
                    dve.sem_inc(mT_ready, 1)
                if kind == "ot":
                    o4 = src[0:TT, 0:384].rearrange("q (t h d) -> q t h d", t=NT, h=4)
                    v.reciprocal(rec[:, :, :], o4[:, :, :, DH])
                    dve.drain()
                    for t in range(NT):
                        r = v.tensor_tensor(tmp[:, t], o4[:, t, :, 0:DH],
                                            rec[:, t].unsqueeze(2).to_broadcast([TT, 4, DH]), ALU.mult)
                    r.then_inc(piece_out[bank], 1)
                    dve.drain()
                    for t in range(NT):
                        hh = sh.h[:, 3 * b + t, 64 * j:64 * j + 64]
                        v.tensor_tensor(hh, hh, tmp[:, t].rearrange("q h d -> q (h d)"), ALU.add)
                    if j == 3:
                        dve.drain()
                        batch_stats(nc, dve, sh, b)

            norm(0)
            v.tensor_scalar(bq4[:, :], sh.cols[:, CIDX["a_bq"], :], DH ** -0.5, None, ALU.mult).then_inc(consts, 1)
            v.memset(halves[:, :, :, :].bitcast(I32), 0)
            v.memset(pick[:, :, :, :, :].bitcast(I32), 0)
            dve.drain()
            for w, highs in ((0, (0, 2)), (1, (0, 1))):
                for gr in range(4):
                    v.tensor_copy(pick[:, w, 0 if gr in highs else 1].rearrange("p r (s g d) -> p r s g d", s=2, g=4)[:, :, :, gr, :],
                                  sh.ident[:, :].rearrange("p (r s d) -> p r s d", r=4, s=2))
            v.tensor_tensor(spread[:, :, :], sh.ident[:, 0:8].unsqueeze(2).to_broadcast([128, 8, TT]),
                            sh.ident[:, 32:40].unsqueeze(2).to_broadcast([128, 8, TT]), ALU.add).then_inc(consts, 1)
            for i, (kind, j) in enumerate(PROLOGUE):
                piece(kind, j, 0, 0, *place(0, i))
                if kind == "stack" and j % 2 == 1:
                    for h in range(max(0, j - 3), min(j - 1, AHEAD)):
                        largest(0, h)

            def body(b, p, first, last):
                for h in range(H):
                    if h == 0 and not last:
                        norm(b + 1)
                    if h < H - AHEAD:
                        largest(b, h + AHEAD)
                    elif not last:
                        largest(b + 1, h + AHEAD - H)
                    for args in pieces(b, p, h, first, last):
                        piece(*args)
                if last:
                    piece(*last_piece(b, p))
            batches(dve, body)

        @block.scalar
        def _(act):
            s = nc.scalar

            def piece(kind, j, b, p, bank, before, number):
                if kind not in ("x", "qk") and (kind, j % 2) != ("stack", 0):
                    return
                act.wait_ge(piece_done, number + 1)
                if kind == "x":
                    s.activation(xT[:, j, :], psM[bank][:, 0:T], ACT.Identity, bias=sh.col("a_b", j),
                                 scale=sh.col("a_g", j)).then_inc(piece_out[bank], 1)
                if kind == "qk":
                    if some(n := 4 * b + j - 1):
                        act.wait_ge(halves_ready, n)
                    bias, scale = (bq4[:, j // 2:j // 2 + 1], DH ** -0.5) if j % 2 == 0 else (sh.col("a_bk", j // 2), 1.0)
                    s.activation(raw[j % 2][:, :], psM[bank][:, 0:T], ACT.Identity, bias=bias,
                                 scale=scale).then_inc(piece_out[bank], 1)
                if kind == "stack":
                    s.activation(qs[p][:, j // 2, :], psM[bank][:, 0:TE], ACT.Copy).then_inc(piece_out[bank], 1)

            def exp(b, u):
                act.wait_ge(st_done, H * NT * b + u + 1)
                if some(n := H * b + u // 3 - 3):
                    act.wait_ge(pv_done, n)
                s.activation(PT[u // 3 % 4][:, u % 3, :], psT[u % 2][0:TT, 0:T], ACT.Exp).then_inc(exp_done, 1)

            def out(b, g):
                act.wait_ge(pv_done, H * b + 4 * g + 4)
                s.activation(oS[:, :], psO[:, 0:T], ACT.Copy).then_inc(o_out, 1)

            for i, (kind, j) in enumerate(PROLOGUE):
                if i == 2:
                    act.wait_ge(consts, 3)
                piece(kind, j, 0, 0, *place(0, i))

            def body(b, p, first, last):
                for h in range(H):
                    if h == 1 and not first:
                        out(b - 1, 3)
                    if h % 4 == 1 and h > 1:
                        out(b, h // 4 - 1)
                    exp(b, 3 * h)
                    exp(b, 3 * h + 1)
                    exp(b, 3 * h + 2)
                    for args in pieces(b, p, h, first, last):
                        piece(*args)
                if last:
                    out(b, 3)
            batches(act, body)

        @block.tensor
        def _(pe):
            mm = nc.tensor.matmul

            def piece(kind, j, b, p, bank, before, number):
                if some(before):
                    pe.wait_ge(piece_out[bank], before)
                dst = psM[bank]
                if kind == "x":
                    if j == 0:
                        pe.wait_ge(xn_ready, b + 1)
                    for t in range(NT):
                        r = nc.tensor.transpose(dst[:, qt(t)], xn[:, t, 128 * j:128 * j + 128], sh.ident[0:TT, 0:TT])
                if kind == "qk":
                    if j == 0:
                        pe.wait_ge(piece_out[1 - bank], before + bank)
                    at = 128 * (j // 2)
                    for c in range(KT):
                        r = mm(dst[:, 0:T], sh.wt("a_q" if j % 2 == 0 else "a_k", c, at, at + 128), xT[:, c, :],
                               start=c == 0, stop=c == KT - 1)
                if kind == "v":
                    for t in range(2 * j, min(2 * j + 2, NT)):
                        at = D * (t % 2)
                        for c in range(KT):
                            r = mm(dst[0:TT, at:at + D], xT[:, c, qt(t)], sh.wt("a_v", c, 0, D),
                                   start=c == 0, stop=c == KT - 1, skip_group_check=True)
                if kind == "stack":
                    w, pair = j % 2, j // 2
                    n = 2 * (pair // 4) + w
                    pe.wait_ge(halves_ready, 4 * b + n + 1)
                    for half in range(2):
                        r = mm(dst[:, 0:TE], pick[:, w, half, pair % 4, :], halves[:, n, half, :], start=half == 0,
                               stop=half == 1)
                if kind == "most":
                    pe.wait_ge(max_done, H * b + 8 * j + 8)
                    for t in range(NT):
                        r = nc.tensor.transpose(dst[0:8, qt(t)], mx[:, t, 8 * j:8 * j + 8], sh.ident[0:TT, 0:TT])
                if kind == "ot":
                    pe.wait_ge(o_out, 4 * b + j + 1)
                    for t in range(NT):
                        r = nc.tensor.transpose(dst[0:TT, 128 * t:128 * t + 128], oS[:, qt(t)], sh.ident[:, :])
                r.then_inc(piece_done, 1)

            def scores(b, p, h):
                for bank, before, _ in stack_places(b, h):
                    pe.wait_ge(piece_out[bank], before + 1)
                if some(n := H * b + h):
                    pe.wait_ge(max_done, n)
                for t in range(NT):
                    r = mm(psS[0:TT, t, 0:TE], qs[p][:, h // 2, qt(t)], ks[p][:, h, :], start=True, stop=True)
                r.then_inc(s_done, 1)

            def scores_less_most(b, p, u):
                h, a = u // 3, u % 3
                if u == 0 or u == 3 * 8:
                    pe.wait_ge(mT_ready, 2 * b + u // 24 + 1)
                if some(n := H * NT * b + u - 1):
                    pe.wait_ge(exp_done, n)
                dst = psT[u % 2][0:TT, 0:TE]
                mm(dst, ks[p][:, h, qt(a)], qs[p][:, h // 2, :], start=True, stop=False)
                mm(dst, spread[:, h % 8, :], mT[h // 8][:, :], start=False, stop=True).then_inc(st_done, 1)

            def values(b, p, h):
                pe.wait_ge(exp_done, H * NT * b + 3 * h + 3)
                if h % 4 == 0 and some(n := 4 * b + h // 4):
                    pe.wait_ge(o_out, n)
                s = 32 * (h % 4)
                for a in range(NT):
                    r = mm(psO[s:s + 32, 0:T], vS[p][:, a, h, :], PT[h % 4][:, a, :], start=a == 0, stop=a == NT - 1)
                r.then_inc(pv_done, 1)

            for i, (kind, j) in enumerate(PROLOGUE):
                if i == 2:
                    pe.wait_ge(consts, 3)
                piece(kind, j, 0, 0, *place(0, i))
                if kind == "stack" and j % 2 == 1:
                    for h in range(max(0, j - 3), min(j - 1, AHEAD)):
                        scores(0, 0, h)

            def body(b, p, first, last):
                for h in range(H):
                    scores_less_most(b, p, 3 * h)
                    scores_less_most(b, p, 3 * h + 1)
                    if h < H - AHEAD:
                        scores(b, p, h + AHEAD)
                    elif not last:
                        scores(b + 1, 1 - p, h + AHEAD - H)
                    scores_less_most(b, p, 3 * h + 2)
                    for args in pieces(b, p, h, first, last):
                        piece(*args)
                    if h > 0:
                        values(b, p, h - 1)
                    elif not first:
                        values(b - 1, 1 - p, H - 1)
                if last:
                    values(b, p, H - 1)
                    piece(*last_piece(b, p))
            batches(pe, body)


def recurrence(nc, sh):
    with ExitStack() as ctx:
        sb = lambda name, shape, dt=F32: ctx.enter_context(nc.sbuf_tensor(name, shape, dt))
        pb = lambda name: ctx.enter_context(nc.psum_tensor(name, [128, 512], F32))
        sem = lambda name: ctx.enter_context(nc.semaphore(name))
        xn = sb("r_xn", [TT, NT, D])
        xT = sb("r_xT", [128, B, KT, T])
        c = sb("r_c", [128, KT, T])
        gates = [sb(f"r_g{i}", [128, KT, T]) for i in range(3)]
        cu = sb("r_cu", [128, KT, T])
        y = [sb(f"r_y{i}", [128, KT, T]) for i in range(2)]
        ps_tmp = sb("r_tmp", [TT, 2, NTILES])
        ps = [pb(f"r_ps{i}") for i in range(8)]
        (scaled, xn_ready, t_done, xT_ready, gate_done, act_done, c_ready, cu_done, cu_out, y_done, y_added, y_out,
         back_done, h_added) = (sem("r_" + n) for n in (
             "scaled", "xn_ready", "t_done", "xT_ready", "gate_done", "act_done", "c_ready", "cu_done", "cu_out",
             "y_done", "y_added", "y_out", "back_done", "h_added"))
        block = ctx.enter_context(nc.Block())
        qt = lambda a: slice(a * TT, (a + 1) * TT)
        GATES = (("f_wf", "f_uf", "f_bf"), ("f_wi", "f_ui", "f_bi"), ("f_wc", "f_uc", "f_bc"))

        @block.gpsimd
        def _(pool):
            token_scale(nc, pool, sh, ps_tmp, "plain", scaled)

        @block.vector
        def _(dve):
            v = nc.vector
            v.memset(c[:, :, :], 0.0)
            dve.drain()
            for k in range(KT):
                r = v.tensor_scalar(c[:, k, :], c[:, k, :], sh.col("f_c0", k), None, ALU.add)
            r.then_inc(c_ready, 1)
            dve.wait_ge(scaled, 1)

            def norm(b):
                for t in range(NT):
                    r = v.tensor_scalar(xn[:, t, :], sh.h[:, 3 * b + t, :], sh.mv[:, 3 * b + t, 0:1],
                                        sh.rs[:, bass.ds(3 * b + t, 1)], ALU.subtract, ALU.mult)
                r.then_inc(xn_ready, 1)

            norm(0)

            def step(b, p, has_next):
                if has_next:
                    dve.wait_ge(t_done, 2 * b + 2)
                    norm(b + 1)
                dve.wait_ge(act_done, 6 * b + 6)
                f, i, g = (x[:, :, :] for x in gates)
                v.tensor_tensor(c[:, :, :], f, c[:, :, :], ALU.mult)
                v.tensor_tensor(i, i, g, ALU.mult)
                dve.drain()
                v.tensor_tensor(c[:, :, :], c[:, :, :], i, ALU.add).then_inc(c_ready, 1)
            both(dve, step)

            def add_state(b, p):
                dve.wait_ge(y_done, b + 1)
                dve.wait_ge(cu_out, 2)
                for k in range(KT):
                    r = v.tensor_tensor(y[p][:, k, :], ps[2 * p + k][:, 0:T], cu[:, k, :], ALU.add)
                r.then_inc(y_added, 1)

            def body(b, p, has_next):
                if has_next:
                    add_state(b + 1, 1 - p)
                dve.wait_ge(back_done, b + 1)
                for t in range(NT):
                    hh = sh.h[:, 3 * b + t, :]
                    v.tensor_tensor(hh, hh, ps[4 + 2 * p + t // 2][0:TT, D * (t % 2):D * (t % 2) + D], ALU.add)
                dve.drain()
                batch_stats(nc, dve, sh, b)
                dve.sem_inc(h_added, 1)
            add_state(0, 0)
            both(dve, body)

        @block.scalar
        def _(act):
            s = nc.scalar

            def turn_out(b):
                for k in range(KT):
                    act.wait_ge(t_done, 2 * b + k + 1)
                    s.activation(xT[:, b, k, :], ps[6 + k][:, 0:T], ACT.Copy).then_inc(xT_ready, 1)
            turn_out(0)

            def step(b, p, has_next):
                if has_next:
                    turn_out(b + 1)
                for g in range(3):
                    for k in range(KT):
                        act.wait_ge(gate_done, 6 * b + 2 * g + k + 1)
                        s.activation(gates[g][:, k, :], ps[2 * g + k][:, 0:T], ACT.Tanh if g == 2 else ACT.Sigmoid,
                                     bias=sh.col(GATES[g][2], k)).then_inc(act_done, 1)
            both(act, step)
            act.wait_ge(cu_done, 1)
            for k in range(KT):
                s.activation(cu[:, k, :], ps[4 + k][:, 0:T], ACT.Identity, bias=sh.col("f_bo", k)).then_inc(cu_out, 1)

            def body(b, p, has_next):
                act.wait_ge(y_added, b + 1)
                s.activation(y[p][:, :, :], y[p][:, :, :], ACT.Tanh).then_inc(y_out, 1)
            both(act, body)

        @block.tensor
        def _(pe):
            mm = nc.tensor.matmul

            def turn(b):
                pe.wait_ge(xn_ready, b + 1)
                pe.wait_ge(xT_ready, 2 * b)
                for k in range(KT):
                    for t in range(NT):
                        r = nc.tensor.transpose(ps[6 + k][:, qt(t)], xn[:, t, 128 * k:128 * k + 128],
                                                sh.ident[0:TT, 0:TT])
                    r.then_inc(t_done, 1)

            def input_part(b):
                pe.wait_ge(xT_ready, 2 * b + 2)
                for g in range(3):
                    for m in range(KT):
                        pe.wait_ge(act_done, 6 * b + (2 * g + m - 5 if not isinstance(b, int) or b > 0 else 0))
                        for k in range(KT):
                            mm(ps[2 * g + m][:, 0:T], sh.wt(GATES[g][0], k, 128 * m, 128 * m + 128), xT[:, b, k, :],
                               start=k == 0, stop=False, skip_group_check=True)

            turn(0)
            input_part(0)

            def step(b, p, has_next):
                pe.wait_ge(c_ready, b + 1)
                for g in range(3):
                    for m in range(KT):
                        for k in range(KT):
                            r = mm(ps[2 * g + m][:, 0:T], sh.wt(GATES[g][1], k, 128 * m, 128 * m + 128), c[:, k, :],
                                   start=False, stop=k == KT - 1, skip_group_check=True)
                        r.then_inc(gate_done, 1)
                    if g == 0 and has_next:
                        turn(b + 1)
                if has_next:
                    input_part(b + 1)
            both(pe, step)
            pe.wait_ge(c_ready, B + 1)
            for m in range(KT):
                for k in range(KT):
                    r = mm(ps[4 + m][:, 0:T], sh.wt("f_uo", k, 128 * m, 128 * m + 128), c[:, k, :],
                           start=k == 0, stop=k == KT - 1)
            r.then_inc(cu_done, 1)

            def output(b, p):
                pe.wait_ge(y_added, b - 1 if not isinstance(b, int) or b > 0 else 0)
                for m in range(KT):
                    for k in range(KT):
                        r = mm(ps[2 * p + m][:, 0:T], sh.wt("f_wo", k, 128 * m, 128 * m + 128), xT[:, b, k, :],
                               start=k == 0, stop=k == KT - 1)
                r.then_inc(y_done, 1)
            output(0, 0)
            pe.wait_ge(cu_out, 2)

            def body(b, p, has_next):
                if has_next:
                    output(b + 1, 1 - p)
                pe.wait_ge(y_out, b + 1)
                pe.wait_ge(h_added, b)
                for t in range(NT):
                    for k in range(KT):
                        at = D * (t % 2) + 128 * k
                        r = nc.tensor.transpose(ps[4 + 2 * p + t // 2][0:TT, at:at + 128], y[p][:, k, qt(t)],
                                                sh.ident[:, :])
                r.then_inc(back_done, 1)
            both(pe, body)


def scan_layer(nc, sh):
    with ExitStack() as ctx:
        sb = lambda name, shape, dt=F32: ctx.enter_context(nc.sbuf_tensor(name, shape, dt))
        pb = lambda name: ctx.enter_context(nc.psum_tensor(name, [128, 512], F32))
        sem = lambda name: ctx.enter_context(nc.semaphore(name))
        xn = sb("s_xn", [TT, NT, D])
        xT = [sb(f"s_xT{i}", [128, KT, T]) for i in range(2)]
        decay = sb("s_decay", [128, KT, T])
        y = sb("s_y", [128, KT, T])
        ps_tmp = sb("s_tmp", [TT, 2, NTILES])
        psA = [pb(f"s_psA{i}") for i in range(2)]
        psK = [pb(f"s_psK{i}") for i in range(2)]
        psQ = [pb(f"s_psQ{i}") for i in range(2)]
        psT = [pb(f"s_psT{i}") for i in range(2)]
        scaled, xn_ready, t_done, xT_ready, a_done, a_out, k_done, q_done, y_ready, back_done, h_added = (
            sem("s_" + n) for n in ("scaled", "xn_ready", "t_done", "xT_ready", "a_done", "a_out", "k_done",
                                    "q_done", "y_ready", "back_done", "h_added"))
        block = ctx.enter_context(nc.Block())
        qt = lambda a: slice(a * TT, (a + 1) * TT)

        @block.gpsimd
        def _(pool):
            token_scale(nc, pool, sh, ps_tmp, "rms", scaled)

        @block.vector
        def _(dve):
            v = nc.vector
            dve.wait_ge(scaled, 1)

            def norm(b):
                for t in range(NT):
                    r = v.tensor_scalar(xn[:, t, :], sh.h[:, 3 * b + t, :], sh.mv[:, 3 * b + t, 0:1],
                                        sh.rs[:, bass.ds(3 * b + t, 1)], ALU.subtract, ALU.mult)
                r.then_inc(xn_ready, 1)
            norm(0)

            def body(b, p, has_next):
                if has_next:
                    dve.wait_ge(t_done, 2 * b + 2)
                    norm(b + 1)
                for m in range(KT):
                    dve.wait_ge(a_out, 2 * b + m + 1)
                    dve.wait_ge(k_done, 2 * b + m + 1)
                    v.tensor_tensor_scan(y[:, m, :], decay[:, m, :], psK[m][:, 0:T], 0.0, ALU.mult, ALU.add)
                for m in range(KT):
                    dve.drain()
                    dve.wait_ge(q_done, 2 * b + m + 1)
                    v.tensor_tensor(y[:, m, :], y[:, m, :], psQ[m][:, 0:T], ALU.mult).then_inc(y_ready, 1)
                dve.wait_ge(back_done, b + 1)
                for t in range(NT):
                    hh = sh.h[:, 3 * b + t, :]
                    r = v.tensor_tensor(hh, hh, psT[t // 2][0:TT, D * (t % 2):D * (t % 2) + D], ALU.add)
                r.then_inc(h_added, 1)
                dve.drain()
                batch_stats(nc, dve, sh, b)
            both(dve, body)

        @block.scalar
        def _(act):
            s = nc.scalar

            def turn_out(b, p):
                for k in range(KT):
                    act.wait_ge(t_done, 2 * b + k + 1)
                    s.activation(xT[p][:, k, :], psT[k][:, 0:T], ACT.Identity, scale=sh.col("s_g", k)).then_inc(xT_ready, 1)
            turn_out(0, 0)

            def body(b, p, has_next):
                if has_next:
                    turn_out(b + 1, 1 - p)
                for m in range(KT):
                    act.wait_ge(a_done, 2 * b + m + 1)
                    act.wait_ge(y_ready, 2 * b)
                    s.activation(decay[:, m, :], psA[m][:, 0:T], ACT.Sigmoid).then_inc(a_out, 1)
            both(act, body)

        @block.tensor
        def _(pe):
            mm = nc.tensor.matmul

            def turn(b):
                pe.wait_ge(xn_ready, b + 1)
                pe.wait_ge(h_added, b - 1 if not isinstance(b, int) or b > 0 else 0)
                for k in range(KT):
                    for t in range(NT):
                        r = nc.tensor.transpose(psT[k][:, qt(t)], xn[:, t, 128 * k:128 * k + 128],
                                                sh.ident[0:TT, 0:TT])
                    r.then_inc(t_done, 1)

            def project(name, dst, p, m, done):
                for k in range(KT):
                    r = mm(dst[m][:, 0:T], sh.wt(name, k, 128 * m, 128 * m + 128), xT[p][:, k, :],
                           start=k == 0, stop=k == KT - 1)
                r.then_inc(done, 1)
            turn(0)

            def body(b, p, has_next):
                pe.wait_ge(xT_ready, 2 * b + 2)
                if has_next:
                    turn(b + 1)
                pe.wait_ge(a_out, 2 * b)
                pe.wait_ge(y_ready, 2 * b)
                for m in range(KT):
                    project("s_a", psA, p, m, a_done)
                    project("s_kv", psK, p, m, k_done)
                for m in range(KT):
                    project("s_q", psQ, p, m, q_done)
                pe.wait_ge(y_ready, 2 * b + 2)
                if has_next:
                    pe.wait_ge(xT_ready, 2 * b + 4)
                for t in range(NT):
                    for k in range(KT):
                        at = D * (t % 2) + 128 * k
                        r = nc.tensor.transpose(psT[t // 2][0:TT, at:at + 128], y[:, k, qt(t)], sh.ident[:, :])
                r.then_inc(back_done, 1)
            both(pe, body)


def quantised(nc, sh, ins):
    R = 32
    GROUP = 16
    with ExitStack() as ctx:
        sb = lambda name, shape, dt=F32: ctx.enter_context(nc.sbuf_tensor(name, shape, dt))
        pb = lambda name: ctx.enter_context(nc.psum_tensor(name, [128, 512], F32))
        sem = lambda name: ctx.enter_context(nc.semaphore(name))
        wq = sb("q_wq", [128, 6, KT, D])
        qi = sb("q_qi", [128, 6, KT, D], I32)
        sc = sb("q_sc", [128, 6, KT, D])
        la = sb("q_la", [R, 6, D])
        lb = sb("q_lb", [R, 6, D])
        g = sb("q_g", [TT, NTILES, D])
        y = sb("q_y", [TT, NTILES, D])
        xn = sb("q_xn", [TT, NT, D])
        xT = [sb(f"q_xT{i}", [128, KT, T]) for i in range(2)]
        mv = sb("q_mv", [TT, NTILES, 2])
        ps_tmp = sb("q_tmp", [TT, 2, NTILES])
        psT = [[pb(f"q_psT{p}{k}") for k in range(KT)] for p in range(2)]
        psY = [[pb(f"q_psY{p}{k}") for k in range(2)] for p in range(2)]
        scaled, w_in, lora_done, w_ready, x_ready, t_done, xT_ready, y_done, y_out, stats_ready, y_scaled, g_ready = (
            sem("q_" + n) for n in ("scaled", "w_in", "lora_done", "w_ready", "x_ready", "t_done", "xT_ready",
                                    "y_done", "y_out", "stats_ready", "y_scaled", "g_ready"))
        block = ctx.enter_context(nc.Block())
        qt = lambda a: slice(a * TT, (a + 1) * TT)
        PASSES = 6

        @block.sync
        def _(sync):
            sync.dma_start(qi[:, :, :, :], ins["qw"]).then_inc(w_in, 16)
            for r in range(128 // GROUP):
                sync.dma_start(sc[GROUP * r:GROUP * r + GROUP, :, :, :], ins["qs"][r].partition_broadcast(GROUP)).then_inc(w_in, 16)
            sync.dma_start(la[:, :, :], ins["qla"]).then_inc(w_in, 16)
            sync.dma_start(lb[:, :, :], ins["qlb"]).then_inc(w_in, 16)

        @block.gpsimd
        def _(pool):
            token_scale(nc, pool, sh, ps_tmp, "plain", scaled)
            gp = nc.gpsimd
            for j in range(3):
                pool.wait_ge(g_ready, j + 1)

                def stage(b, p, has_next, j=j):
                    pool.wait_ge(t_done, B * 2 * j + b)
                    for t in range(NT):
                        r = gp.tensor_copy(xn[:, t, :], g[:, 3 * b + t, :])
                    r.then_inc(x_ready, 1)
                both(pool, stage)
                pool.wait_ge(stats_ready, j + 1)
                gp.tensor_tensor(ps_tmp[:, 0, :], mv[:, :, 1], sh.eps[0:TT, :], ALU.add)
                pool.drain()
                gp.tensor_tensor(sh.rs[:, :], ps_tmp[:, 0, :], sh.mhalf[0:TT, :], ALU.pow).then_inc(y_scaled, 1)
                pool.drain()

        @block.vector
        def _(dve):
            v = nc.vector
            dve.wait_ge(w_in, 16 * 11)
            v.tensor_scalar(wq[:, :, :, :], qi[:, :, :, :], 1.0 / 7.5, 1.0, ALU.mult, ALU.subtract)
            dve.drain()
            v.tensor_tensor(wq[:, :, :, :], wq[:, :, :, :], sc[:, :, :, :], ALU.mult)
            for i in range(6):
                dve.drain()
                dve.wait_ge(lora_done, i + 1)
                v.tensor_tensor(wq[:, i, :, :], wq[:, i, :, :],
                                psT[i % 2][0][:, :].rearrange("p (k o) -> p k o", k=KT), ALU.add).then_inc(w_ready, 1)
            dve.wait_ge(scaled, 1)
            with dve.Fori(0, NTILES) as t:
                v.tensor_scalar(g[:, t, :], sh.h[:, t, :], sh.mv[:, t, 0:1],
                                sh.rs[:, bass.ds(t, 1)], ALU.subtract, ALU.mult)
            dve.drain()
            dve.sem_inc(g_ready, 1)
            for n in range(PASSES):
                first = n % 2 == 0
                j = n // 2
                if not first:
                    dve.wait_ge(y_scaled, j + 1)

                    def norm(b):
                        for t in range(NT):
                            r = v.tensor_scalar(xn[:, t, :], y[:, 3 * b + t, :], mv[:, 3 * b + t, 0:1],
                                                sh.rs[:, bass.ds(3 * b + t, 1)], ALU.subtract, ALU.mult)
                        r.then_inc(x_ready, 1)
                    norm(0)

                def body(b, p, has_next, n=n, first=first):
                    if has_next and not first:
                        dve.wait_ge(t_done, B * n + b + 1)
                        norm(b + 1)
                    dve.wait_ge(y_done, B * n + b + 1)
                    for t in range(NT):
                        src = psY[p][t // 2][0:TT, D * (t % 2):D * (t % 2) + D]
                        r = v.tensor_tensor(y[:, 3 * b + t, :], src, sh.row(f"q_{n}"), ALU.add)
                    r.then_inc(y_out, 1)
                    dve.drain()
                    if first:
                        batch_stats(nc, dve, sh, b, y, mv)
                    else:
                        bt = bass.ds(NT * b, NT)
                        v.tensor_tensor(g[:, bt, :], g[:, bt, :], y[:, bt, :], ALU.add)
                        if n == PASSES - 1:
                            dve.drain()
                            v.tensor_tensor(sh.h[:, bt, :], sh.h[:, bt, :], g[:, bt, :], ALU.add)
                            dve.drain()
                            batch_stats(nc, dve, sh, b)
                both(dve, body)
                dve.drain()
                if first:
                    dve.sem_inc(stats_ready, 1)
                elif n < PASSES - 1:
                    dve.sem_inc(g_ready, 1)

        @block.scalar
        def _(act):
            s = nc.scalar
            for n in range(PASSES):
                def turn_out(b, p, n=n):
                    act.wait_ge(t_done, B * n + b + 1)
                    for k in range(KT):
                        src = psT[p][k][:, 0:T]
                        if n % 2 == 0:
                            r = s.activation(xT[p][:, k, :], src, ACT.Copy)
                        else:
                            r = s.activation(xT[p][:, k, :], src, ACT.Gelu, bias=sh.col(f"q_b{n // 2}", k),
                                             scale=sh.col(f"q_g{n // 2}", k))
                    r.then_inc(xT_ready, 1)
                both(act, lambda b, p, has_next: turn_out(b, p))

        @block.tensor
        def _(pe):
            mm = nc.tensor.matmul
            pe.wait_ge(w_in, 16 * 11)
            for i in range(6):
                if i >= 2:
                    pe.wait_ge(w_ready, i - 1)
                for k in range(KT):
                    r = mm(psT[i % 2][0][:, D * k:D * k + D], la[:, i, 128 * k:128 * k + 128], lb[:, i, :],
                           start=True, stop=True)
                r.then_inc(lora_done, 1)
            pe.wait_ge(w_ready, 6)
            for n in range(PASSES):

                def turn(b, p, n=n):
                    pe.wait_ge(x_ready, B * n + b + 1)
                    pe.wait_ge(xT_ready, B * n + b - 1 if n > 0 or not isinstance(b, int) or b > 0 else 0)
                    for k in range(KT):
                        for t in range(NT):
                            r = nc.tensor.transpose(psT[p][k][:, qt(t)], xn[:, t, 128 * k:128 * k + 128],
                                                    sh.ident[0:TT, 0:TT])
                    r.then_inc(t_done, 1)
                turn(0, 0)

                def body(b, p, has_next, n=n):
                    if has_next:
                        turn(b + 1, 1 - p)
                    pe.wait_ge(xT_ready, B * n + b + 1)
                    pe.wait_ge(y_out, B * n + b - 1 if n > 0 else (b if not isinstance(b, int) else max(b - 1, 0)))
                    for t in range(NT):
                        for k in range(KT):
                            r = mm(psY[p][t // 2][0:TT, D * (t % 2):D * (t % 2) + D], xT[p][:, k, qt(t)],
                                   wq[:, n, k, :], start=k == 0, stop=k == KT - 1, skip_group_check=True)
                    r.then_inc(y_done, 1)
                both(pe, body)


def masked_attention(nc, sh, ins, experts):
    NP = 9
    LOWEST = -3.4028234663852886e38
    with ExitStack() as ctx:
        sb = lambda name, shape, dt=F32: ctx.enter_context(nc.sbuf_tensor(name, shape, dt))
        pb = lambda name: ctx.enter_context(nc.psum_tensor(name, [128, 512], F32))
        sem = lambda name: ctx.enter_context(nc.semaphore(name))
        xn = sb("m_xn", [TT, NT, D])
        xT = sb("m_xT", [128, KT, T])
        qT = [sb(f"m_qT{i}", [128, KT, T]) for i in range(2)]
        kT = [sb(f"m_kT{i}", [128, KT, T]) for i in range(2)]
        vS = [sb(f"m_vS{i}", [TT, NT, D]) for i in range(2)]
        mask = sb("m_mask", [TT, 5 * TT])
        Sm = [sb(f"m_S{i}", [TT, T]) for i in range(2)]
        P = [sb(f"m_P{i}", [TT, T]) for i in range(2)]
        PT = [sb(f"m_PT{i}", [TT, NT, TT]) for i in range(2)]
        mx, nm, su, rec = (sb("m_" + n, [TT, 2]) for n in ("mx", "nm", "su", "rec"))
        bq = sb("m_bq", [128, KT])
        ps_tmp = sb("m_tmp", [TT, 2, NTILES])
        psM = [pb(f"m_psM{i}") for i in range(2)]
        psV = pb("m_psV")
        psS = [pb(f"m_psS{i}") for i in range(2)]
        psP = [pb(f"m_psP{i}") for i in range(2)]
        psO = pb("m_psO")
        (scaled, consts, xn_ready, piece_done, piece_out, v_done, v_out, s_done, max_done, exp_done, t_done, pt_done,
         pv_done, h_added, row_begun) = (sem("m_" + n) for n in (
             "scaled", "consts", "xn_ready", "piece_done", "piece_out", "v_done", "v_out", "s_done", "max_done",
             "exp_done", "t_done", "pt_done", "pv_done", "h_added", "row_begun"))
        block = ctx.enter_context(nc.Block())
        qt = lambda a: slice(a * TT, (a + 1) * TT)

        @block.sync
        def _(sync):
            experts.load(sync, ins["moe1"], range(3, E))

        @block.gpsimd
        def _(pool):
            token_scale(nc, pool, sh, ps_tmp, "plain", scaled)
            nc.gpsimd.memset(mask[:, :], 0.0)
            pool.drain()
            nc.gpsimd.affine_select(out=mask[:, :], in_=mask[:, :], compare_op=ALU.not_equal, fill=LOWEST,
                                    base=2 * TT, pattern=[[-1, 5 * TT]], channel_multiplier=1).then_inc(consts, 1)

        @block.vector
        def _(dve):
            v = nc.vector
            v.tensor_scalar(bq[:, :], sh.cols[:, CIDX["m_bq"], :], 1.0 / D, None, ALU.mult).then_inc(consts, 1)
            dve.wait_ge(consts, 2)
            dve.wait_ge(scaled, 1)

            def norm(b):
                for t in range(NT):
                    r = v.tensor_scalar(xn[:, t, :], sh.h[:, 3 * b + t, :], sh.mv[:, 3 * b + t, 0:1],
                                        sh.rs[:, bass.ds(3 * b + t, 1)], ALU.subtract, ALU.mult)
                r.then_inc(xn_ready, 1)

            def value_out(b, p, t):
                dve.wait_ge(v_done, NT * b + t + 1)
                v.tensor_tensor(vS[p][:, t, :], psV[0:TT, 0:D], sh.row("m_bv"), ALU.add).then_inc(v_out, 1)

            norm(0)
            for t in range(NT):
                value_out(0, 0, t)

            def body(b, p, has_next):
                def row_max(u):
                    i = (p + u) % 2
                    dve.wait_ge(s_done, NT * b + u + 1)
                    dve.wait_ge(exp_done, NT * b + (u - 1 if u >= 1 else 0))
                    dve.sem_inc(row_begun, 1)
                    at = (2 - u) * TT
                    v.tensor_tensor_reduce(Sm[i][:, :], psS[i][0:TT, 0:T], mask[:, at:at + T], 1.0, LOWEST,
                                           ALU.add, ALU.max, mx[:, i:i + 1])
                    dve.drain()
                    v.tensor_scalar(nm[:, i:i + 1], mx[:, i:i + 1], -1.0, None, ALU.mult).then_inc(max_done, 1)

                def turned(u):
                    i = (p + u) % 2
                    dve.wait_ge(t_done, NT * b + u + 1)
                    dve.wait_ge(pv_done, NT * b + (u - 1 if u >= 1 else 0))
                    v.tensor_copy(PT[i][:, :, :], psP[i][0:TT, 0:T].rearrange("k (a q) -> k a q", a=NT)).then_inc(pt_done, 1)

                def combine(u):
                    i = (p + u) % 2
                    v.reciprocal(rec[:, i:i + 1], su[:, i:i + 1])
                    dve.drain()
                    dve.wait_ge(pv_done, NT * b + u + 1)
                    hh = sh.h[:, 3 * b + u, :]
                    v.scalar_tensor_tensor(hh, psO[0:TT, 0:D], rec[:, i:i + 1], hh, ALU.mult, ALU.add).then_inc(h_added, 1)

                row_max(0)
                if has_next:
                    dve.wait_ge(piece_done, 6 * b + 2)
                    norm(b + 1)
                row_max(1)
                turned(0)
                row_max(2)
                turned(1)
                combine(0)
                turned(2)
                combine(1)
                if has_next:
                    value_out(b + 1, 1 - p, 0)
                combine(2)
                if has_next:
                    value_out(b + 1, 1 - p, 1)
                    value_out(b + 1, 1 - p, 2)
                dve.drain()
                batch_stats(nc, dve, sh, b)
            both(dve, body)

        @block.scalar
        def _(act):
            s = nc.scalar
            act.wait_ge(consts, 2)

            def piece(b, p, k):
                act.wait_ge(piece_done, 6 * b + k + 1)
                src = psM[k % 2][:, 0:T]
                j = k % 2
                if k < 2:
                    r = s.activation(xT[:, j, :], src, ACT.Copy)
                elif k < 4:
                    r = s.activation(qT[p][:, j, :], src, ACT.Identity, bias=bq[:, j:j + 1], scale=1.0 / D)
                else:
                    r = s.activation(kT[p][:, j, :], src, ACT.Identity, bias=sh.col("m_bk", j))
                r.then_inc(piece_out, 1)
            for k in range(6):
                piece(0, 0, k)

            def body(b, p, has_next):
                def exp(u):
                    i = (p + u) % 2
                    act.wait_ge(max_done, NT * b + u + 1)
                    act.wait_ge(t_done, NT * b + (u - 1 if u >= 1 else 0))
                    act.wait_ge(h_added, NT * b + (u - 1 if u >= 1 else 0))
                    s.activation(P[i][:, :], Sm[i][:, :], ACT.Exp, bias=nm[:, i:i + 1],
                                 accum_out=su[:, i:i + 1]).then_inc(exp_done, 1)

                def next_piece(k):
                    if has_next:
                        piece(b + 1, 1 - p, k)
                exp(0)
                next_piece(0)
                next_piece(1)
                exp(1)
                next_piece(2)
                exp(2)
                next_piece(3)
                next_piece(4)
                next_piece(5)
            both(act, body)

        @block.tensor
        def _(pe):
            mm = nc.tensor.matmul

            def piece(b, p, k):
                if k == 0:
                    pe.wait_ge(xn_ready, b + 1)
                if k in (0, 1):
                    pe.wait_ge(piece_out, 6 * b)
                else:
                    pe.wait_ge(piece_out, 6 * b + max(2, k - 1))
                j = k % 2
                if k < 2:
                    for t in range(NT):
                        r = nc.tensor.transpose(psM[j][:, qt(t)], xn[:, t, 128 * j:128 * j + 128],
                                                sh.ident[0:TT, 0:TT])
                else:
                    for c in range(KT):
                        r = mm(psM[j][:, 0:T], sh.wt("m_q" if k < 4 else "m_k", c, 128 * j, 128 * j + 128),
                               xT[:, c, :], start=c == 0, stop=c == KT - 1)
                r.then_inc(piece_done, 1)

            def value(b, t):
                pe.wait_ge(v_out, NT * b + t)
                for c in range(KT):
                    r = mm(psV[0:TT, 0:D], xT[:, c, qt(t)], sh.wt("m_v", c, 0, D), start=c == 0, stop=c == KT - 1)
                r.then_inc(v_done, 1)

            for k in range(6):
                piece(0, 0, k)
            for t in range(NT):
                value(0, t)

            def body(b, p, has_next):
                def scores(u):
                    i = (p + u) % 2
                    pe.wait_ge(max_done, NT * b + (u - 1 if u >= 1 else 0))
                    for c in range(KT):
                        r = mm(psS[i][0:TT, 0:T], qT[p][:, c, qt(u)], kT[p][:, c, :], start=c == 0, stop=c == KT - 1)
                    r.then_inc(s_done, 1)

                def turn(u):
                    i = (p + u) % 2
                    pe.wait_ge(exp_done, NT * b + u + 1)
                    pe.wait_ge(pt_done, NT * b + (u - 1 if u >= 1 else 0))
                    for a in range(NT):
                        r = nc.tensor.transpose(psP[i][0:TT, qt(a)], P[i][:, qt(a)], sh.ident[0:TT, 0:TT])
                    r.then_inc(t_done, 1)

                def product(u):
                    i = (p + u) % 2
                    pe.wait_ge(pt_done, NT * b + u + 1)
                    pe.wait_ge(h_added, NT * b + u)
                    for a in range(NT):
                        r = mm(psO[0:TT, 0:D], PT[i][:, a, :], vS[p][:, a, :], start=a == 0, stop=a == NT - 1)
                    r.then_inc(pv_done, 1)

                def next_piece(k):
                    if has_next:
                        piece(b + 1, 1 - p, k)

                def next_value(t):
                    if has_next:
                        value(b + 1, t)
                pe.wait_ge(piece_out, 6 * b + 6)
                pe.wait_ge(v_out, NT * b + NT)
                scores(0)
                scores(1)
                next_piece(0)
                next_piece(1)
                turn(0)
                scores(2)
                next_piece(2)
                turn(1)
                product(0)
                next_piece(3)
                next_piece(4)
                turn(2)
                product(1)
                next_piece(5)
                next_value(0)
                product(2)
                next_value(1)
                next_value(2)
            both(pe, body)


class Experts:
    SIZE = KT * 1024 + 8 * D

    def __init__(self, nc, ctx):
        end = 212863 // 32 * 32
        self.at = end - 4 * E * self.SIZE
        self.w = nc.alloc_sbuf_tensor_at("expert_w", [128, E, self.SIZE], F32, offset=self.at)
        self.loaded = ctx.enter_context(nc.semaphore("experts_loaded"))

    def load(self, eng, src, which):
        for e in which:
            eng.dma_start(self.w[:, e, :], src[e]).then_inc(self.loaded, 16)


def router(nc, sh, ins, pre, wname, bname, capacity, o):
    NX = NTILES * E
    with ExitStack() as ctx:
        sb = lambda name, shape, dt=F32: ctx.enter_context(nc.sbuf_tensor(pre + name, shape, dt))
        pb = lambda name: ctx.enter_context(nc.psum_tensor(pre + name, [128, 512], F32))
        sem = lambda name: ctx.enter_context(nc.semaphore(pre + name))
        xn = [sb(f"xn{i}", [TT, NT, D]) for i in range(2)]
        xT = [sb(f"xT{i}", [128, KT, T]) for i in range(2)]
        wr = sb("wr", [128, KT, E])
        br = sb("br", [TT, E])
        L = sb("L", [TT, NTILES, E])
        oh = sb("oh", [TT, NTILES, E])
        w = sb("w", [TT, NTILES, E])
        m = sb("m", [TT, NTILES])
        idx = sb("idx", [TT, NTILES])
        em8 = sb("em8", [TT, E])
        tri = sb("tri", [TT, TT])
        ones = sb("ones", [TT, TT])
        cnt = sb("cnt", [TT, E, NTILES])
        inc = sb("inc", [TT, E, NTILES])
        again = sb("again", [TT, E, NTILES])
        one8 = sb("one8", [TT, E])
        tot = sb("tot", [TT, E])
        toti = sb("toti", [TT, E], I32)
        base = sb("base", [TT, E])
        tok = sb("tok", [TT, NTILES])
        sl = sb("sl", [TT, NTILES])
        ps_tmp = sb("tmp", [TT, 2, NTILES])
        NS = o["tiles"] if not capacity else 1
        tno = sb("tno", [TT, NS])
        te = sb("te", [TT, NS, E])
        ts1 = sb("ts1", [TT, NS])
        psT = [[pb(f"psT{p}{k}") for k in range(KT)] for p in range(2)]
        psL = [pb(f"psL{p}") for p in range(2)]
        psR, psC = pb("psR"), pb("psC")
        scaled, wr_in, consts, xn_ready, copied, t_done, xT_ready, l_done, l_out, oh_ready, counted, m_ready, p_ready = (
            sem(n) for n in ("scaled", "wr_in", "consts", "xn_ready", "copied", "t_done", "xT_ready", "l_done", "l_out",
                             "oh_ready", "counted", "m_ready", "p_ready"))
        block = ctx.enter_context(nc.Block())
        qt = lambda a: slice(a * TT, (a + 1) * TT)
        bc = lambda x: x.unsqueeze(2).to_broadcast([TT, NTILES, E])

        @block.sync
        def _(sync):
            sync.dma_start(wr[:, :, :], ins[wname]).then_inc(wr_in, 16)
            sync.dma_start(br[:, :], ins[bname].partition_broadcast(TT)).then_inc(wr_in, 16)

        @block.gpsimd
        def _(pool):
            g = nc.gpsimd
            token_scale(nc, pool, sh, ps_tmp, "plain", scaled)
            g.iota(em8[:, :], pattern=[[1, E]], base=-E, channel_multiplier=0, allow_small_or_imprecise_dtypes=True)
            g.iota(tok[:, :], pattern=[[TT, NTILES]], base=0, channel_multiplier=1,
                   allow_small_or_imprecise_dtypes=True)
            g.iota(tno[:, :], pattern=[[1, NS]], base=0, channel_multiplier=0, allow_small_or_imprecise_dtypes=True)
            g.memset(ones[:, :], 1.0)
            g.memset(one8[:, :], 1.0)
            g.memset(again[:, :, :], 1.0)
            pool.drain()
            g.memset(again[:, :, 0:1], 0.0)
            g.affine_select(out=tri[:, :], in_=ones[:, :], compare_op=ALU.is_gt, fill=0.0, base=0,
                            pattern=[[1, TT]], channel_multiplier=-1).then_inc(consts, 1)

            def body(b, p, has_next):
                pool.wait_ge(xn_ready, b + 1)
                for t in range(NT):
                    r = g.tensor_copy(o["xall"][:, 3 * b + t, :], xn[p][:, t, :])
                r.then_inc(copied, 1)
            both(pool, body)

        @block.vector
        def _(dve):
            v = nc.vector
            dve.wait_ge(scaled, 1)

            def norm(b, p):
                ago = b - 1 if not isinstance(b, int) or b > 0 else 0
                dve.wait_ge(copied, ago)
                dve.wait_ge(t_done, ago)
                for t in range(NT):
                    r = v.tensor_scalar(xn[p][:, t, :], sh.h[:, 3 * b + t, :], sh.mv[:, 3 * b + t, 0:1],
                                        sh.rs[:, bass.ds(3 * b + t, 1)], ALU.subtract, ALU.mult)
                r.then_inc(xn_ready, 1)
            norm(0, 0)
            dve.wait_ge(wr_in, 32)

            def body(b, p, has_next):
                if has_next:
                    norm(b + 1, 1 - p)
                dve.wait_ge(l_done, b + 1)
                v.tensor_tensor(L[:, bass.ds(3 * b, 3), :], psL[p][0:TT, 0:3 * E].rearrange("q (t e) -> q t e", e=E),
                                br[:, :].unsqueeze(1).to_broadcast([TT, NT, E]), ALU.add).then_inc(l_out, 1)
            both(dve, body)
            dve.drain()
            dve.wait_ge(consts, 1)
            if not capacity:
                v.tensor_scalar(L[:, :, :], L[:, :, :], 16.635532, None, ALU.min)
                dve.drain()
            v.tensor_reduce(m[:, :], L[:, :, :], AX.X, ALU.max).then_inc(m_ready, 1)
            dve.drain()
            v.tensor_tensor(w[:, :, :], L[:, :, :], bc(m[:, :]), ALU.is_ge)
            dve.drain()
            ebc = em8[:, :].unsqueeze(1).to_broadcast([TT, NTILES, E])
            v.tensor_tensor(w[:, :, :], w[:, :, :], ebc, ALU.mult)
            dve.drain()
            v.tensor_reduce(idx[:, :], w[:, :, :], AX.X, ALU.min)
            dve.drain()
            v.tensor_tensor(oh[:, :, :], ebc, bc(idx[:, :]), ALU.is_equal).then_inc(oh_ready, 1)
            dve.wait_ge(counted, 1)
            v.tensor_copy(cnt[:, :, :], psC[0:TT, 0:NX].rearrange("q (t e) -> q e t", e=E))
            dve.drain()
            v.tensor_tensor_scan(inc[:, :, :].rearrange("q e t -> q (e t)"), again[:, :, :].rearrange("q e t -> q (e t)"),
                                 cnt[:, :, :].rearrange("q e t -> q (e t)"), 0.0, ALU.mult, ALU.add)
            dve.drain()
            v.tensor_copy(tot[:, :], inc[:, :, NTILES - 1])
            v.tensor_tensor(cnt[:, :, :], inc[:, :, :], cnt[:, :, :], ALU.subtract)
            dve.drain()
            v.tensor_tensor(w[:, :, :], psR[0:TT, 0:NX].rearrange("q (t e) -> q t e", e=E),
                            cnt[:, :, :].rearrange("q e t -> q t e"), ALU.add)
            if not capacity:
                v.tensor_scalar(tot[:, :], tot[:, :], 127.0, None, ALU.add)
                dve.drain()
                v.tensor_copy(toti[:, :], tot[:, :])
                dve.drain()
                v.tensor_scalar(toti[:, :], toti[:, :], 7, None, ALU.arith_shift_right)
                dve.drain()
                v.tensor_copy(tot[:, :], toti[:, :])
                dve.drain()
                v.tensor_tensor_scan(base[:, :], one8[:, :], tot[:, :], 0.0, ALU.mult, ALU.add)
                dve.drain()
                v.tensor_tensor(te[:, :, :], base[:, :].unsqueeze(1).to_broadcast([TT, NS, E]),
                                tno[:, :].unsqueeze(2).to_broadcast([TT, NS, E]), ALU.is_le)
                dve.drain()
                v.tensor_reduce(ts1[:, :], te[:, :, :], AX.X, ALU.add)
                dve.drain()
                v.tensor_scalar(ts1[:, :], ts1[:, :], float(E - 1), None, ALU.min)
                v.tensor_tensor(base[:, :], base[:, :], tot[:, :], ALU.subtract)
                dve.drain()
                v.tensor_copy(o["tile_expert"][:, :], ts1[:, :])
                v.tensor_scalar(base[:, :], base[:, :], 128.0, None, ALU.mult)
                dve.drain()
                v.tensor_tensor(w[:, :, :], w[:, :, :], base[:, :].unsqueeze(1).to_broadcast([TT, NTILES, E]), ALU.add)
                dve.drain()
                v.tensor_tensor(w[:, :, :], w[:, :, :], oh[:, :, :], ALU.mult)
                dve.drain()
                v.tensor_reduce(sl[:, :], w[:, :, :], AX.X, ALU.add)
                dve.drain()
                v.tensor_copy(o["slot"][:, :], sl[:, :])
                dve.wait_ge(p_ready, 1)
                v.tensor_scalar(o["prob"][:, :], o["prob"][:, :], 1.0, None, ALU.add)
                dve.drain()
                v.reciprocal(o["prob"][:, :], o["prob"][:, :])
            else:
                dve.drain()
                v.tensor_tensor(w[:, :, :], w[:, :, :], oh[:, :, :], ALU.mult)
                dve.drain()
                v.tensor_reduce(sl[:, :], w[:, :, :], AX.X, ALU.add)
                v.tensor_scalar(idx[:, :], idx[:, :], float(E), float(capacity), ALU.add, ALU.mult)
                dve.drain()
                v.tensor_scalar(o["keep"][:, :], sl[:, :], float(capacity), None, ALU.is_lt)
                v.tensor_scalar(o["drop"][:, :], sl[:, :], float(capacity), None, ALU.is_ge)
                v.tensor_scalar(m[:, :], sl[:, :], float(capacity - 1), None, ALU.min)
                dve.drain()
                v.tensor_tensor(m[:, :], m[:, :], idx[:, :], ALU.add)
                v.tensor_tensor(sl[:, :], sl[:, :], idx[:, :], ALU.add)
                v.tensor_scalar(tok[:, :], tok[:, :], float(E * capacity), None, ALU.add)
                dve.drain()
                v.tensor_copy(o["back"][:, :], m[:, :])
                v.tensor_tensor(sl[:, :], sl[:, :], o["keep"][:, :], ALU.mult)
                v.tensor_tensor(tok[:, :], tok[:, :], o["drop"][:, :], ALU.mult)
                dve.drain()
                v.tensor_tensor(sl[:, :], sl[:, :], tok[:, :], ALU.add)
                dve.drain()
                v.tensor_copy(o["slot"][:, :], sl[:, :])

        @block.scalar
        def _(act):
            s = nc.scalar

            def body(b, p, has_next):
                act.wait_ge(t_done, b + 1)
                for k in range(KT):
                    r = s.activation(xT[p][:, k, :], psT[p][k][:, 0:T], ACT.Copy)
                r.then_inc(xT_ready, 1)
            both(act, body)
            if not capacity:
                act.wait_ge(m_ready, 1)
                s.activation(o["prob"][:, :], m[:, :], ACT.Exp, scale=-1.0).then_inc(p_ready, 1)

        @block.tensor
        def _(pe):
            mm = nc.tensor.matmul

            def turn(b, p):
                pe.wait_ge(xn_ready, b + 1)
                pe.wait_ge(xT_ready, b - 1 if not isinstance(b, int) or b > 0 else 0)
                for k in range(KT):
                    for t in range(NT):
                        r = nc.tensor.transpose(psT[p][k][:, qt(t)], xn[p][:, t, 128 * k:128 * k + 128],
                                                sh.ident[0:TT, 0:TT])
                r.then_inc(t_done, 1)
            turn(0, 0)
            pe.wait_ge(wr_in, 32)

            def body(b, p, has_next):
                if has_next:
                    turn(b + 1, 1 - p)
                pe.wait_ge(xT_ready, b + 1)
                pe.wait_ge(l_out, b)
                for t in range(NT):
                    for k in range(KT):
                        r = mm(psL[p][0:TT, E * t:E * t + E], xT[p][:, k, qt(t)], wr[:, k, :],
                               start=k == 0, stop=k == KT - 1, skip_group_check=True)
                r.then_inc(l_done, 1)
            both(pe, body)
            pe.wait_ge(oh_ready, 1)
            ohf = oh[:, :, :].rearrange("q t e -> q (t e)")
            mm(psC[0:TT, 0:NX], ones[:, :], ohf, start=True, stop=True)
            mm(psR[0:TT, 0:NX], tri[:, :], ohf, start=True, stop=True).then_inc(counted, 1)


MOE_TILES = (B * T + E * 127) // 128


def top1_experts(nc, sh, ins, experts, xs, ys):
    FF = 1024
    with ExitStack() as ctx:
        o = {"tiles": MOE_TILES}
        o["slot"] = ctx.enter_context(nc.sbuf_tensor("t_slot", [TT, NTILES], U32))
        o["prob"] = ctx.enter_context(nc.sbuf_tensor("t_prob", [TT, NTILES], F32))
        o["tile_expert"] = ctx.enter_context(nc.sbuf_tensor("t_te", [TT, MOE_TILES], I32))
        sem = lambda name: ctx.enter_context(nc.semaphore("t_" + name))
        with ExitStack() as c1:
            o["xall"] = c1.enter_context(nc.sbuf_tensor("t_xall", [TT, NTILES, D], F32))
            router(nc, sh, ins, "tr_", "t_wr", "t_br", 0, o)
            scatter_tokens(nc, o, xs, "ts_", lambda sync: experts.load(sync, ins["moe1"], range(0, 3)))

        with ExitStack() as c2:
            sb = lambda name, shape, dt=F32: c2.enter_context(nc.sbuf_tensor("t_" + name, shape, dt))
            pb = lambda name: c2.enter_context(nc.psum_tensor("t_" + name, [128, 512], F32))
            xb = [sb(f"xb{i}", [128, D]) for i in range(2)]
            xT = [sb(f"xT{i}", [128, KT, 128]) for i in range(2)]
            hg = [sb(f"hg{i}", [128, FF]) for i in range(2)]
            hT = sb("hT", [128, 8, 128])
            yb = [sb(f"yb{i}", [128, D]) for i in range(2)]
            psT = pb("psT")
            psH = [[pb(f"psH{p}{i}") for i in range(2)] for p in range(2)]
            psG = [pb(f"psG{i}") for i in range(2)]
            psY = pb("psY")
            x_in = [sem(f"x_in{i}") for i in range(2)]
            y_sent = [sem(f"y_sent{i}") for i in range(2)]
            x_turned, xT_ready, h_done, g_ready, g_turned, gT_ready, y_done, y_out = (sem(n) for n in (
                "x_turned", "xT_ready", "h_done", "g_ready", "g_turned", "gT_ready", "y_done", "y_out"))
            NS = MOE_TILES
            block = c2.enter_context(nc.Block())

            def pairs(eng, body):
                with eng.Fori(0, NS // 2 - 1) as i:
                    body(2 * i, 0, i, True, True)
                    body(2 * i + 1, 1, i, True, True)
                body(NS - 2, 0, NS // 2 - 1, True, False)
                body(NS - 1, 1, NS // 2 - 1, False, False)

            @block.sync
            def _(sync):
                def load(s, p):
                    sync.dma_start(xb[p][:, :], xs[bass.ds(s * 128, 128), :]).then_inc(x_in[p], 16)
                load(0, 0)
                load(1, 1)

                def body(s, p, i, nx, nx2):
                    if nx2:
                        sync.wait_ge(x_turned, s + 1)
                        load(s + 2, p)
                pairs(sync, body)

            @block.scalar
            def _(act):
                sc = nc.scalar

                def body(s, p, i, nx, nx2):
                    for q in range(2):
                        act.wait_ge(h_done, 2 * s + q + 1)
                        act.wait_ge(g_turned, s)
                        sc.activation(hg[p][:, 512 * q:512 * q + 512], psH[p][q][:, :], ACT.Gelu).then_inc(g_ready, 1)
                    act.wait_ge(y_done, s + 1)
                    act.wait_ge(y_sent[p], 16 * i)
                    sc.activation(yb[p][:, :], psY[:, 0:D], ACT.Copy).then_inc(y_out, 1)
                    act.wait_ge(y_out, s + 1)
                    act.dma_start(ys[bass.ds(s * 128, 128), :], yb[p][:, :]).then_inc(y_sent[p], 16)
                pairs(act, body)
                for p in range(2):
                    act.wait_ge(y_sent[p], 16 * (NS // 2))

            @block.vector
            def _(dve):
                v = nc.vector

                def turn_out(s, p):
                    dve.wait_ge(x_turned, s + 1)
                    v.tensor_copy(xT[p][:, :, :], psT[:, 0:2 * 128].rearrange("p (k q) -> p k q", k=KT)).then_inc(xT_ready, 1)
                turn_out(0, 0)
                turn_out(1, 1)

                def body(s, p, i, nx, nx2):
                    for q in range(2):
                        dve.wait_ge(g_turned, s + 1) if q == 0 else None
                        dve.wait_ge(y_done, s)
                        v.tensor_copy(hT[:, 4 * q:4 * q + 4, :],
                                      psG[q][:, :].rearrange("p (c q) -> p c q", c=4)).then_inc(gT_ready, 1)
                    if nx2:
                        turn_out(s + 2, p)
                pairs(dve, body)

            @block.tensor
            def _(pe):
                mm = nc.tensor.matmul

                def expert(s):
                    return nc.tensor.value_load(o["tile_expert"][0:1, bass.ds(s, 1)], min_val=0, max_val=E - 1)

                def turn(s, p, i):
                    pe.wait_ge(x_in[p], 16 * (i + 1))
                    pe.wait_ge(xT_ready, s)
                    for k in range(KT):
                        r = nc.tensor.transpose(psT[:, 128 * k:128 * k + 128], xb[p][:, 128 * k:128 * k + 128], sh.ident[:, :])
                    r.then_inc(x_turned, 1)

                def first(s, p):
                    e = expert(s)
                    pe.wait_ge(xT_ready, s + 1)
                    for q in range(2):
                        pe.wait_ge(g_ready, 2 * s - 2 if not isinstance(s, int) or s > 0 else 0)
                        for k in range(KT):
                            r = mm(psH[p][q][:, :], xT[p][:, k, :],
                                   experts.w[:, e, 1024 * k + 512 * q:1024 * k + 512 * q + 512],
                                   start=k == 0, stop=k == KT - 1)
                        r.then_inc(h_done, 1)
                turn(0, 0, 0)
                turn(1, 1, 0)
                pe.wait_ge(experts.loaded, 16 * E)
                first(0, 0)

                def body(s, p, i, nx, nx2):
                    if nx:
                        first(s + 1, 1 - p)
                    pe.wait_ge(g_ready, 2 * s + 2)
                    pe.wait_ge(gT_ready, 2 * s)
                    for c in range(8):
                        r = nc.tensor.transpose(psG[c // 4][:, 128 * (c % 4):128 * (c % 4) + 128],
                                                hg[p][:, 128 * c:128 * c + 128], sh.ident[:, :])
                    r.then_inc(g_turned, 1)
                    e = expert(s)
                    if nx2:
                        turn(s + 2, p, i + 1)
                    pe.wait_ge(y_out, s)
                    for c in range(8):
                        if c % 4 == 0:
                            pe.wait_ge(gT_ready, 2 * s + c // 4 + 1)
                        at = KT * FF + D * c
                        r = mm(psY[:, 0:D], hT[:, c, :], experts.w[:, e, at:at + D], start=c == 0, stop=c == 7)
                    r.then_inc(y_done, 1)
                pairs(pe, body)

        combine_experts(nc, sh, ctx, o, ys, "tc_", None)


def scatter_tokens(nc, o, xs, pre, meanwhile):
    with nc.semaphore(pre + "scattered") as scattered, nc.Block() as block:
        @block.gpsimd
        def _(pool):
            for t in range(NTILES):
                nc.gpsimd.indirect_dma_start(out=xs[:, :], out_offset=bass.IndirectOffsetOnAxis(o["slot"][:, t:t + 1], 0),
                                             in_=o["xall"][:, t, :], in_offset=None).then_inc(scattered, 16)

        @block.sync
        def _(sync):
            meanwhile(sync)
            sync.wait_ge(scattered, 16 * NTILES)


def combine_experts(nc, sh, ctx, o, ys, pre, out):
    with ExitStack() as c2:
        y = c2.enter_context(nc.sbuf_tensor(pre + "y", [TT, NTILES, D], F32))
        st = c2.enter_context(nc.sbuf_tensor(pre + "st", [TT, 6], F32))
        fetched = [c2.enter_context(nc.semaphore(f"{pre}fetched{b}")) for b in range(B)]
        added = c2.enter_context(nc.semaphore(pre + "added"))
        sent = c2.enter_context(nc.semaphore(pre + "sent"))
        block = c2.enter_context(nc.Block())
        rows = o["slot"] if out is None else o["back"]

        @block.gpsimd
        def _(pool):
            for t in range(NTILES):
                nc.gpsimd.indirect_dma_start(out=y[:, t, :], out_offset=None, in_=ys[:, :],
                                             in_offset=bass.IndirectOffsetOnAxis(rows[:, t:t + 1], 0)).then_inc(fetched[t // NT], 16)

        @block.vector
        def _(dve):
            v = nc.vector
            for b in range(B):
                dve.wait_ge(fetched[b], 16 * NT)
                for t in range(NT * b, NT * b + NT):
                    hh = sh.h[:, t, :]
                    if out is None:
                        r = v.scalar_tensor_tensor(hh, y[:, t, :], o["prob"][:, t:t + 1], hh, ALU.mult, ALU.add)
                    else:
                        v.tensor_scalar(y[:, t, :], y[:, t, :], o["keep"][:, t:t + 1], None, ALU.mult)
                        dve.drain()
                        v.scalar_tensor_tensor(y[:, t, :], o["xall"][:, t, :], o["drop"][:, t:t + 1], y[:, t, :],
                                               ALU.mult, ALU.add)
                        dve.drain()
                        r = v.tensor_tensor(hh, hh, y[:, t, :], ALU.add)
                if out is None:
                    dve.drain()
                    batch_stats(nc, dve, sh, b)
                else:
                    r.then_inc(added, 1)

        @block.sync
        def _(sync):
            if out is not None:
                for b in range(B):
                    sync.wait_ge(added, b + 1)
                    sync.dma_start(out[b].rearrange("(t p) c -> p t c", p=TT),
                                   sh.h[:, NT * b:NT * b + NT, :]).then_inc(sent, 16)
                sync.wait_ge(sent, 16 * B)


H3, KVH, DH3 = 16, 4, 64
HEAD_ORDER = [(2 * (c // 4) + half) * (H3 // KVH) + c % 4 for c in range(8) for half in range(2)]


def alibi_attention(nc, sh, ins, stream):
    NU = H3 * NT
    AHEAD = 8
    NB = 12
    assert NU % NB == 0
    NP = 15
    BIG = 3.4028234663852886e38
    PI = 3.141592653589793
    with ExitStack() as ctx:
        sb = lambda name, shape, dt=F32: ctx.enter_context(nc.sbuf_tensor("l_" + name, shape, dt))
        pb = lambda name: ctx.enter_context(nc.psum_tensor("l_" + name, [128, 512], F32))
        sem = lambda name: ctx.enter_context(nc.semaphore("l_" + name))
        wq_in = sb("wq_in", [128, H3, DH3 // 2, 2])
        wq = sb("wq", [128, H3, DH3 // 2, 2])
        wtmp = sb("wtmp", [128, H3, DH3 // 2])
        wk = sb("wk", [128, D])
        wv = sb("wv", [128, D])
        wo = sb("wo", [128, 8, D])
        ang = sb("ang", [128, 2, H3])
        turns = sb("turns", [128, 2, H3])
        cs = sb("cs", [128, 2, H3])
        slope = sb("slope", [TT, H3])
        rel = sb("rel", [TT, T])
        future = sb("future", [TT, T])
        am = sb("am", [TT, H3, T])
        xn = sb("xn", [TT, NT, D])
        xT = sb("xT", [128, KT, T])
        qT = [sb(f"qT{i}", [128, 8, T]) for i in range(2)]
        kz = [sb(f"kz{i}", [128, KVH, T]) for i in range(2)]
        vS = [sb(f"vS{i}", [TT, NT, D]) for i in range(2)]
        Sm = [sb(f"S{i}", [TT, T]) for i in range(3)]
        P = [sb(f"P{i}", [TT, T]) for i in range(NB)]
        PT = [sb(f"PT{i}", [TT, NT, T]) for i in range(2)]
        oT = [sb(f"oT{i}", [128, T]) for i in range(2)]
        nm = sb("nm", [TT, NB])
        su = sb("su", [TT, NB])
        ri = sb("ri", [TT, NB])
        ps_tmp = sb("tmp", [TT, 2, NTILES])
        psS = [pb(f"psS{i}") for i in range(2)]
        psP = [pb(f"psP{i}") for i in range(2)]
        psO, psM = pb("psO"), pb("psM")
        psW = [pb(f"psW{i}") for i in range(2)]
        (w_in, scaled, rel_ready, consts, ang_ready, sin_ready, slope_ready, xn_ready, piece_done, piece_out, s_done,
         min_done, exp_done, rec_done, p_ready, t_done, pt_done, pv_done, o_out, w_done, h_added, row_begun,
         head_begun, p_last_ready) = (sem(n) for n in (
             "w_in", "scaled", "rel_ready", "consts", "ang_ready", "sin_ready", "slope_ready", "xn_ready", "piece_done",
             "piece_out", "s_done", "min_done", "exp_done", "rec_done", "p_ready", "t_done", "pt_done", "pv_done",
             "o_out", "w_done", "h_added", "row_begun", "head_begun",
             "p_last_ready"))
        block = ctx.enter_context(nc.Block())
        qt = lambda a: slice(a * TT, (a + 1) * TT)

        PIECE_AT = list(range(4, 4 + 2 * NP, 2))

        def of(b, u):
            return (b, u) if u < NU else (b + 1, u - NU)

        @block.sync
        def _(sync):
            for half in range(2):
                sync.dma_start(ang[:, half, :], ins["l_ang"].partition_broadcast(128)).then_inc(w_in, 16)
            sync.dma_start(slope[:, :], ins["l_slope"].partition_broadcast(TT)).then_inc(w_in, 16)
            sync.dma_start(wq_in[:, :, :, :], ins["l_wq"].rearrange("p (h d r) -> p h d r", h=H3, r=2)).then_inc(w_in, 16)
            sync.dma_start(wk[:, :], ins["l_wk"]).then_inc(w_in, 16)
            sync.dma_start(wv[:, :], ins["l_wv"]).then_inc(w_in, 16)
            sync.dma_start(wo[:, :, :], ins["l_wo"]).then_inc(w_in, 16)
            stream.prefetch(sync)

        @block.gpsimd
        def _(pool):
            g = nc.gpsimd
            token_scale(nc, pool, sh, ps_tmp, "plain", scaled)
            g.iota(rel[:, :], pattern=[[-1, T]], base=2 * TT, channel_multiplier=1, allow_small_or_imprecise_dtypes=True)
            g.memset(future[:, :], 0.0)
            for i in range(2):
                g.memset(kz[i][:, :, :], 0.0)
            pool.drain()
            g.affine_select(out=future[:, :], in_=future[:, :], compare_op=ALU.is_ge, fill=BIG, base=2 * TT,
                            pattern=[[-1, T]], channel_multiplier=1).then_inc(rel_ready, 1)

            def body(b, p, has_next):
                for h in range(H3):
                    pool.wait_ge(rec_done, H3 * b + h + 1)
                    pool.sem_inc(head_begun, 1)
                    for t in range(2):
                        i, n = (3 * h + t) % NB, TT * (t + 1)
                        g.tensor_scalar(P[i][:, 0:n], P[i][:, 0:n], ri[:, i:i + 1], None, ALU.mult).then_inc(p_ready, 1)
            both(pool, body)

        @block.vector
        def _(dve):
            v = nc.vector
            dve.wait_ge(w_in, 16 * 7)
            v.tensor_scalar(ang[:, 1, :], ang[:, 1, :], PI / 2, None, ALU.add)
            dve.drain()
            v.tensor_scalar(turns[:, :, :], ang[:, :, :], 1.0 / (2 * PI), None, ALU.mult)
            dve.drain()
            v.tensor_scalar(turns[:, :, :], turns[:, :, :], 12582912.0, None, ALU.add)
            dve.drain()
            v.tensor_scalar(turns[:, :, :], turns[:, :, :], 12582912.0, None, ALU.subtract)
            dve.drain()
            v.scalar_tensor_tensor(ang[:, :, :], turns[:, :, :], -6.28125, ang[:, :, :], ALU.mult, ALU.add)
            dve.drain()
            v.scalar_tensor_tensor(ang[:, :, :], turns[:, :, :], -(2 * PI - 6.28125), ang[:, :, :], ALU.mult, ALU.add)
            dve.drain()
            v.tensor_scalar(ang[:, :, :], ang[:, :, :], 3.1415925, -3.1415925, ALU.min, ALU.max).then_inc(ang_ready, 1)
            dve.wait_ge(sin_ready, 1)
            v.tensor_scalar(cs[:, :, :], cs[:, :, :], -(DH3 ** -0.5), None, ALU.mult)
            dve.drain()
            sn = cs[:, 0, :].unsqueeze(2).to_broadcast([128, H3, DH3 // 2])
            cn = cs[:, 1, :].unsqueeze(2).to_broadcast([128, H3, DH3 // 2])
            v.tensor_tensor(wq[:, :, :, 0], wq_in[:, :, :, 0], cn, ALU.mult)
            v.tensor_tensor(wtmp[:, :, :], wq_in[:, :, :, 1], sn, ALU.mult)
            dve.drain()
            v.tensor_tensor(wq[:, :, :, 0], wq[:, :, :, 0], wtmp[:, :, :], ALU.subtract)
            v.tensor_tensor(wq[:, :, :, 1], wq_in[:, :, :, 0], sn, ALU.mult)
            dve.drain()
            v.tensor_tensor(wtmp[:, :, :], wq_in[:, :, :, 1], cn, ALU.mult)
            dve.drain()
            v.tensor_tensor(wq[:, :, :, 1], wq[:, :, :, 1], wtmp[:, :, :], ALU.add).then_inc(consts, 1)
            dve.wait_ge(rel_ready, 1)
            dve.wait_ge(slope_ready, 1)
            v.tensor_scalar(slope[:, :], slope[:, :], -1.0, None, ALU.mult)
            dve.drain()
            for h in range(H3):
                v.scalar_tensor_tensor(am[:, h, :], rel[:, :], slope[:, h:h + 1], future[:, :], ALU.mult, ALU.add)
            dve.wait_ge(scaled, 1)

            def norm(b):
                for t in range(NT):
                    r = v.tensor_scalar(xn[:, t, :], sh.h[:, 3 * b + t, :], sh.mv[:, 3 * b + t, 0:1],
                                        sh.rs[:, bass.ds(3 * b + t, 1)], ALU.subtract, ALU.mult)
                r.then_inc(xn_ready, 1)

            def piece(b, p, k):
                if k >= 12:
                    dve.wait_ge(piece_done, NP * b + k + 1)
                    v.tensor_copy(vS[p][:, k - 12, :], psM[0:TT, 0:D]).then_inc(piece_out, 1)

            def row(b, u):
                n = TT * (u % 3 + 1)
                dve.wait_ge(s_done, NU * b + u + 1)
                if not (isinstance(b, int) and NU * b + u < 3):
                    dve.wait_ge(exp_done, NU * b + u - 2)
                dve.sem_inc(row_begun, 1)
                v.tensor_tensor_reduce(Sm[u % 3][:, 0:n], psS[u % 2][0:TT, 0:n], am[:, u // 3, T - n:T], 1.0, BIG,
                                       ALU.add, ALU.min, nm[:, u % NB:u % NB + 1]).then_inc(min_done, 1)

            def reciprocals(b, h):
                dve.wait_ge(exp_done, NU * b + 3 * h + 3)
                a = 3 * (h % (NB // 3))
                v.tensor_scalar(ri[:, a:a + 3], su[:, a:a + 3], 1.0, None, ALU.add)
                dve.drain()
                v.reciprocal(ri[:, a:a + 3], ri[:, a:a + 3]).then_inc(rec_done, 1)

            def turned(b, u):
                h, t = u // 3, u % 3
                dve.wait_ge(t_done, NU * b + u + 1)
                if t == 0:
                    dve.wait_ge(pv_done, H3 * b + (h - 1 if h >= 2 else 0))
                v.tensor_copy(PT[h % 2][:, 0:t + 1, qt(t)],
                              psP[u % 2][0:TT, 0:TT * (t + 1)].rearrange("k (a q) -> k a q", a=t + 1)).then_inc(pt_done, 1)

            def row_step(b, r, has_next):
                if r < NU or has_next:
                    row(*of(b, r))
                h = r // 3 - 1
                if r % 3 == 1 and h >= 0 and (h < H3 or has_next):
                    reciprocals(*((b, h) if h < H3 else (b + 1, h - H3)))

            norm(0)
            for k in range(NP):
                piece(0, 0, k)
            for r in range(AHEAD):
                row_step(0, r, True)

            def body(b, p, has_next):
                for u in range(NU):
                    row_step(b, u + AHEAD, has_next)
                    turned(b, u)
                    if u == 1 and has_next:
                        dve.wait_ge(piece_done, NP * b + NP)
                        norm(b + 1)
                    if u in PIECE_AT and has_next:
                        piece(b + 1, 1 - p, PIECE_AT.index(u))
                dve.wait_ge(w_done, b + 1)
                for t in range(NT):
                    hh = sh.h[:, 3 * b + t, :]
                    r = v.tensor_tensor(hh, hh, psW[t // 2][0:TT, D * (t % 2):D * (t % 2) + D], ALU.add)
                r.then_inc(h_added, 1)
                dve.drain()
                batch_stats(nc, dve, sh, b)
            both(dve, body)

        @block.scalar
        def _(act):
            s = nc.scalar
            act.wait_ge(ang_ready, 1)
            s.activation(cs[:, :, :], ang[:, :, :], ACT.Sin).then_inc(sin_ready, 1)
            s.activation(slope[:, :], slope[:, :], ACT.Exp).then_inc(slope_ready, 1)
            act.wait_ge(rel_ready, 1)

            def piece(b, p, k):
                if k >= 12:
                    return
                act.wait_ge(piece_done, NP * b + k + 1)
                if k < 2:
                    r = s.activation(xT[:, k, :], psM[:, 0:T], ACT.Copy)
                elif k < 10:
                    r = s.activation(qT[p][:, k - 2, :], psM[:, 0:T], ACT.Copy)
                else:
                    for half in range(2):
                        ph = slice(64 * half, 64 * half + 64)
                        r = s.activation(kz[p][ph, 2 * (k - 10) + half, :], psM[ph, 0:T], ACT.Copy)
                r.then_inc(piece_out, 1)

            def exp(b, u):
                n = TT * (u % 3 + 1)
                act.wait_ge(min_done, NU * b + u + 1)
                act.wait_ge(t_done, NU * b + (u - NB + 1 if u >= NB or u < AHEAD and not (isinstance(b, int) and b == 0) else 0))
                i = u % NB
                s.activation(P[i][:, 0:n], Sm[u % 3][:, 0:n], ACT.Exp, bias=nm[:, i:i + 1], scale=-1.0,
                             accum_out=su[:, i:i + 1]).then_inc(exp_done, 1)

            def scale_last(b, h):
                i = (3 * h + 2) % NB
                act.wait_ge(rec_done, H3 * b + h + 1)
                s.activation(P[i][:, :], P[i][:, :], ACT.Copy, scale=ri[:, i:i + 1]).then_inc(p_last_ready, 1)

            def out(b, c):
                act.wait_ge(pv_done, H3 * b + 2 * c + 2)
                act.wait_ge(w_done, b)
                s.activation(oT[c % 2][:, :], psO[:, 0:T], ACT.Copy).then_inc(o_out, 1)

            def exp_step(b, r, has_next):
                if r < NU or has_next:
                    exp(*of(b, r))
                h = r // 3 - 2
                if r % 3 == 0 and h >= 0 and (h < H3 or has_next):
                    scale_last(*((b, h) if h < H3 else (b + 1, h - H3)))

            for k in range(NP):
                piece(0, 0, k)
            for r in range(AHEAD):
                exp_step(0, r, True)

            def body(b, p, has_next):
                for u in range(NU):
                    exp_step(b, u + AHEAD, has_next)
                    if u in PIECE_AT and has_next:
                        piece(b + 1, 1 - p, PIECE_AT.index(u))
                    if u % 6 == 3 and u >= 9:
                        out(b, u // 6 - 1)
                out(b, 7)
            both(act, body)

        @block.tensor
        def _(pe):
            mm = nc.tensor.matmul
            pe.wait_ge(consts, 1)

            def piece(b, p, k):
                if k == 0:
                    pe.wait_ge(xn_ready, b + 1)
                pe.wait_ge(piece_out, NP * b + k)
                if k < 2:
                    for t in range(NT):
                        r = nc.tensor.transpose(psM[:, qt(t)], xn[:, t, 128 * k:128 * k + 128], sh.ident[0:TT, 0:TT])
                elif k < 10:
                    r = mm(psM[:, 0:T], wq[:, 2 * (k - 2):2 * (k - 2) + 2, :, :].rearrange("p h d r -> p (h d r)"),
                           xT[:, 1, :], start=True, stop=True)
                elif k < 12:
                    r = mm(psM[:, 0:T], wk[:, 128 * (k - 10):128 * (k - 10) + 128], xT[:, 1, :], start=True, stop=True)
                else:
                    r = mm(psM[0:TT, 0:D], xT[:, 0, qt(k - 12)], wv[:, :], start=True, stop=True)
                r.then_inc(piece_done, 1)

            def scores(b, p, u):
                h, t = u // 3, u % 3
                n = TT * (t + 1)
                if not (isinstance(b, int) and NU * b + u < 2):
                    pe.wait_ge(min_done, NU * b + u - 1)
                c = h // 2
                mm(psS[u % 2][0:TT, 0:n], qT[p][:, c, qt(t)], kz[p][:, 2 * (c // 4) + h % 2, 0:n],
                   start=True, stop=True).then_inc(s_done, 1)

            def turn(b, u):
                if u % 3 < 2:
                    pe.wait_ge(p_ready, 2 * (H3 * b + u // 3) + u % 3 + 1)
                else:
                    pe.wait_ge(p_last_ready, H3 * b + u // 3 + 1)
                pe.wait_ge(pt_done, NU * b + (u - 1 if u >= 2 else 0))
                for a in range(u % 3 + 1):
                    r = nc.tensor.transpose(psP[u % 2][0:TT, qt(a)], P[u % NB][:, qt(a)], sh.ident[0:TT, 0:TT])
                r.then_inc(t_done, 1)

            def values(b, p, h):
                pe.wait_ge(pt_done, NU * b + 3 * h + 3)
                if h % 2 == 0:
                    pe.wait_ge(o_out, 8 * b + h // 2)
                c = h // 2
                kv = 2 * (c // 4) + h % 2
                ph = slice(64 * (h % 2), 64 * (h % 2) + 64)
                for a in range(NT):
                    r = mm(psO[ph, TT * a:T], vS[p][:, a, DH3 * kv:DH3 * kv + DH3], PT[h % 2][:, a, TT * a:T],
                           start=a == 0, stop=a == NT - 1, skip_group_check=True)
                r.then_inc(pv_done, 1)

            def project(b, c):
                pe.wait_ge(o_out, 8 * b + c + 1)
                if c == 0:
                    pe.wait_ge(h_added, b)
                for t in range(NT):
                    r = mm(psW[t // 2][0:TT, D * (t % 2):D * (t % 2) + D], oT[c % 2][:, qt(t)], wo[:, c, :],
                           start=c == 0 and t != 1, stop=c == 7, skip_group_check=True)
                if c == 7:
                    r.then_inc(w_done, 1)

            for k in range(NP):
                piece(0, 0, k)

            pe.wait_ge(piece_out, NP)
            for u in range(AHEAD):
                scores(0, 0, u)

            def body(b, p, has_next):
                for u in range(NU):
                    if u + AHEAD < NU:
                        scores(b, p, u + AHEAD)
                    elif has_next:
                        if u + AHEAD == NU:
                            pe.wait_ge(piece_out, NP * (b + 1) + NP)
                        scores(b + 1, 1 - p, u + AHEAD - NU)
                    turn(b, u)
                    if u % 3 == 1 and u >= 4:
                        values(b, p, u // 3 - 1)
                    if u in PIECE_AT and has_next:
                        piece(b + 1, 1 - p, PIECE_AT.index(u))
                    if u % 6 == 4 and u >= 10:
                        project(b, u // 6 - 1)
                values(b, p, H3 - 1)
                project(b, 7)
            both(pe, body)


CAP = B * T // E
GELU_IN = 1.4142135623730951 / 1.41421
GELU_OUT = 1.41421 / 1.4142135623730951


class Stream:

    def __init__(self, nc, ctx, src):
        self.src = src
        self.w = [ctx.enter_context(nc.sbuf_tensor(f"c_w{i}", [128, Experts.SIZE], F32)) for i in range(2)]
        self.w_in = [ctx.enter_context(nc.semaphore(f"c_w_in{i}")) for i in range(2)]

    def load(self, eng, e, p):
        eng.dma_start(self.w[p][:, :], self.src[e]).then_inc(self.w_in[p], 16)

    def prefetch(self, eng):
        self.load(eng, 0, 0)
        self.load(eng, 1, 1)


def capacity_experts(nc, sh, ins, stream, xs, ys, out):
    assert CAP == T
    with ExitStack() as ctx:
        o = {}
        o["xall"] = ctx.enter_context(nc.sbuf_tensor("c_xall", [TT, NTILES, D], F32))
        for n, dt in (("slot", U32), ("back", U32), ("keep", F32), ("drop", F32)):
            o[n] = ctx.enter_context(nc.sbuf_tensor("c_" + n, [TT, NTILES], dt))
        router(nc, sh, ins, "cr_", "c_wr", "c_br", CAP, o)
        scatter_tokens(nc, o, xs, "cs_", lambda sync: None)

        with ExitStack() as c2:
            sb = lambda name, shape, dt=F32: c2.enter_context(nc.sbuf_tensor("c_" + name, shape, dt))
            pb = lambda name: c2.enter_context(nc.psum_tensor("c_" + name, [128, 512], F32))
            sem = lambda name: c2.enter_context(nc.semaphore("c_" + name))
            NF = 8
            xb = [sb(f"xb{i}", [TT, NT, D]) for i in range(2)]
            xT = [sb(f"xT{i}", [128, KT, T]) for i in range(2)]
            hT = [sb(f"hT{i}", [128, NF, T]) for i in range(2)]
            yb = [sb(f"yb{i}", [TT, NT, D]) for i in range(2)]
            b1 = sb("b1", [128, E, NF])
            b2 = sb("b2", [TT, E, D])
            psT = [pb(f"psT{i}") for i in range(2)]
            psH = [pb(f"psH{i}") for i in range(4)]
            psY = [pb(f"psY{i}") for i in range(2)]
            b_in = sem("b_in")
            x_in = [sem(f"x_in{i}") for i in range(2)]
            y_sent = [sem(f"y_sent{i}") for i in range(2)]
            b1_ready, x_turned, xT_ready, h_done, g_ready, y_done, y_out = (sem(n) for n in (
                "b1_ready", "x_turned", "xT_ready", "h_done", "g_ready", "y_done", "y_out"))
            block = c2.enter_context(nc.Block())
            qt = lambda a: slice(a * TT, (a + 1) * TT)

            @block.sync
            def _(sync):
                def load(e, p):
                    sync.dma_start(xb[p][:, :, :], xs[bass.ds(e * CAP, CAP), :].rearrange("(t p) c -> p t c", p=TT)).then_inc(x_in[p], 16)

                def store(e, p):
                    sync.wait_ge(y_out, NT * e + NT)
                    sync.dma_start(ys[bass.ds(e * CAP, CAP), :].rearrange("(t p) c -> p t c", p=TT), yb[p][:, :, :]).then_inc(y_sent[p], 16)
                load(0, 0)
                load(1, 1)
                with sync.Fori(0, E // 2 - 1) as i:
                    for p in range(2):
                        sync.wait_ge(x_turned, 2 * i + p + 1)
                        load(2 * i + p + 2, p)
                        sync.wait_ge(y_done, NT * (2 * i + p + 1))
                        sync.dma_start(stream.w[p][:, :], ins["moe2"][bass.ds(2 * i + p + 2, 1), :, :].rearrange("e p n -> (e p) n")).then_inc(stream.w_in[p], 16)
                        store(2 * i + p, p)
                store(E - 2, 0)
                store(E - 1, 1)
                for p in range(2):
                    sync.wait_ge(y_sent[p], 16 * (E // 2))

            @block.gpsimd
            def _(pool):
                pool.dma_start(b1[:, :, :], ins["c_b1"]).then_inc(b_in, 16)
                pool.dma_start(b2[:, :, :], ins["c_b2"].partition_broadcast(TT)).then_inc(b_in, 16)

            def experts2(eng, body):
                with eng.Fori(0, E // 2 - 1) as i:
                    body(2 * i, 0, i, True)
                    body(2 * i + 1, 1, i, True)
                body(E - 2, 0, E // 2 - 1, True)
                body(E - 1, 1, E // 2 - 1, False)

            @block.vector
            def _(dve):
                v = nc.vector
                dve.wait_ge(b_in, 32)
                v.tensor_scalar(b1[:, :, :], b1[:, :, :], GELU_IN, None, ALU.mult).then_inc(b1_ready, 1)

                def turn_out(e, p):
                    for k in range(KT):
                        dve.wait_ge(x_turned, e + 1) if k == 0 else None
                        r = v.tensor_copy(xT[p][:, k, :], psT[k][:, 0:T])
                    r.then_inc(xT_ready, 1)
                turn_out(0, 0)

                def body(e, p, i, has_next):
                    if has_next:
                        turn_out(e + 1, 1 - p)
                    dve.wait_ge(y_sent[p], 16 * i)
                    for t in range(NT):
                        dve.wait_ge(y_done, NT * e + t + 1)
                        v.scalar_tensor_tensor(yb[p][:, t, :], psY[t % 2][0:TT, 0:D], GELU_OUT, b2[:, e, :],
                                               ALU.mult, ALU.add).then_inc(y_out, 1)
                experts2(dve, body)

            @block.scalar
            def _(act):
                s = nc.scalar
                act.wait_ge(b1_ready, 1)

                def body(e, p, i, has_next):
                    for f in range(NF):
                        act.wait_ge(h_done, NF * e + f + 1)
                        s.activation(hT[p][:, f, :], psH[f % 4][:, 0:T], ACT.Gelu, bias=b1[:, e, f:f + 1],
                                     scale=GELU_IN).then_inc(g_ready, 1)
                experts2(act, body)

            @block.tensor
            def _(pe):
                mm = nc.tensor.matmul

                def turn(e, p, i):
                    pe.wait_ge(x_in[p], 16 * (i + 1))
                    pe.wait_ge(xT_ready, e)
                    for k in range(KT):
                        for t in range(NT):
                            r = nc.tensor.transpose(psT[k][:, qt(t)], xb[p][:, t, 128 * k:128 * k + 128],
                                                    sh.ident[0:TT, 0:TT])
                    r.then_inc(x_turned, 1)

                def first(e, p, i):
                    pe.wait_ge(stream.w_in[p], 16 * (i + 1))
                    pe.wait_ge(xT_ready, e + 1)
                    for f in range(NF):
                        pe.wait_ge(g_ready, NF * e + (f - 3 if f >= 4 else (f - 3 if not isinstance(e, int) or e > 0 else 0)))
                        for k in range(KT):
                            r = mm(psH[f % 4][:, 0:T], stream.w[p][:, 1024 * k + 128 * f:1024 * k + 128 * f + 128],
                                   xT[p][:, k, :], start=k == 0, stop=k == KT - 1)
                        r.then_inc(h_done, 1)
                turn(0, 0, 0)
                first(0, 0, 0)

                def body(e, p, i, has_next):
                    if has_next:
                        turn(e + 1, 1 - p, i + p)
                        first(e + 1, 1 - p, i + p)
                    pe.wait_ge(g_ready, NF * e + NF)
                    for t in range(NT):
                        pe.wait_ge(y_out, NT * e + (t - 1 if t >= 2 else 0))
                        for f in range(NF):
                            at = KT * 1024 + D * f
                            r = mm(psY[t % 2][0:TT, 0:D], hT[p][:, f, qt(t)], stream.w[p][:, at:at + D],
                                   start=f == 0, stop=f == NF - 1)
                        r.then_inc(y_done, 1)
                experts2(pe, body)

        combine_experts(nc, sh, ctx, o, ys, "cc_", out)


def clear_semaphores(nc):
    used = sorted(nc.released_uncleared_semaphores)
    runs = []
    for n in used:
        if runs and runs[-1][1] == n:
            runs[-1][1] = n + 1
        else:
            runs.append([n, n + 1])
    with nc.Block() as block:
        @block.sync
        def _(sync):
            for a, b in runs:
                sync.sem_clear(range(a, b))


def program(nc, ins, out):
    dram = lambda name, rows: nc.dram_tensor(name, [rows, D], F32, kind="Internal").ap()
    with ExitStack() as ctx:
        h0 = nc.dram_tensor("h0_scratch", [B, T, D], F32, kind="Internal").ap()
        xs, ys = dram("xs_scratch", 128 * MOE_TILES), dram("ys_scratch", 128 * MOE_TILES)
        xs2, ys2 = dram("xs2_scratch", E * CAP + B * T), dram("ys2_scratch", E * CAP)
        sh = Shared(nc, ctx, ins)
        experts = Experts(nc, ctx)
        with ExitStack() as early:
            sh.early(early)
            tokenise(nc, sh, ins, h0)
            attention16(nc, sh, [xs, xs2[0:E * CAP, :]])
            recurrence(nc, sh)
            scan_layer(nc, sh)
            quantised(nc, sh, ins)
            masked_attention(nc, sh, ins, experts)
        clear_semaphores(nc)
        top1_experts(nc, sh, ins, experts, xs, ys)
        stream = Stream(nc, ctx, ins["moe2"])
        alibi_attention(nc, sh, ins, stream)
        capacity_experts(nc, sh, ins, stream, xs2, ys2, out)


def layout(inp):
    import numpy as np
    a = {k: np.asarray(v) for k, v in inp.items()}
    o = {}
    o["x"] = a["x"].reshape(B * IMG, IMG)
    o["txt"] = a["txt"]
    for lv, name, n in ((0, "L0_tok_Wd3", 8 * 128), (1, "L0_tok_Wd2", 4 * 64), (2, "L0_tok_Wd1", 2 * 32)):
        o[f"wd{lv}"] = a[name].reshape(3, 16, n, 3).transpose(1, 3, 0, 2).reshape(16, 3, 3 * n)
    o["wa"] = np.tile(a["L0_tok_Wa"].reshape(16, 64), (8, 1))
    o["gb"] = np.concatenate([a["L0_tok_ba"], a["L0_tok_bd1"], a["L0_tok_bd2"], a["L0_tok_bd3"]])
    w = {"a_q": a["L0_attn_Wq"], "a_k": a["L0_attn_Wk"], "a_v": a["L0_attn_Wv"]}
    for n in ("wf", "uf", "wi", "ui", "wc", "uc", "wo", "uo"):
        w["f_" + n] = a["L0_ffn_" + n].T
    w["s_q"], w["s_kv"], w["s_a"] = (a["L1_attn_w_qkva"][i * D:(i + 1) * D].T for i in range(3))
    w["m_q"], w["m_k"], w["m_v"] = (a["L2_attn_" + n].T for n in ("Wq", "Wk", "Wv"))
    o["w"] = np.stack([w[n].reshape(KT, 128, D).transpose(1, 0, 2) for n in WNAMES], 1)
    c = {"a_g": a["L0_attn_ln_g"], "a_b": a["L0_attn_ln_b"], "a_bq": a["L0_attn_bq"], "a_bk": a["L0_attn_bk"],
         "f_bf": a["L0_ffn_bf"], "f_bi": a["L0_ffn_bi"], "f_bc": a["L0_ffn_bc"], "f_bo": a["L0_ffn_bo"],
         "f_c0": a["L0_ffn_in_c"], "s_g": a["L1_attn_gamma"], "m_bq": a["L2_attn_bq"], "m_bk": a["L2_attn_bk"]}
    for i in range(3):
        c[f"q_g{i}"], c[f"q_b{i}"] = a["L1_ffn_ln_gamma"][i], a["L1_ffn_ln_beta"][i]
    o["cols"] = np.stack([c[n].reshape(KT, 128).T for n in CNAMES], 1)
    r = {"a_bv": a["L0_attn_bv"], "m_bv": a["L2_attn_bv"]}
    for i in range(6):
        r[f"q_{i}"] = a["L1_ffn_biases"][i]
    o["rows"] = np.stack([r[n] for n in RNAMES])
    moe = lambda w1, w2: np.concatenate([
        w1.reshape(E, KT, 128, 1024).transpose(0, 2, 1, 3).reshape(E, 128, -1),
        w2.reshape(E, 8, 128, D).transpose(0, 2, 1, 3).reshape(E, 128, -1)], 2)
    o["moe1"] = moe(a["L2_ffn_W1"], a["L2_ffn_W2"])
    o["t_wr"], o["t_br"] = a["L2_ffn_Wr"].reshape(KT, 128, E).transpose(1, 0, 2), a["L2_ffn_br"]
    o["moe2"] = moe(a["L3_ffn_W1"], a["L3_ffn_W2"])
    o["c_wr"], o["c_br"] = a["L3_ffn_W_sw"].reshape(KT, 128, E).transpose(1, 0, 2), a["L3_ffn_b_sw"]
    o["c_b1"] = a["L3_ffn_b1"].reshape(E, 8, 128).transpose(2, 0, 1)
    o["c_b2"] = a["L3_ffn_b2"]
    order = np.array(HEAD_ORDER)
    o["l_wq"] = a["L3_attn_Wq"].reshape(128, H3, DH3)[:, order].reshape(128, H3 * DH3)
    o["l_wk"], o["l_wv"] = a["L3_attn_Wk"], a["L3_attn_Wv"]
    o["l_wo"] = a["L3_attn_Wo"].reshape(H3, DH3, D)[order].reshape(8, 128, D).transpose(1, 0, 2)
    o["l_ang"], o["l_slope"] = a["L3_attn_q_phase_angle"][order], a["L3_attn_alibi_log_slopes"][order]
    o["qw"] = a["L1_ffn_qweights"].transpose(2, 0, 1).reshape(KT, 128, 6, D).transpose(1, 2, 0, 3)
    o["qs"] = a["L1_ffn_scales"].transpose(2, 0, 1).reshape(KT, 8, 6, D).transpose(1, 2, 0, 3)
    o["qla"] = a["L1_ffn_lora_a"].transpose(1, 0, 2)
    o["qlb"] = a["L1_ffn_lora_b"].transpose(2, 0, 1)
    return {k: np.ascontiguousarray(v) for k, v in o.items()}


def kernel(**inputs):
    import concourse.bacc as _bacc
    from concourse import mybir as _mybir
    from concourse.bass_utils import run_bass_kernel_spmd as _run

    nc = _bacc.Bacc("TRN2", target_bir_lowering=False, num_devices=1)
    arrays, args = {}, {}
    for name, a in layout(inputs).items():
        arrays[f"in_{name}_dram"] = a
        args[name] = nc.dram_tensor(f"in_{name}_dram", a.shape, _mybir.dt.from_np(a.dtype), kind="ExternalInput").ap()
    out = nc.dram_tensor("out_0_dram", (B, T, D), F32, kind="ExternalOutput").ap()
    program(nc, args, out)
    r = _run(nc, [arrays], core_ids=[0])
    return r.results[0]["out_0_dram"]
```
